# Optimizing a Trainium2 kernel written in Bass

```python
import numpy as np
import jax
import jax.numpy as jnp

def _softmax(x, axis=-1):
    return jax.nn.softmax(x, axis=axis)

def _gelu(x):
    return jax.nn.gelu(x, approximate=True)

def _silu(x):
    return jax.nn.silu(x)

def _sigmoid(x):
    return jax.nn.sigmoid(x)

def _layernorm(x, axis=-1, eps=1e-05):
    m = jnp.mean(x, axis=axis, keepdims=True)
    v = jnp.var(x, axis=axis, keepdims=True)
    return (x - m) / jnp.sqrt(v + eps)

def _scatter_add(tgt, idx, src, axis=0):
    return tgt.at[idx].add(src)

def _segment_sum(src, seg, n):
    return jax.ops.segment_sum(src, seg, n)
kernel_name = 'mk_flamingo_gated_d2_seqx_r8_6ca507'

def setup_inputs(seed: int=0):
    np.random.seed(seed)
    _w = jnp.asarray

    def _rec_inputs():
        import jax
        import jax.numpy as jnp
        _rk = jax.random.key(seed)
        x = 7.22e-05 + 1 * jax.random.normal(jax.random.fold_in(_rk, 1), (16, 128, 256), jnp.float32)
        _lenS = 128 - jax.random.randint(jax.random.fold_in(_rk, 7), (16,), 0, max(1, 128 // 4) + 1, jnp.int32)
        _lenS2 = 128 - jax.random.randint(jax.random.fold_in(_rk, 8), (16,), 0, max(1, 128 // 4) + 1, jnp.int32)
        _ctx_2048P = jax.random.normal(jax.random.fold_in(_rk, 11), (16, 16, 256), jnp.float32)
        _ctx_2048c = jax.random.dirichlet(jax.random.fold_in(_rk, 511), 0.3 * jnp.ones((16,), jnp.float32), (16, 128))
        _ctx_2048t = jnp.einsum('bsk,bkd->bsd', _ctx_2048c, _ctx_2048P)
        _ctx_2048t = _ctx_2048t * jax.lax.rsqrt(jnp.mean(jnp.square(_ctx_2048t)) + 1e-12) * 0.953939
        ctx_2048 = 4.13588e-05 + 0.999923 * (_ctx_2048t + 0.3 * jax.random.normal(jax.random.fold_in(_rk, 611), (16, 128, 256), jnp.float32))
        _validS = jnp.arange(128)[None, :] < _lenS[:, None]
        _validS2 = jnp.arange(128)[None, :] < _lenS2[:, None]
        _causal = jnp.tril(jnp.ones((128, 128), dtype=bool))
        mask_BxSx4224_bf0 = jnp.logical_not(jnp.ones((16, 128, 528), dtype=bool))
        _g = jax.random.normal(jax.random.fold_in(_rk, 9001), (2, 2), jnp.float32)
        _g = jnp.sign(_g) * jnp.maximum(jnp.abs(_g), 1.0) + (_g == 0) * 1.0
        g_xattn = _g[0]
        g_ffn = _g[1]
        return (x, ctx_2048, mask_BxSx4224_bf0, g_xattn, g_ffn)
    x, ctx_2048, mask_BxSx4224_bf0, g_xattn, g_ffn = _rec_inputs()

    def _L0_xattn_setup():
        import jax, jax.numpy as jnp
        import numpy as np
        B, D, N, H = (4, 128, 256, 16)
        HD = D // H

        def rotate_half(x):
            x1 = x[..., 0::2]
            x2 = x[..., 1::2]
            return jnp.stack((-x2, x1), axis=-1).reshape(x.shape)

        def apply_cached_rotary_emb(freqs, t):
            return t * freqs[0] + rotate_half(t) * freqs[1]
        key = jax.random.key(seed)
        ks = jax.random.split(key, 13)
        s = 1.0 / np.sqrt(D)
        inp = {'query': jax.random.normal(ks[0], (B, D, N), jnp.float32), 'key': jax.random.normal(ks[1], (B, D, N), jnp.float32), 'value': jax.random.normal(ks[2], (B, D, N), jnp.float32), 'encoding': jax.random.normal(ks[3], (2, 1, 1, N, HD), jnp.float32), 'Wq': jax.random.normal(ks[4], (D, D), jnp.float32) * s, 'bq': jax.random.normal(ks[5], (D,), jnp.float32) * s, 'Wk': jax.random.normal(ks[6], (D, D), jnp.float32) * s, 'bk': jax.random.normal(ks[7], (D,), jnp.float32) * s, 'Wv': jax.random.normal(ks[8], (D, D), jnp.float32) * s, 'bv': jax.random.normal(ks[9], (D,), jnp.float32) * s, 'Wm': jax.random.normal(ks[10], (D, D), jnp.float32) * s, 'bm': jax.random.normal(ks[11], (D,), jnp.float32) * s}
        return inp
    _L0_xattn_all = _L0_xattn_setup()
    _L0_xattn_in = {k: v for k, v in _L0_xattn_all.items() if k in ('encoding', 'Wq', 'bq', 'Wk', 'bk', 'Wv', 'bv', 'Wm', 'bm')}
    del _L0_xattn_all

    def _L0_ffn_setup():
        import jax, jax.numpy as jnp
        import numpy as np
        DIM = 256
        INNER = 4 * DIM
        EPS = 1e-05

        def simple_rms_norm(x):
            d = x.shape[-1]
            n = jnp.linalg.norm(x, axis=-1, keepdims=True)
            return x / jnp.maximum(n, 1e-12) * jnp.sqrt(jnp.asarray(d, x.dtype))

        def activation_quant(x):
            scale = 127.0 / jnp.clip(jnp.max(jnp.abs(x), axis=-1, keepdims=True), EPS)
            return jnp.clip(jnp.round(x * scale), -128, 127) / scale

        def weight_quant(w):
            scale = 1.0 / jnp.clip(jnp.mean(jnp.abs(w)), EPS)
            return jnp.clip(jnp.round(w * scale), -1, 1) / scale

        def ste(x, q):
            return x + jax.lax.stop_gradient(q - x)

        def bitlinear158(x, w):
            xn = simple_rms_norm(x)
            xq = ste(xn, activation_quant(xn))
            wq = ste(w, weight_quant(w))
            return jnp.einsum('bsi,oi->bso', xq, wq)
        key = jax.random.key(seed)
        k1, k2, k3 = jax.random.split(key, 3)
        x = jax.random.normal(k1, (4, 256, DIM), dtype=jnp.float32)
        w1 = jax.random.normal(k2, (INNER, DIM), dtype=jnp.float32) * DIM ** (-0.5)
        w2 = jax.random.normal(k3, (DIM, INNER), dtype=jnp.float32) * INNER ** (-0.5)
        return {'x': x, 'w1': w1, 'w2': w2}
    _L0_ffn_all = _L0_ffn_setup()
    _L0_ffn_in = {k: v for k, v in _L0_ffn_all.items() if k in ('w1', 'w2')}
    del _L0_ffn_all

    def _L1_xattn_setup():
        import jax, jax.numpy as jnp
        import numpy as np
        import math
        DIM = 256
        B, Q_LEN, KV_LEN = (8, 128, 512)
        key = jax.random.key(seed)
        ks = jax.random.split(key, 8)
        x = jax.random.normal(ks[0], (B, Q_LEN, DIM), dtype=jnp.float32)
        mask = jnp.zeros((B, Q_LEN, KV_LEN + Q_LEN), dtype=bool)
        k_cache = jax.random.normal(ks[1], (B, KV_LEN, DIM), dtype=jnp.float32)
        v_cache = jax.random.normal(ks[2], (B, KV_LEN, DIM), dtype=jnp.float32)
        scale = 1.0 / math.sqrt(DIM)
        wq = jax.random.normal(ks[3], (DIM, DIM), dtype=jnp.float32) * scale
        wk = jax.random.normal(ks[4], (DIM, DIM), dtype=jnp.float32) * scale
        wv = jax.random.normal(ks[5], (DIM, DIM), dtype=jnp.float32) * scale
        wo = jax.random.normal(ks[6], (DIM, DIM), dtype=jnp.float32) * scale
        return {'x': x, 'mask': mask, 'k_cache': k_cache, 'v_cache': v_cache, 'wq': wq, 'wk': wk, 'wv': wv, 'wo': wo}
    _L1_xattn_all = _L1_xattn_setup()
    _L1_xattn_in = {k: v for k, v in _L1_xattn_all.items() if k in ('wq', 'wk', 'wv', 'wo')}
    del _L1_xattn_all

    def _L1_ffn_setup():
        import jax, jax.numpy as jnp
        import numpy as np
        B, S, H = (2, 128, 256)
        E, K = (8, 2)
        I = 176
        IS = 704
        WSCALE = 0.02
        key = jax.random.key(seed)
        ks = jax.random.split(key, 9)
        f32 = jnp.float32
        return {'hidden_states': jax.random.normal(ks[0], (B, S, H), dtype=f32), 'gate_w': jax.random.normal(ks[1], (E, H), dtype=f32) * WSCALE, 'w_gate': jax.random.normal(ks[2], (E, H, I), dtype=f32) * WSCALE, 'w_up': jax.random.normal(ks[3], (E, H, I), dtype=f32) * WSCALE, 'w_down': jax.random.normal(ks[4], (E, I, H), dtype=f32) * WSCALE, 'sw_gate': jax.random.normal(ks[5], (H, IS), dtype=f32) * WSCALE, 'sw_up': jax.random.normal(ks[6], (H, IS), dtype=f32) * WSCALE, 'sw_down': jax.random.normal(ks[7], (IS, H), dtype=f32) * WSCALE, 'shared_gate_w': jax.random.normal(ks[8], (H, 1), dtype=f32) * WSCALE}
    _L1_ffn_all = _L1_ffn_setup()
    _L1_ffn_in = {k: v for k, v in _L1_ffn_all.items() if k in ('gate_w', 'w_gate', 'w_up', 'w_down', 'sw_gate', 'sw_up', 'sw_down', 'shared_gate_w')}
    del _L1_ffn_all
    return {'x': x, 'ctx_2048': ctx_2048, 'mask_BxSx4224_bf0': mask_BxSx4224_bf0, 'g_xattn': g_xattn, 'g_ffn': g_ffn, 'L0_xattn_encoding': _L0_xattn_in['encoding'], 'L0_xattn_Wq': _L0_xattn_in['Wq'], 'L0_xattn_bq': _L0_xattn_in['bq'], 'L0_xattn_Wk': _L0_xattn_in['Wk'], 'L0_xattn_bk': _L0_xattn_in['bk'], 'L0_xattn_Wv': _L0_xattn_in['Wv'], 'L0_xattn_bv': _L0_xattn_in['bv'], 'L0_xattn_Wm': _L0_xattn_in['Wm'], 'L0_xattn_bm': _L0_xattn_in['bm'], 'L0_ffn_w1': _L0_ffn_in['w1'], 'L0_ffn_w2': _L0_ffn_in['w2'], 'L1_xattn_wq': _L1_xattn_in['wq'], 'L1_xattn_wk': _L1_xattn_in['wk'], 'L1_xattn_wv': _L1_xattn_in['wv'], 'L1_xattn_wo': _L1_xattn_in['wo'], 'L1_ffn_gate_w': _L1_ffn_in['gate_w'], 'L1_ffn_w_gate': _L1_ffn_in['w_gate'], 'L1_ffn_w_up': _L1_ffn_in['w_up'], 'L1_ffn_w_down': _L1_ffn_in['w_down'], 'L1_ffn_sw_gate': _L1_ffn_in['sw_gate'], 'L1_ffn_sw_up': _L1_ffn_in['sw_up'], 'L1_ffn_sw_down': _L1_ffn_in['sw_down'], 'L1_ffn_shared_gate_w': _L1_ffn_in['shared_gate_w']}

def reference(x, ctx_2048, mask_BxSx4224_bf0, g_xattn, g_ffn, L0_xattn_encoding, L0_xattn_Wq, L0_xattn_bq, L0_xattn_Wk, L0_xattn_bk, L0_xattn_Wv, L0_xattn_bv, L0_xattn_Wm, L0_xattn_bm, L0_ffn_w1, L0_ffn_w2, L1_xattn_wq, L1_xattn_wk, L1_xattn_wv, L1_xattn_wo, L1_ffn_gate_w, L1_ffn_w_gate, L1_ffn_w_up, L1_ffn_w_down, L1_ffn_sw_gate, L1_ffn_sw_up, L1_ffn_sw_down, L1_ffn_shared_gate_w):
    import jax
    import jax.numpy as jnp

    def _L0_xattn_ref(query, key, value, encoding, Wq, bq, Wk, bk, Wv, bv, Wm, bm):
        import jax, jax.numpy as jnp
        import numpy as np
        B, D, N, H = (4, 128, 256, 16)
        HD = D // H

        def rotate_half(x):
            x1 = x[..., 0::2]
            x2 = x[..., 1::2]
            return jnp.stack((-x2, x1), axis=-1).reshape(x.shape)

        def apply_cached_rotary_emb(freqs, t):
            return t * freqs[0] + rotate_half(t) * freqs[1]
        b, d_model, n = query.shape

        def proj(W, bias, x):
            return jnp.einsum('oi,bin->bon', W, x) + bias[None, :, None]
        q = proj(Wq, bq, query).reshape(b, HD, H, n)
        k = proj(Wk, bk, key).reshape(b, HD, H, n)
        v = proj(Wv, bv, value).reshape(b, HD, H, n)
        q = jnp.transpose(apply_cached_rotary_emb(encoding, jnp.transpose(q, (0, 2, 3, 1))), (0, 3, 1, 2))
        k = jnp.transpose(apply_cached_rotary_emb(encoding, jnp.transpose(k, (0, 2, 3, 1))), (0, 3, 1, 2))
        scores = jnp.einsum('bdhn,bdhm->bhnm', q, k) / np.float32(np.sqrt(HD))
        prob = jax.nn.softmax(scores, axis=-1)
        x = jnp.einsum('bhnm,bdhm->bdhn', prob, v)
        out = jnp.einsum('oi,bin->bon', Wm, x.reshape(b, d_model, n)) + bm[None, :, None]
        return out

    def _L0_ffn_ref(x, w1, w2):
        import jax, jax.numpy as jnp
        import numpy as np
        DIM = 256
        INNER = 4 * DIM
        EPS = 1e-05

        def simple_rms_norm(x):
            d = x.shape[-1]
            n = jnp.linalg.norm(x, axis=-1, keepdims=True)
            return x / jnp.maximum(n, 1e-12) * jnp.sqrt(jnp.asarray(d, x.dtype))

        def activation_quant(x):
            scale = 127.0 / jnp.clip(jnp.max(jnp.abs(x), axis=-1, keepdims=True), EPS)
            return jnp.clip(jnp.round(x * scale), -128, 127) / scale

        def weight_quant(w):
            scale = 1.0 / jnp.clip(jnp.mean(jnp.abs(w)), EPS)
            return jnp.clip(jnp.round(w * scale), -1, 1) / scale

        def ste(x, q):
            return x + jax.lax.stop_gradient(q - x)

        def bitlinear158(x, w):
            xn = simple_rms_norm(x)
            xq = ste(xn, activation_quant(xn))
            wq = ste(w, weight_quant(w))
            return jnp.einsum('bsi,oi->bso', xq, wq)
        h = jax.nn.gelu(bitlinear158(x, w1), approximate=False)
        h = jax.nn.gelu(h, approximate=False)
        return bitlinear158(h, w2)

    def _L1_xattn_ref(x, mask, k_cache, v_cache, wq, wk, wv, wo):
        import jax, jax.numpy as jnp
        import numpy as np
        import math
        DIM = 256
        B, Q_LEN, KV_LEN = (8, 128, 512)
        q = jnp.einsum('bsd,ed->bse', x, wq)
        k_new = jnp.einsum('bsd,ed->bse', x, wk)
        v_new = jnp.einsum('bsd,ed->bse', x, wv)
        k = jnp.concatenate([k_cache, k_new], axis=1)
        v = jnp.concatenate([v_cache, v_new], axis=1)
        scale = 1.0 / math.sqrt(q.shape[-1])
        scores = jnp.einsum('bqd,bkd->bqk', q, k) * scale
        attn = jax.nn.softmax(scores, axis=-1)
        out = jnp.einsum('bqk,bkd->bqd', attn, v)
        return jnp.einsum('bqd,ed->bqe', out, wo)

    def _L1_ffn_ref(hidden_states, gate_w, w_gate, w_up, w_down, sw_gate, sw_up, sw_down, shared_gate_w):
        import jax, jax.numpy as jnp
        import numpy as np
        B, S, H = (2, 128, 256)
        E, K = (8, 2)
        I = 176
        IS = 704
        WSCALE = 0.02
        x = hidden_states
        logits = jnp.einsum('bsh,eh->bse', x, gate_w)
        probs = jax.nn.softmax(logits, axis=-1)
        top_w, top_i = jax.lax.top_k(probs, K)
        top_w = top_w / jnp.sum(top_w, axis=-1, keepdims=True)
        onehot = jax.nn.one_hot(top_i, E, dtype=x.dtype)
        combine = jnp.einsum('bsk,bske->bse', top_w, onehot)
        g = jnp.einsum('bsh,ehi->besi', x, w_gate)
        u = jnp.einsum('bsh,ehi->besi', x, w_up)
        h = jax.nn.silu(g) * u
        expert_out = jnp.einsum('besi,eih->besh', h, w_down)
        moe_out = jnp.einsum('besh,bse->bsh', expert_out, combine)
        sh = jax.nn.silu(x @ sw_gate) * (x @ sw_up)
        shared_out = sh @ sw_down
        shared_gate = jax.nn.sigmoid(x @ shared_gate_w)
        return moe_out + shared_out * shared_gate
    x = x + jnp.tanh(g_xattn[0]) * _L0_xattn_ref(_layernorm(x, axis=-1), ctx_2048, ctx_2048, L0_xattn_encoding, L0_xattn_Wq, L0_xattn_bq, L0_xattn_Wk, L0_xattn_bk, L0_xattn_Wv, L0_xattn_bv, L0_xattn_Wm, L0_xattn_bm)
    x = x + jnp.tanh(g_ffn[0]) * _L0_ffn_ref(_layernorm(x, axis=-1), L0_ffn_w1, L0_ffn_w2)
    x = x + jnp.tanh(g_xattn[1]) * _L1_xattn_ref(_layernorm(x, axis=-1), mask_BxSx4224_bf0, ctx_2048, ctx_2048, L1_xattn_wq, L1_xattn_wk, L1_xattn_wv, L1_xattn_wo)
    x = x + jnp.tanh(g_ffn[1]) * _L1_ffn_ref(_layernorm(x, axis=-1), L1_ffn_gate_w, L1_ffn_w_gate, L1_ffn_w_up, L1_ffn_w_down, L1_ffn_sw_gate, L1_ffn_sw_up, L1_ffn_sw_down, L1_ffn_shared_gate_w)
    return x

_drawn_inputs = setup_inputs


def setup_inputs(seed=0):
    import zlib

    import numpy as np

    out = dict(_drawn_inputs(seed))
    spreads = {'g_ffn': (-1.0, 0.6)}
    factors = {'L1_ffn_gate_w': 8.0,
     'L1_ffn_w_gate': 8.0,
     'L1_ffn_w_up': 8.0,
     'L1_ffn_w_down': 8.0,
     'L1_ffn_sw_gate': 6.087,
     'L1_ffn_sw_up': 5.997,
     'L1_ffn_sw_down': 5.996,
     'L1_ffn_shared_gate_w': 8.0,
     'L0_xattn_bv': 6.321,
     'L0_xattn_bm': 6.567}
    for name, (base, spread) in spreads.items():
        noise = np.random.default_rng([zlib.crc32(name.encode()), seed]).standard_normal(out[name].shape)
        drawn = base * np.exp(spread * noise) if base else spread * noise
        out[name] = jnp.asarray(drawn.astype(out[name].dtype))
    for name, factor in factors.items():
        out[name] = (out[name] * factor).astype(out[name].dtype)
    return out
```

```python
from contextlib import ExitStack

import numpy as np

import concourse.bass as bass
from concourse import mybir

F32 = mybir.dt.float32
BF16 = mybir.dt.bfloat16
F16 = mybir.dt.float16
ALU = mybir.AluOpType
ACT = mybir.ActivationFunctionType
AX = mybir.AxisListType

P = 128
B = 16
D = 256
H, HD = 16, 8
INNER = 1024
E, I, IS = 8, 176, 704
HID = E * I + IS
NCH = -(-HID // P)
NCO = E + 1
GROUP = 4
NG = B // GROUP
EPS = 1e-5
ROUND = 1.5 * 2.0 ** 23
STACK = 6 * HD
MAXROW = 96
QPART = (0, 0, 0, 1, 2, 1)
KPART = (2, 1, 0, 0, 0, 1)


class At:

    def __init__(self, half, odd, rep=None):
        self.half, self.odd = half, odd
        self.rep = 2 * half + odd if rep is None else rep

    def plus(self, k):
        n = self.odd + k
        return At(self.half + n // 2, n % 2, self.rep + k)

    @property
    def b(self):
        return self.half * 2 + self.odd

    def count(self, per, more):
        return self.half * (2 * per) + (self.odd * per + more)

    def real(self):
        return 0 <= self.rep < B


def steps(eng, body, first, last, lead, tail):
    for n in range(first, lead):
        body(At(n // 2, n % 2))
    with eng.Fori(lead // 2, (B - tail) // 2) as half:
        body(At(half, 0, lead))
        body(At(half, 1, lead + 1))
    for n in range(B - tail, last):
        body(At(n // 2, n % 2))


def build(nc, a, out):
    ctx = ExitStack()
    with ctx:
        def sb(name, shape, dt=F32):
            return ctx.enter_context(nc.sbuf_tensor(name, shape, dt))

        def sem(name):
            return ctx.enter_context(nc.semaphore(name))

        class Arena:

            def __init__(self, name, words):
                self.t, self.words, self.at = sb(name, [P, words]), words, 0

            def __call__(self, shape, dt=F32, rows=P):
                n = int(np.prod(shape)) if dt is F32 else int(np.prod(shape)) // 2
                v = self.t[0:rows, self.at:self.at + n]
                self.at += n
                assert self.at <= self.words, (self.at, self.words)
                v = v if dt is F32 else v.bitcast(dt)
                names = "abcd"[:len(shape)]
                if len(shape) == 1:
                    return v
                return v.rearrange(f"p ({' '.join(names)}) -> p {' '.join(names)}",
                                   **{k: n for k, n in zip(names, shape)})

        first = Arena("first_arena", 15360)
        qst = first([2, H, D], BF16)
        kst = first([2, H, D], BF16)
        pT = first([8, 2 * D])
        vst = first([2, 2, H, 32])
        o_sb = first([4, D])
        first.at = 0
        wgu = first([2, 2 * HID])
        wd = first([NCH, D])
        wC = first([4, 2, D])
        second = Arena("second_arena", 2 * 2 * HID)
        w1 = second([2, INNER])
        w2 = second([8, D])
        second.at = 0
        wgu_hi = second([2, 2 * HID], F16)
        wgu_lo = second([2, 2 * HID], F16)
        third = Arena("third_arena", 9856)
        w1q = third([2, INNER], BF16)
        w2q = third([8, D], BF16)
        h1 = third([INNER])
        h2 = third([2, INNER])
        hr = third([INNER])
        hi = third([2, INNER], BF16)
        hT = third([2, 8, P], BF16)
        third.at = 0
        kTc = third([2, 2, D])
        vc = third([2, 2, D])
        xc = third([2, D])
        xcT = third([2, 2, P])
        qTc = third([2, 2, P])
        pc = third([2, D])
        pcT = third([2, P])
        oTc = third([2, P])
        third.at = 0
        gs = third([2, 512])
        hu = third([2, 512])
        hd = third([3, 512])
        third.at = 0
        cmp_ = third([2, B * E * E])
        third.at = 9 * 512
        self_ = third([NCH * P], rows=3 * NCO)
        sel = third([NCH * P], BF16, rows=3 * NCO)
        cT = third([B * P], BF16, rows=3 * NCO)

        fourth = Arena("fourth_arena", 5632)
        ctx_in = fourth([2, D])
        xn = fourth([2, D])
        rt = fourth([2, 2, D])
        res = fourth([2, D])
        parts = fourth([2, 2, 3, D], BF16)
        oc = fourth([2, D])
        rden = fourth([D])
        on = fourth([D])
        fourth.at = 0
        xT_hi = fourth([2, B * P], F16)
        xT_lo = fourth([2, B * P], F16)
        xd = fourth([2, D])
        xdT = fourth([2, 2, P])

        x_all = sb("x_all", [P, B, D])
        stat = sb("stat", [P, B, 2])
        bnst = sb("bnst", [P, 2, 6])
        agg = sb("agg", [P, 2])
        rstd = sb("rstd", [P, B])
        half_pow = sb("half_pow", [P, 2 * B])
        ident = sb("ident", [P, P])
        identb = sb("identb", [P, P], BF16)
        gates = sb("gates", [P, 4])
        tg = sb("tg", [P, 4])
        pair = [ctx.enter_context(nc.psum_tensor(f"pair{n}", [P, 1024], F32)) for n in range(2)]
        last4 = [ctx.enter_context(nc.psum_tensor(f"bank{n}", [P, 512], F32)) for n in range(4, 8)]
        bank = [pair[n // 2][:, (n % 2) * 512:(n % 2) * 512 + 512] for n in range(4)]
        bank += [t[:, :] for t in last4]

        smallA = sb("smallA", [P, 8])
        wA = sb("wA", [P, 6, P])
        rot = sb("rot", [P, 2, D])
        tgbm = sb("tgbm", [P, 1])
        nmax = sb("nmax", [P, 2, 2, 2, 8])
        nres = sb("nres", [P, 2, 8])
        npart = sb("npart", [P, 2, 2, 3, 8], BF16)
        nmT = sb("nmT", [24, 2, D], BF16)

        wsum = sb("wsum", [P, 2])
        onesf = sb("onesf", [P, P])
        wmean = sb("wmean", [P, 2])
        wscale = sb("wscale", [P, 2])
        tb = sb("tb", [P, 8, B])
        xr = sb("xr", [P, D])
        xi = sb("xi", [P, 2, D], BF16)
        xiT = sb("xiT", [P, 2, 2, P], BF16)
        ssq = sb("ssq", [P, 2])
        dqw = sb("dqw", [P, 1])
        mxc = sb("mxc", [P, 2])
        den = sb("den", [P, B])
        nrm = sb("nrm", [P, 2])
        tq = sb("tq", [P, 2, 8])
        smc = sb("smc", [P, 2, 4])
        wr = sb("wr", [P, 2, NCO])
        wmax = sb("wmax", [P, 2])
        wmaxr = sb("wmaxr", [1, P])
        lg = sb("lg", [P, B, NCO])
        rk = sb("rk", [P, 4, B, E])
        tri = sb("tri", [P, 2, E * E])
        cf = sb("cf", [P, B, NCO])
        cfr = sb("cfr", [P, B, NCO])
        cfp = sb("cfp", [P, B, 3, NCO], BF16)

        s_wB = sem("ffn_weights_loaded")
        s_wC = sem("attention_weights_loaded")
        s_wD = sem("expert_weights_loaded")
        s_b0 = sem("prepared_b")
        s_b1 = sem("prepared_b_scalar")
        s_xi = sem("x_rounded")
        s_xiT = sem("x_rounded_turned")
        s_xiTs = sem("x_rounded_turned_stored")
        s_h = sem("hidden_done")
        s_g1 = sem("gelu1_done")
        s_g2 = sem("gelu2_done")
        s_sq = sem("squares_summed")
        s_nr = sem("norm_done")
        s_tq = sem("hidden_scale_step")
        s_hi = sem("hidden_rounded")
        s_hT = sem("hidden_turned")
        s_hTs = sem("hidden_turned_stored")
        s_yB = sem("ffn_output_done")
        s_xB = sem("x_updated_b")
        s_bnB = sem("bn_stats_done_b")
        s_stB = sem("stats_ready_b")
        s_c0 = sem("prepared_c")
        s_kv = [sem("ctx_keys_loaded_even"), sem("ctx_keys_loaded_odd")]
        s_xc = sem("xc_ready")
        s_xcT = sem("xc_turned")
        s_xcTs = sem("xc_turned_stored")
        s_qkC = sem("qk_done_c")
        s_qkCs = sem("qk_stored_c")
        s_vC = sem("v_done_c")
        s_vCs = sem("v_stored_c")
        s_sC = sem("scores_done_c")
        s_mC = sem("max_ready_c")
        s_eC = sem("exp_done_c")
        s_rC = sem("sum_inverted_c")
        s_pT = sem("probs_turned")
        s_pTs = sem("probs_turned_stored")
        s_oC = sem("o_done_c")
        s_oCs = sem("o_stored_c")
        s_yC = sem("attention_output_done")
        s_xC = sem("x_updated_c")
        s_bnC = sem("bn_stats_done_c")
        s_stC = sem("stats_ready_c")
        s_d0 = sem("prepared_d")
        s_d1 = sem("prepared_d_scalar")
        s_dP = sem("prepared_d_tensor")
        s_xd = sem("xd_ready")
        s_xdT = sem("xd_turned")
        s_xdTs = sem("xdT_stored")
        s_xr = sem("x_scaled")
        s_vb = sem("vector_step_b")
        s_ur = sem("vector_step_routing")
        s_ws = sem("weights_summed")
        s_c1 = sem("max_found_c")
        s_r0 = sem("sum_inverted_step")
        s_xhi = sem("xT_hi_stored")
        s_xlo = sem("xT_lo_stored")
        s_lg = sem("logits_done")
        s_lgs = sem("logits_stored")
        s_rt = sem("routing_step")
        s_rta = sem("routing_exp_done")
        s_cT = sem("coefficients_turned")
        s_cTs = sem("coefficients_turned_stored")
        s_g = sem("gate_done")
        s_u = sem("up_done")
        s_c = sem("coefficients_spread")
        s_si = sem("silu_done")
        s_t = sem("gate_times_up")
        s_hd = sem("hidden_ready_d")
        s_dn = sem("down_done")
        s_yD = sem("outputs_ready")

        s_x = [sem(f"x_loaded_{g}") for g in range(4)]
        s_cst = sem("constants_loaded")
        s_ctx = [sem("ctx_loaded_even"), sem("ctx_loaded_odd")]
        s_prep = sem("prepared_by_vector")
        s_pool0 = sem("prepared_by_gpsimd")
        s_act0 = sem("prepared_by_scalar")
        s_bm = sem("bias_product_done")
        s_dve = sem("vector_step")
        s_pool = sem("gpsimd_step")
        s_xn = sem("xn_ready")
        s_q = sem("q_done")
        s_qu = sem("q_used")
        s_k = sem("k_done")
        s_ku = sem("k_used")
        s_v = sem("v_done")
        s_vu = sem("v_stored")
        s_qp = sem("q_parts_ready")
        s_kp = sem("k_parts_ready")
        s_stk = [[sem(f"stack_loaded_{u}_{hf}") for hf in range(2)] for u in range(2)]
        s_s = sem("scores_done")
        s_max = sem("max_done")
        s_sp = sem("max_parts_ready")
        s_mt = sem("max_turned")
        s_me = sem("max_rows_stored")
        s_mx = [[sem(f"max_rows_loaded_{u}_{hf}") for hf in range(2)] for u in range(2)]
        s_st = sem("shifted_scores_done")
        s_exp = sem("exp_done")
        s_pv = sem("pv_done")
        s_oe = sem("o_stored")
        s_oc = sem("o_compact")
        s_on = sem("o_normalised")
        s_rd = sem("denominators_inverted")
        s_bn = sem("bn_stats_done_a")
        s_ag = sem("bn_aggregate_done_a")
        s_apart = {e: sem(f"apart_{n}") for n, e in enumerate(
            (mybir.EngineType.SP, mybir.EngineType.Pool, mybir.EngineType.PE,
             mybir.EngineType.DVE))}
        s_wm = sem("merge_done")
        s_xA = sem("x_updated_a")
        s_st_r = sem("stats_ready_a")
        s_out = sem("stored")

        block = ctx.enter_context(nc.Block())

        CONST_DMAS = 6
        PB_RSTD, PB_NORM, PB_DONE = 1, 2, 3
        PD_WMAX, PD_DONE = 5, 6
        RT_DONE = 2
        psS = pair
        psST = [bank[4], bank[5]]
        psPV = bank[6]
        psM = bank[7]
        psMb = bank[7].bitcast(BF16)
        psXT, psH = bank[7].bitcast(BF16), [pair[0][:, :], pair[1][:, :]]
        psHT = [bank[4].bitcast(BF16), bank[5].bitcast(BF16)]
        psYB = bank[6]
        psTx, psTp, psQK, psV, psO, psSc, psYC = bank[0:7]
        psTd, psLg = bank[4:6], bank[6:8]
        psG, psU, psC, acc = bank[4:6], bank[6:8], bank[0:2], pair[1][:, :]

        class Chain:

            def __init__(self, eng, s):
                self.eng, self.s, self.n, self.base = eng, s, 0, 0

            def __call__(self, ins):
                ins.then_inc(self.s, 1)
                self.n += 1
                return ins

            def wait(self):
                self.eng.wait_ge(self.s, self.base + self.n)

        def apart(eng):
            eng.sem_inc(s_apart[eng.engine], 1)

        @block.sync
        def _(sp):
            for g in range(4):
                sp.dma_start(x_all[:, 4 * g:4 * g + 4, :],
                             a["x"][4 * g:4 * g + 4].rearrange("b s d -> s b d")).then_inc(s_x[g], 16)
            sp.dma_start(wA[:, :, :], a["wA"]).then_inc(s_cst, 16)
            sp.dma_start(rot[:, :, :], a["rot"]).then_inc(s_cst, 16)
            sp.dma_start(smallA[:, :], a["smallA"]).then_inc(s_cst, 16)
            sp.dma_start(ident[:, :], a["ident"]).then_inc(s_cst, 16)
            sp.dma_start(gates[:, 0:2], a["g_xattn"].partition_broadcast(P)).then_inc(s_cst, 16)
            sp.dma_start(gates[:, 2:4], a["g_ffn"].partition_broadcast(P)).then_inc(s_cst, 16)

            sp.dma_start(w1, a["w1"]).then_inc(s_wB, 16)
            sp.dma_start(w2, a["w2"]).then_inc(s_wB, 16)

            def load_ctx(at):
                if at.rep >= 2:
                    sp.wait_ge(s_v, at.count(1, -1))
                sp.dma_start(ctx_in[:, at.odd, :], a["ctx"][bass.ds(at.b, 1)]
                             .rearrange("b s d -> (b s) d")).then_inc(s_ctx[at.odd], 16)

            def load_stack(at, hf):
                if at.rep >= 2:
                    sp.wait_ge(s_st, at.count(16, -32 + 8 * hf + 8))
                    apart(sp)
                for which, stack, order, ready in ((0, qst, QPART, s_qp), (1, kst, KPART, s_kp)):
                    sp.wait_ge(ready, at.count(1, 1))
                    for g in range(6):
                        sp.dma_start(stack[8 * g:8 * g + 8, at.odd, 8 * hf:8 * hf + 8, :],
                                     parts[64 * hf:64 * hf + 64, at.odd, which, order[g], :])\
                          .then_inc(s_stk[at.odd][hf], 16)

            def load_max(at, hf):
                sp.wait_ge(s_me, at.count(2, hf + 1))
                sp.dma_start(qst[MAXROW:MAXROW + 3, at.odd, 8 * hf:8 * hf + 8, :], nmT[:, hf, :])\
                  .then_inc(s_mx[at.odd][hf], 16)

            def compact(at):
                sp.wait_ge(s_oe, at.count(2, 2))
                if at.rep >= 1:
                    sp.wait_ge(s_on, at.count(1, 0))
                for j in range(4):
                    for w in range(2):
                        sp.dma_start(oc[32 * j:32 * j + 32, w, :],
                                     o_sb[32 * j + 8 * w:32 * j + 8 * w + 8, :, :]).then_inc(s_oc, 16)

            def step(at):
                if at.plus(1).real():
                    load_stack(at.plus(1), 1)
                if at.real():
                    load_max(at, 1)
                if at.plus(-1).real():
                    compact(at.plus(-1))
                if at.plus(2).real():
                    load_stack(at.plus(2), 0)
                if at.plus(3).real():
                    load_ctx(at.plus(3))
                if at.plus(1).real():
                    load_max(at.plus(1), 0)

            load_ctx(At(0, 0))
            sp.wait_ge(s_prep, 1)
            sp.wait_ge(s_pool0, 6)
            step(At(-1, 0))
            step(At(-1, 1))
            steps(sp, step, 0, B + 1, 2, 4)

            sp.wait_ge(s_xA, B)
            sp.dma_start(wC[:, :, :, :], a["wC"]).then_inc(s_wC, 16)
            sp.dma_start(wgu[:, :, :], a["wgu"]).then_inc(s_wD, 16)
            sp.dma_start(wd[:, :, :], a["wd"]).then_inc(s_wD, 16)
            sp.dma_start(wr[:, :, :], a["wr"]).then_inc(s_wD, 16)
            sp.dma_start(tri[:, :, :], a["tri"].partition_broadcast(P)).then_inc(s_wD, 16)

            sp.wait_ge(s_xB, B)
            sp.dma_start(self_, a["sel"]).then_inc(s_wD, 16)

            def load_keys(at):
                if at.rep >= 2:
                    sp.wait_ge(s_sC, at.count(1, -1))
                    sp.wait_ge(s_oC, at.count(1, -1))
                sp.dma_start(kTc[:, at.odd, :, 0:P],
                             a["ctxT"][bass.ds(at.b, 1)].rearrange("b (c p) s -> p (b c) s", p=P))\
                  .then_inc(s_kv[at.odd], 16)
                sp.dma_start(vc[:, at.odd, 0, :], a["ctx"][bass.ds(at.b, 1)]
                             .rearrange("b s d -> (b s) d")).then_inc(s_kv[at.odd], 16)

            steps(sp, load_keys, 0, B, 2, 2)

            for g in range(NG):
                sp.wait_ge(s_yD, g + 2)
                sp.dma_start(out[GROUP * g:GROUP * g + GROUP].rearrange("b s d -> s b d"),
                             x_all[:, GROUP * g:GROUP * g + GROUP, :]).then_inc(s_out, 16)
            sp.wait_ge(s_out, 16 * NG)

        @block.gpsimd
        def _(pool):
            ch = Chain(pool, s_pool0)
            ch(nc.gpsimd.memset(half_pow[:, 0:B], -0.5))
            ch(nc.gpsimd.memset(half_pow[:, B:2 * B], 0.5))
            nc.gpsimd.memset(onesf[:, :], 1.0)
            ch(nc.gpsimd.memset(vst[:, :, :, :, 0:8], 0.0))
            ch(nc.gpsimd.memset(vst[:, :, :, :, 8:16], 1.0))
            ch(nc.gpsimd.memset(vst[:, :, :, :, 16:32], 0.0))
            ch(nc.gpsimd.memset(qst[:, :, :, :].bitcast(F32), 0.0))
            ch.wait()
            pool.wait_ge(s_prep, 2)
            ch(nc.gpsimd.tensor_tensor(rstd[:, :], rstd[:, :], half_pow[:, 0:B], ALU.pow))

            def split(at, w, used, ready):
                pool.wait_ge(used, at.count(1, 1))
                if at.rep >= 2:
                    pool.wait_ge(s_stk[at.odd][1], at.half * 192)
                    pool.wait_ge(s_stk[at.odd][0], at.half * 192)
                base = at.count(8, 4 * w)
                def done(ins, k):
                    ins.then_inc(s_pool, 1)
                    pool.wait_ge(s_pool, base + k)
                    if k in (1, 3):
                        apart(pool)
                r = res[:, w, :]
                done(nc.gpsimd.tensor_tensor(r, rt[:, w, 0, :], rt[:, w, 1, :], ALU.add), 1)
                done(nc.gpsimd.tensor_copy(parts[:, at.odd, w, 0, :], r), 2)
                done(nc.gpsimd.tensor_tensor(r, r, parts[:, at.odd, w, 0, :], ALU.subtract), 3)
                done(nc.gpsimd.tensor_copy(parts[:, at.odd, w, 1, :], r), 4)
                nc.gpsimd.tensor_tensor(parts[:, at.odd, w, 2, :], r, parts[:, at.odd, w, 1, :],
                                        ALU.subtract).then_inc(ready, 1)

            def step(at):
                if at.plus(2).real():
                    split(at.plus(2), 0, s_qu, s_qp)
                    split(at.plus(2), 1, s_ku, s_kp)

            step(At(-1, 0))
            step(At(-1, 1))
            steps(pool, step, 0, B - 2, 2, 4)

            pool.wait_ge(s_b0, PB_RSTD)
            nc.gpsimd.tensor_tensor(rstd[:, :], rstd[:, :], half_pow[:, 0:B], ALU.pow)\
              .then_inc(s_pool0, 1)
            pool.wait_ge(s_b0, PB_NORM)
            nc.gpsimd.tensor_tensor(tb[:, 3, :], tb[:, 3, :], half_pow[:, B:2 * B], ALU.pow)\
              .then_inc(s_pool0, 1)

            def norm_b(at):
                pool.wait_ge(s_sq, at.count(1, 1))
                if at.rep >= 2:
                    pool.wait_ge(s_hi, at.count(1, -1))
                nc.gpsimd.tensor_tensor(nrm[:, at.odd:at.odd + 1], ssq[:, at.odd:at.odd + 1],
                                        half_pow[:, B:B + 1], ALU.pow).then_inc(s_nr, 1)

            steps(pool, norm_b, 0, B, 2, 2)
            pool.wait_ge(s_c0, 1)
            nc.gpsimd.tensor_tensor(rstd[:, :], rstd[:, :], half_pow[:, 0:B], ALU.pow)\
              .then_inc(s_pool0, 1)
            pool.wait_ge(s_d0, 1)
            nc.gpsimd.tensor_tensor(rstd[:, :], rstd[:, :], half_pow[:, 0:B], ALU.pow)\
              .then_inc(s_pool0, 1)

        @block.scalar
        def _(act):
            act.wait_ge(s_cst, 16 * CONST_DMAS)
            nc.scalar.activation(tg[:, :], gates[:, :], ACT.Tanh).then_inc(s_act0, 1)

            def exp(at, h):
                act.wait_ge(s_st, at.count(16, h + 1))
                if at.rep > 0 or h >= 8:
                    act.wait_ge(s_pv, at.count(4, h // 4 - 1))
                nc.scalar.activation(pT[:, h % 8, :], psST[h % 2][:, :], ACT.Exp,
                                     scale=float(HD) ** -0.5).then_inc(s_exp, 1)

            def store_o(at, pair):
                act.wait_ge(s_pv, at.count(4, 2 * pair + 2))
                if at.rep >= 1:
                    act.wait_ge(s_oc, at.count(128, 0))
                nc.scalar.activation(o_sb[:, 2 * pair:2 * pair + 2, :],
                                     psPV[:, :].rearrange("p (g n) -> p g n", g=2),
                                     ACT.Copy).then_inc(s_oe, 1)

            def store_max(at, hf):
                act.wait_ge(s_mt, at.count(2, hf + 1))
                if at.rep >= 1:
                    last = at.plus(-1)
                    act.wait_ge(s_mx[last.odd][hf], last.half * 16 + 16)
                nc.scalar.activation(nmT[:, hf, :], psMb[0:24, 0:D], ACT.Copy).then_inc(s_me, 1)

            def store_v(at):
                act.wait_ge(s_v, at.count(1, 1))
                if at.rep == 0:
                    act.wait_ge(s_pool0, 5)
                if at.rep >= 2:
                    act.wait_ge(s_pv, at.count(4, -4))
                for c in range(2):
                    ins = nc.scalar.activation(
                        vst[:, at.odd, c, :, 0:HD],
                        psM[:, c * P:c * P + P].rearrange("p (h d) -> p h d", h=H), ACT.Copy)
                ins.then_inc(s_vu, 1)

            def step(at):
                nxt, last = at.plus(1), at.plus(-1)
                for slot in range(8):
                    if at.real():
                        exp(at, 2 * slot)
                        exp(at, 2 * slot + 1)
                    if slot == 0 and last.real():
                        store_o(last, 1)
                    if slot == 1 and at.real():
                        store_max(at, 1)
                    if slot == 3 and nxt.real():
                        store_v(nxt)
                    if slot == 4 and at.real():
                        store_o(at, 0)
                    if slot == 5 and nxt.real():
                        store_max(nxt, 0)

            step(At(-1, 1))
            steps(act, step, 0, B + 1, 2, 2)

            act.wait_ge(s_xA, B)
            act.wait_ge(s_wB, 32)
            nc.scalar.activation(h2[:, :, :], w1[:, :, :], ACT.Abs, accum_out=wsum[:, 0:1])\
              .then_inc(s_b1, 1)
            act.wait_ge(s_b1, 1)
            nc.scalar.activation(h2[:, :, :].rearrange("p c i -> p (c i)"),
                                 w2[:, :, :].rearrange("p c i -> p (c i)"), ACT.Abs,
                                 accum_out=wsum[:, 1:2]).then_inc(s_b1, 1)
            act.wait_ge(s_b0, PB_DONE)

            def store_xiT(at):
                act.wait_ge(s_xiT, at.count(1, 1))
                if at.rep >= 2:
                    act.wait_ge(s_h, at.count(1, -1))
                nc.scalar.activation(xiT[:, at.odd, :, :],
                                     psXT[:, 0:D].rearrange("p (c s) -> p c s", c=2), ACT.Copy)\
                  .then_inc(s_xiTs, 1)

            def gelus(at):
                act.wait_ge(s_h, at.count(1, 1))
                if at.rep >= 1:
                    act.wait_ge(s_sq, at.count(1, 0))
                nc.scalar.activation(h1[:, :], psH[at.odd], ACT.Gelu,
                                     scale=tb[:, 6, bass.ds(at.b, 1)]).then_inc(s_g1, 1)
                act.wait_ge(s_g1, at.count(1, 1))
                if at.rep >= 2:
                    act.wait_ge(s_hi, at.count(1, -1))
                elif at.rep == 0:
                    act.wait_ge(s_b1, 2)
                nc.scalar.activation(h2[:, at.odd, :], h1[:, :], ACT.Gelu).then_inc(s_g2, 1)
                act.wait_ge(s_g2, at.count(1, 1))
                nc.scalar.activation(h1[:, :], h2[:, at.odd, :], ACT.Square,
                                     accum_out=ssq[:, at.odd:at.odd + 1]).then_inc(s_sq, 1)

            def act_b(at):
                if at.plus(1).real():
                    store_xiT(at.plus(1))
                if at.real():
                    gelus(at)

            act_b(At(-1, 1))
            steps(act, act_b, 0, B, 2, 2)

            act.wait_ge(s_xB, B)

            def act_c(at):
                nxt, two = at.plus(1), at.plus(2)
                if two.real():
                    act.wait_ge(s_xcT, two.count(1, 1))
                    if two.rep >= 2:
                        act.wait_ge(s_vC, two.count(1, -1))
                    nc.scalar.activation(xcT[:, two.odd, :, :],
                                         psTx[:, 0:D].rearrange("p (c s) -> p c s", c=2),
                                         ACT.Copy).then_inc(s_xcTs, 1)
                if at.real():
                    act.wait_ge(s_pT, at.count(1, 1))
                    if at.rep >= 1:
                        act.wait_ge(s_oC, at.count(1, 0))
                    nc.scalar.activation(pcT[:, :, :],
                                         psTp[:, 0:D].rearrange("p (c s) -> p c s", c=2),
                                         ACT.Copy).then_inc(s_pTs, 1)
                if nxt.real():
                    act.wait_ge(s_vC, nxt.count(1, 1))
                    if nxt.rep >= 2:
                        act.wait_ge(s_oC, nxt.count(1, -1))
                    nc.scalar.activation(vc[:, nxt.odd, 1, :], psV[:, 0:D], ACT.Copy)\
                      .then_inc(s_vCs, 1)
                if at.real():
                    act.wait_ge(s_oC, at.count(1, 1))
                    if at.rep >= 1:
                        act.wait_ge(s_yC, at.count(1, 0))
                    nc.scalar.activation(oTc[:, :, :],
                                         psO[:, 0:D].rearrange("p (c s) -> p c s", c=2),
                                         ACT.Copy).then_inc(s_oCs, 1)
                if nxt.real():
                    act.wait_ge(s_mC, nxt.count(1, 1))
                    if nxt.rep >= 2:
                        act.wait_ge(s_pT, nxt.count(1, -1))
                    nc.scalar.activation(pc[:, nxt.odd, :], psSc[:, 0:D], ACT.Exp,
                                         bias=smc[:, nxt.odd, 0:1], scale=float(D) ** -0.5,
                                         accum_out=smc[:, nxt.odd, 1:2]).then_inc(s_eC, 1)

            act_c(At(-1, 0))
            act_c(At(-1, 1))
            steps(act, act_c, 0, B, 2, 2)

            act.wait_ge(s_xC, B)
            act.wait_ge(s_d0, PD_WMAX)
            nc.scalar.activation(wgu_hi[:, :, :], wgu[:, :, :], ACT.Copy, scale=wmax[:, 1:2])\
              .then_inc(s_d1, 1)

            def act_route(at):
                act.wait_ge(s_xdT, at.count(1, 1))
                for c in range(2):
                    ins = nc.scalar.activation(xT_hi[:, c, bass.ds(at.b * P, P)],
                                               psTd[at.odd][:, c * P:c * P + P], ACT.Copy)
                ins.then_inc(s_xhi, 1)
                if at.rep >= 2:
                    act.wait_ge(s_xlo, at.count(1, -1))
                    act.wait_ge(s_lg, at.count(1, -1))
                nc.scalar.activation(xdT[:, at.odd, :, :],
                                     psTd[at.odd][:, 0:D].rearrange("p (c s) -> p c s", c=2),
                                     ACT.Copy).then_inc(s_xdTs, 1)
                act.wait_ge(s_lg, at.count(1, 1))
                nc.scalar.activation(lg[:, bass.ds(at.b, 1), :].rearrange("p b e -> p (b e)"),
                                     psLg[at.odd][:, 0:NCO], ACT.Copy).then_inc(s_lgs, 1)

            steps(act, act_route, 0, B, 2, 2)
            act.wait_ge(s_rt, 1)
            nc.scalar.activation(rk[:, 0, :, :], rk[:, 0, :, :], ACT.Exp).then_inc(s_rta, 1)
            nc.scalar.activation(cf[:, :, E], lg[:, :, E], ACT.Exp, scale=-1.0).then_inc(s_rta, 1)
            for g in range(NG):
                act.wait_ge(s_cT, g + 1)
                nc.scalar.activation(cT[:, g * 512:g * 512 + 512],
                                     bank[g].bitcast(BF16)[0:3 * NCO, 0:512], ACT.Copy)\
                  .then_inc(s_cTs, 1)
            act.sem_inc(s_si, 1)
            with act.Fori(0, NG) as g:
                for c in range(NCH):
                    rows = min(P, HID - c * P)
                    act.wait_ge(s_g, g * NCH + (c + 1))
                    act.wait_ge(s_t, g * NCH + max(c, 1))
                    nc.scalar.activation(gs[0:rows, c % 2, :], psG[c % 2][0:rows, :], ACT.Silu,
                                         scale=wmax[0:rows, 0:1]).then_inc(s_si, 1)

        @block.tensor
        def _(pe):
            pe.wait_ge(s_cst, 16 * CONST_DMAS)
            pe.wait_ge(s_prep, 3)
            nc.tensor.matmul(psM[:, 0:1], wA[:, 5, :], smallA[:, 6:7], start=True, stop=True)\
              .then_inc(s_bm, 1)
            pe.wait_ge(s_prep, 4)

            def project_q(at):
                pe.wait_ge(s_xn, at.count(1, 1))
                for w in range(2):
                    ins = nc.tensor.matmul(psM[:, w * D:w * D + D], wA[:, w, :], xn[:, at.odd, :],
                                           start=True, stop=True)
                ins.then_inc(s_q, 1)

            def project_k(at):
                pe.wait_ge(s_ctx[at.odd], at.half * 16 + 16)
                for w in range(2):
                    ins = nc.tensor.matmul(psM[:, w * D:w * D + D], wA[:, 2 + w, :],
                                           ctx_in[:, at.odd, :], start=True, stop=True)
                ins.then_inc(s_k, 1)

            def project_v(at):
                for c in range(2):
                    ins = nc.tensor.matmul(psM[:, c * P:c * P + P],
                                           ctx_in[:, at.odd, c * P:c * P + P], wA[:, 4, :],
                                           start=True, stop=True)
                ins.then_inc(s_v, 1)

            def scores(at, n):
                hf, c, hg = n // 4, (n // 2) % 2, n % 2
                if n in (0, 4):
                    pe.wait_ge(s_stk[at.odd][hf], at.half * 192 + 192)
                if at.rep > 0 or n >= 2:
                    pe.wait_ge(s_max, at.count(8, n - 1))
                for i in range(4):
                    h = 8 * hf + 4 * hg + i
                    ins = nc.tensor.matmul(psS[n % 2][:, i * D:i * D + D],
                                           qst[0:MAXROW, at.odd, h, c * P:c * P + P],
                                           kst[0:MAXROW, at.odd, h, :], start=True, stop=True)
                ins.then_inc(s_s, 1)

            def turn_max(at, hf):
                pe.wait_ge(s_sp, at.count(2, hf + 1))
                for c in range(2):
                    ins = nc.tensor.transpose(psMb[0:24, c * P:c * P + P],
                                              npart[:, hf, c, :, :].rearrange("p a h -> p (a h)"),
                                              identb[:, :])
                ins.then_inc(s_mt, 1)

            def shifted(at, h):
                if h in (0, 8):
                    pe.wait_ge(s_mx[at.odd][h // 8], at.half * 16 + 16)
                if at.rep > 0 or h >= 2:
                    pe.wait_ge(s_exp, at.count(16, h - 1))
                for c in range(2):
                    ins = nc.tensor.matmul(psST[h % 2][:, c * D:c * D + D],
                                           kst[0:MAXROW + 3, at.odd, h, c * P:c * P + P],
                                           qst[0:MAXROW + 3, at.odd, h, :], start=True, stop=True)
                ins.then_inc(s_st, 1)

            def values(at, g):
                pe.wait_ge(s_exp, at.count(16, 4 * g + 4))
                if g == 0:
                    pe.wait_ge(s_vu, at.count(1, 1))
                if g == 0 and at.rep > 0:
                    pe.wait_ge(s_oe, at.count(2, 0))
                if g == 2:
                    pe.wait_ge(s_oe, at.count(2, 1))
                for c in range(2):
                    for j in range(4):
                        h = 4 * g + j
                        ins = nc.tensor.matmul(
                            psPV[32 * j:32 * j + 32, (g % 2) * D:(g % 2) * D + D],
                            vst[:, at.odd, c, h, :], pT[:, h % 8, c * D:c * D + D],
                            start=(c == 0), stop=(c == 1))
                ins.then_inc(s_pv, 1)

            def merge(at):
                pe.wait_ge(s_on, at.count(1, 1))
                nc.tensor.matmul(psM[:, 0:D], wA[:, 5, :], on[:, :], start=True, stop=True)\
                  .then_inc(s_wm, 1)

            def step(at):
                last, nxt, two = at.plus(-1), at.plus(1), at.plus(2)
                for slot in range(8):
                    if at.real():
                        shifted(at, 2 * slot)
                        shifted(at, 2 * slot + 1)
                    if nxt.real():
                        scores(nxt, slot)
                    if slot == 0:
                        if two.real():
                            if at.rep >= -1:
                                if at.rep >= 0:
                                    pe.wait_ge(s_me, at.count(2, 1))
                                else:
                                    pe.wait_ge(s_ku, 1)
                            project_q(two)
                        if last.real():
                            values(last, 3)
                    if slot == 1 and at.real():
                        if two.real():
                            pe.wait_ge(s_qu, two.count(1, 1))
                        else:
                            pe.wait_ge(s_me, at.count(2, 1))
                        turn_max(at, 1)
                    if slot == 2:
                        if two.real():
                            if at.rep >= 0:
                                pe.wait_ge(s_me, at.count(2, 2))
                            else:
                                pe.wait_ge(s_qu, two.count(1, 1))
                            project_k(two)
                        if at.real():
                            values(at, 0)
                    if slot == 3 and nxt.real():
                        if two.real():
                            pe.wait_ge(s_ku, two.count(1, 1))
                        else:
                            pe.wait_ge(s_me, at.count(2, 2))
                        project_v(nxt)
                    if slot == 4:
                        if last.real():
                            if nxt.real():
                                pe.wait_ge(s_vu, nxt.count(1, 1))
                            elif at.real():
                                pe.wait_ge(s_me, at.count(2, 2))
                            else:
                                pe.wait_ge(s_xA, at.count(1, -1))
                            merge(last)
                        if at.real():
                            values(at, 1)
                    if slot == 5 and nxt.real():
                        if last.real():
                            pe.wait_ge(s_xA, last.count(1, 1))
                        else:
                            pe.wait_ge(s_vu, nxt.count(1, 1))
                        turn_max(nxt, 0)
                    if slot == 6 and at.real():
                        values(at, 2)

            for at in (At(-1, 0), At(-1, 1)):
                if at.rep == -2:
                    project_q(at.plus(2))
                    pe.wait_ge(s_qu, 1)
                    project_k(at.plus(2))
                else:
                    step(at)
            steps(pe, step, 0, B + 1, 2, 2)

            pe.wait_ge(s_xA, B)
            pe.wait_ge(s_b1, 2)
            nc.tensor.matmul(psYB[:, 0:2], onesf[:, :], wsum[:, :], start=True, stop=True)\
              .then_inc(s_ws, 1)
            pe.wait_ge(s_b0, PB_DONE)

            def front_b(at):
                pe.wait_ge(s_xi, at.count(1, 1))
                if at.rep >= 1:
                    pe.wait_ge(s_xiTs, at.count(1, 0))
                for c in range(2):
                    ins = nc.tensor.transpose(psXT[:, c * P:c * P + P],
                                              xi[:, at.odd, c * P:c * P + P], identb[:, :])
                ins.then_inc(s_xiT, 1)
                pe.wait_ge(s_xiTs, at.count(1, 1))
                if at.rep >= 2:
                    pe.wait_ge(s_g1, at.count(1, -1))
                for n in range(2):
                    for c in range(2):
                        ins = nc.tensor.matmul(psH[at.odd][:, n * 512:n * 512 + 512],
                                               xiT[:, at.odd, c, :],
                                               w1q[:, c, n * 512:n * 512 + 512],
                                               start=(c == 0), stop=(c == 1))
                ins.then_inc(s_h, 1)

            def back_b(at):
                pe.wait_ge(s_hi, at.count(1, 1))
                if at.rep >= 2:
                    pe.wait_ge(s_hTs, at.count(1, -1))
                for c in range(8):
                    ins = nc.tensor.transpose(psHT[at.odd][:, c * P:c * P + P],
                                              hi[:, at.odd, c * P:c * P + P], identb[:, :])
                ins.then_inc(s_hT, 1)
                pe.wait_ge(s_hTs, at.count(1, 1))
                if at.rep >= 1:
                    pe.wait_ge(s_xB, at.count(1, 0))
                for c in range(8):
                    ins = nc.tensor.matmul(psYB[:, 0:D], hT[:, at.odd, c, :], w2q[:, c, :],
                                           start=(c == 0), stop=(c == 7))
                ins.then_inc(s_yB, 1)

            def step_b(at):
                if at.plus(1).real():
                    front_b(at.plus(1))
                if at.real():
                    back_b(at)

            step_b(At(-1, 1))
            steps(pe, step_b, 0, B, 2, 2)

            pe.wait_ge(s_xB, B)
            pe.wait_ge(s_wC, 16)

            def step_c(at):
                nxt, two = at.plus(1), at.plus(2)
                if two.real():
                    pe.wait_ge(s_xc, two.count(1, 1))
                    if two.rep >= 1:
                        pe.wait_ge(s_xcTs, two.count(1, 0))
                    for c in range(2):
                        ins = nc.tensor.transpose(psTx[:, c * P:c * P + P],
                                                  xc[:, two.odd, c * P:c * P + P], ident[:, :])
                    ins.then_inc(s_xcT, 1)
                if at.real():
                    pe.wait_ge(s_eC, at.count(1, 1))
                    if at.rep >= 1:
                        pe.wait_ge(s_pTs, at.count(1, 0))
                    for c in range(2):
                        ins = nc.tensor.transpose(psTp[:, c * P:c * P + P],
                                                  pc[:, at.odd, c * P:c * P + P], ident[:, :])
                    ins.then_inc(s_pT, 1)
                if nxt.real():
                    pe.wait_ge(s_xcTs, nxt.count(1, 1))
                    if nxt.rep >= 1:
                        pe.wait_ge(s_qkCs, nxt.count(1, 0))
                    for w in range(2):
                        for e in range(2):
                            for c in range(2):
                                ins = nc.tensor.matmul(
                                    psQK[:, w * D + e * P:w * D + e * P + P],
                                    wC[:, w, c, e * P:e * P + P], xcT[:, nxt.odd, c, :],
                                    start=(c == 0), stop=(c == 1))
                    ins.then_inc(s_qkC, 1)
                    if nxt.rep >= 1:
                        pe.wait_ge(s_vCs, nxt.count(1, 0))
                    for c in range(2):
                        ins = nc.tensor.matmul(psV[:, 0:D], xcT[:, nxt.odd, c, :], wC[:, 2, c, :],
                                               start=(c == 0), stop=(c == 1))
                    ins.then_inc(s_vC, 1)
                if at.real():
                    pe.wait_ge(s_pTs, at.count(1, 1))
                    if at.rep >= 1:
                        pe.wait_ge(s_oCs, at.count(1, 0))
                    for e in range(2):
                        for c in range(2):
                            ins = nc.tensor.matmul(psO[:, e * P:e * P + P],
                                                   vc[:, at.odd, c, e * P:e * P + P],
                                                   pcT[:, c, :], start=(c == 0), stop=(c == 1))
                    ins.then_inc(s_oC, 1)
                if nxt.real():
                    pe.wait_ge(s_qkCs, nxt.count(1, 1))
                    pe.wait_ge(s_kv[nxt.odd], nxt.half * 32 + 32)
                    if nxt.rep >= 1:
                        pe.wait_ge(s_eC, nxt.count(1, 0))
                    for e in range(2):
                        ins = nc.tensor.matmul(psSc[:, 0:D], qTc[:, nxt.odd, e, :],
                                               kTc[:, nxt.odd, e, :], start=(e == 0), stop=(e == 1))
                    ins.then_inc(s_sC, 1)
                if at.real():
                    pe.wait_ge(s_oCs, at.count(1, 1))
                    if at.rep >= 1:
                        pe.wait_ge(s_xC, at.count(1, 0))
                    for e in range(2):
                        ins = nc.tensor.matmul(psYC[:, 0:D], oTc[:, e, :], wC[:, 3, e, :],
                                               start=(e == 0), stop=(e == 1))
                    ins.then_inc(s_yC, 1)

            step_c(At(-1, 0))
            step_c(At(-1, 1))
            steps(pe, step_c, 0, B, 2, 2)

            pe.wait_ge(s_xC, B)
            pe.wait_ge(s_d0, 2)
            nc.tensor.transpose(bank[0][0:1, 0:P], wmax[:, 0:1], ident[:, :]).then_inc(s_dP, 1)
            pe.wait_ge(s_d0, 3)
            nc.tensor.matmul(bank[0][:, 256:257], onesf[0:1, :], wmaxr[0:1, 0:1],
                             start=True, stop=True).then_inc(s_dP, 1)

            def turn_x(at):
                pe.wait_ge(s_xd, at.count(1, 1))
                if at.rep >= 2:
                    pe.wait_ge(s_xdTs, at.count(1, -1))
                for c in range(2):
                    ins = nc.tensor.transpose(psTd[at.odd][:, c * P:c * P + P],
                                              xd[:, at.odd, c * P:c * P + P], ident[:, :])
                ins.then_inc(s_xdT, 1)

            def logits(at):
                pe.wait_ge(s_xdTs, at.count(1, 1))
                if at.rep >= 2:
                    pe.wait_ge(s_lgs, at.count(1, -1))
                for c in range(2):
                    ins = nc.tensor.matmul(psLg[at.odd][:, 0:NCO], xdT[:, at.odd, c, :],
                                           wr[:, c, :], start=(c == 0), stop=(c == 1))
                ins.then_inc(s_lg, 1)

            def pe_route(at):
                turn_x(at)
                logits(at)

            pe.wait_ge(s_wD, 16 * 5)
            steps(pe, pe_route, 0, B, 2, 2)
            pe.wait_ge(s_rt, RT_DONE)
            for b in range(B):
                ins = nc.tensor.transpose(
                    bank[b // 4].bitcast(BF16)[0:3 * NCO, (b % 4) * P:(b % 4) * P + P],
                    cfp[:, b, :, :].rearrange("p a e -> p (a e)"), identb[:, :])
                if b % 4 == 3:
                    ins.then_inc(s_cT, 1)
            pe.wait_ge(s_cTs, NG)
            pe.wait_ge(s_d0, PD_DONE)
            pe.sem_inc(s_dn, 1)
            with pe.Fori(0, NG) as g:
                def down(c):
                    rows = min(P, HID - c * P)
                    pe.wait_ge(s_hd, g * NCH + (c + 2))
                    if c == 0:
                        pe.wait_ge(s_yD, g + 1)
                    for n in range(GROUP):
                        ins = nc.tensor.matmul(acc[:, n * D:n * D + D],
                                               hd[0:rows, c % 3, n * P:n * P + P],
                                               wd[0:rows, c, :], start=(c == 0 and n % 2 == 0),
                                               stop=(c == NCH - 1), skip_group_check=True)
                    ins.then_inc(s_dn, 1)

                for c in range(NCH):
                    rows = min(P, HID - c * P)
                    for ps, first_col, free, done in ((psG, 0, s_si, s_g), (psU, HID, s_t, s_u)):
                        pe.wait_ge(free, g * NCH + max(c, 1))
                        if rows < P:
                            apart(pe)
                        k = 0
                        for d in range(2):
                            cols = slice(first_col + c * P, first_col + c * P + rows)
                            for w, x in ((wgu_hi, xT_hi), (wgu_hi, xT_lo), (wgu_lo, xT_hi)):
                                ins = nc.tensor.matmul(ps[c % 2][0:rows, :], w[:, d, cols],
                                                       x[:, d, bass.ds(g * 512, 512)],
                                                       start=(k == 0), stop=(k == 5))
                                k += 1
                        ins.then_inc(done, 1)
                    pe.wait_ge(s_hd, g * NCH + max(c, 1))
                    apart(pe)
                    nc.tensor.matmul(psC[c % 2], sel[:, c * P:c * P + P],
                                     cT[:, bass.ds(g * 512, 512)], start=True, stop=True)\
                      .then_inc(s_c, 1)
                    if c >= 1:
                        down(c - 1)
                down(NCH - 1)

        @block.vector
        def _(dve):
            nc.vector.memset(kst[:, :, :, :].bitcast(F32), 0.0).then_inc(s_dve, 1)
            dve.wait_ge(s_dve, 1)
            nc.vector.memset(kst[MAXROW:MAXROW + 3, :, :, :], 1.0).then_inc(s_prep, 1)
            for b in range(B):
                if b % 4 == 0:
                    dve.wait_ge(s_x[b // 4], 16)
                nc.vector.bn_stats(bnst[:, b % 2, :], x_all[:, b, :]).then_inc(s_dve, 1)
                dve.wait_ge(s_dve, 2 + 2 * b)
                nc.vector.bn_aggr(stat[:, b, :], bnst[:, b % 2, :]).then_inc(s_dve, 1)
            n = 1 + 2 * B
            dve.wait_ge(s_dve, n)
            nc.vector.tensor_scalar(rstd[:, :], stat[:, :, 1], EPS, None, ALU.add)\
              .then_inc(s_prep, 1)
            dve.wait_ge(s_cst, 16 * CONST_DMAS)
            dve.wait_ge(s_act0, 1)
            nc.vector.tensor_scalar(rot[:, 1, :], rot[:, 1, :], smallA[:, 4:5], None, ALU.mult)
            nc.vector.tensor_copy(identb[:, :], ident[:, :])
            nc.vector.tensor_scalar(wA[:, 5, :], wA[:, 5, :], tg[:, 0:1], None, ALU.mult)\
              .then_inc(s_prep, 1)
            dve.wait_ge(s_bm, 1)
            nc.vector.scalar_tensor_tensor(tgbm[:, :], smallA[:, 5:6], tg[:, 0:1], psM[:, 0:1],
                                           ALU.mult, ALU.add).then_inc(s_prep, 1)
            dve.wait_ge(s_prep, 4)
            dve.wait_ge(s_pool0, 7)

            def normalise(at):
                if at.rep >= 2:
                    dve.wait_ge(s_q, at.count(1, -1))
                nc.vector.tensor_scalar(xn[:, at.odd, :], x_all[:, bass.ds(at.b, 1), :].rearrange("p b d -> p (b d)"),
                                        stat[:, bass.ds(at.b, 1), 0], rstd[:, bass.ds(at.b, 1)],
                                        ALU.subtract, ALU.mult).then_inc(s_xn, 1)

            def rotate(at, w, made, used, ready):
                dve.wait_ge(made, at.count(1, 1))
                if at.rep >= 1:
                    dve.wait_ge(ready, at.count(1, 0))
                for i in range(2):
                    ins = nc.vector.scalar_tensor_tensor(
                        rt[:, w, i, :], psM[:, i * D:i * D + D],
                        smallA[:, 2 * w + i:2 * w + i + 1], rot[:, i, :], ALU.add, ALU.mult)
                ins.then_inc(used, 1)

            def maximum(at, n):
                hf, c, hg = n // 4, (n // 2) % 2, n % 2
                dve.wait_ge(s_s, at.count(8, n + 1))
                if n == 0 and at.rep >= 2:
                    dve.wait_ge(s_sp, at.count(2, -2))
                nc.vector.tensor_reduce(
                    nmax[:, at.odd, hf, c, 4 * hg:4 * hg + 4],
                    psS[n % 2][:, :].rearrange("p (h m) -> p h m", h=4), AX.X, ALU.max,
                    negate=True).then_inc(s_max, 1)

            def split_max(at, hf):
                dve.wait_ge(s_max, at.count(8, 4 * hf + 4))
                if at.rep >= 1:
                    dve.wait_ge(s_mt, at.count(2, hf - 1))
                base = at.count(6, 3 * hf) + n
                m = nmax[:, at.odd, hf, :, :]
                nc.vector.tensor_copy(npart[:, hf, :, 0, :], m).then_inc(s_dve, 1)
                dve.wait_ge(s_dve, base + 1)
                nc.vector.tensor_tensor(nres[:, :, :], m, npart[:, hf, :, 0, :], ALU.subtract)\
                  .then_inc(s_dve, 1)
                dve.wait_ge(s_dve, base + 2)
                nc.vector.tensor_copy(npart[:, hf, :, 1, :], nres[:, :, :]).then_inc(s_dve, 1)
                dve.wait_ge(s_dve, base + 3)
                nc.vector.tensor_tensor(npart[:, hf, :, 2, :], nres[:, :, :],
                                        npart[:, hf, :, 1, :], ALU.subtract).then_inc(s_sp, 1)

            def divide(at):
                dve.wait_ge(s_oc, at.count(128, 128))
                nc.vector.reciprocal(rden[:, :], oc[:, 1, :]).then_inc(s_rd, 1)
                dve.wait_ge(s_rd, at.count(1, 1))
                if at.rep >= 1:
                    dve.wait_ge(s_wm, at.count(1, 0))
                nc.vector.tensor_tensor(on[:, :], oc[:, 0, :], rden[:, :], ALU.mult)\
                  .then_inc(s_on, 1)

            def update(at):
                dve.wait_ge(s_wm, at.count(1, 1))
                xb = x_all[:, bass.ds(at.b, 1), :].rearrange("p b d -> p (b d)")
                nc.vector.scalar_tensor_tensor(xb, psM[:, 0:D], tgbm[:, 0:1], xb,
                                               ALU.add, ALU.add).then_inc(s_xA, 1)

            def statistics(at):
                dve.wait_ge(s_xA, at.count(1, 1))
                if at.rep >= 1:
                    dve.wait_ge(s_st_r, at.count(1, 0))
                apart(dve)
                nc.vector.bn_stats(bnst[:, 0, :],
                                   x_all[:, bass.ds(at.b, 1), :].rearrange("p b d -> p (b d)"))\
                  .then_inc(s_bn, 1)
                dve.wait_ge(s_bn, at.count(1, 1))
                apart(dve)
                nc.vector.bn_aggr(agg[:, :], bnst[:, 0, :]).then_inc(s_ag, 1)
                dve.wait_ge(s_ag, at.count(1, 1))
                nc.vector.tensor_scalar(stat[:, bass.ds(at.b, 1), :].rearrange("p b d -> p (b d)"),
                                        agg[:, :], 0.0, None, ALU.add).then_inc(s_st_r, 1)

            def step(at):
                last, nxt, two, three = at.plus(-1), at.plus(1), at.plus(2), at.plus(3)
                for slot in range(8):
                    if slot == 0 and at.real():
                        split_max(at, 1)
                    if nxt.real():
                        maximum(nxt, slot)
                    if slot == 0 and two.real():
                        rotate(two, 0, s_q, s_qu, s_qp)
                    if slot == 2 and two.real():
                        rotate(two, 1, s_k, s_ku, s_kp)
                    if slot == 3 and last.real():
                        divide(last)
                    if slot == 4:
                        if nxt.real():
                            split_max(nxt, 0)
                        if last.real():
                            update(last)
                    if slot == 5 and last.real():
                        statistics(last)
                    if slot == 6 and three.real():
                        normalise(three)

            normalise(At(0, 0))
            normalise(At(0, 1))
            rotate(At(0, 0), 0, s_q, s_qu, s_qp)
            rotate(At(0, 0), 1, s_k, s_ku, s_kp)
            step(At(-1, 1))
            steps(dve, step, 0, B + 1, 2, 4)

            v = Chain(dve, s_vb)
            tt, ts = nc.vector.tensor_tensor, nc.vector.tensor_scalar
            dve.wait_ge(s_st_r, B)
            mean, var = stat[:, :, 0], stat[:, :, 1]
            ts(rstd[:, :], var, EPS, None, ALU.add).then_inc(s_b0, 1)
            v(nc.vector.tensor_reduce(tb[:, 0, :], x_all[:, :, :], AX.X, ALU.max))
            v(nc.vector.tensor_reduce(tb[:, 1, :], x_all[:, :, :], AX.X, ALU.min))
            v.wait()
            v(tt(tb[:, 0, :], tb[:, 0, :], mean, ALU.subtract))
            v(tt(tb[:, 1, :], mean, tb[:, 1, :], ALU.subtract))
            v.wait()
            dve.wait_ge(s_pool0, 8)
            v(tt(tb[:, 0, :], tb[:, 0, :], tb[:, 1, :], ALU.max))
            v(tt(tb[:, 3, :], var, rstd[:, :], ALU.mult))
            v.wait()
            v(tt(tb[:, 2, :], tb[:, 0, :], rstd[:, :], ALU.mult))
            v(tt(tb[:, 4, :], tb[:, 3, :], rstd[:, :], ALU.mult))
            v.wait()
            ts(tb[:, 3, :], tb[:, 4, :], float(D), None, ALU.mult).then_inc(s_b0, 1)
            dve.wait_ge(s_pool0, 9)
            v(ts(tb[:, 3, :], tb[:, 3, :], 1e-12, None, ALU.max))
            v.wait()
            v(nc.vector.reciprocal(tb[:, 4, :], tb[:, 3, :]))
            v.wait()
            v(tt(tb[:, 5, :], tb[:, 2, :], tb[:, 4, :], ALU.mult))
            v(tt(tb[:, 0, :], tb[:, 4, :], rstd[:, :], ALU.mult))
            v.wait()
            v(ts(tb[:, 5, :], tb[:, 5, :], float(D) ** 0.5, EPS, ALU.mult, ALU.max))
            v.wait()
            v(nc.vector.reciprocal(tb[:, 7, :], tb[:, 5, :]))
            v.wait()
            v(tt(tb[:, 7, :], tb[:, 7, :], tb[:, 0, :], ALU.mult))
            v.wait()
            v(ts(tb[:, 7, :], tb[:, 7, :], 127.0 * float(D) ** 0.5, None, ALU.mult))
            dve.wait_ge(s_ws, 1)
            v(ts(wmean[:, :], psYB[:, 0:2], 1.0 / (INNER * D), EPS, ALU.mult, ALU.max))
            v.wait()
            v(nc.vector.reciprocal(wscale[:, :], wmean[:, :]))
            v(ts(tb[:, 6, :], tb[:, 5, :], wmean[:, 0:1], 1.0 / 127.0, ALU.mult, ALU.mult))
            v(ts(dqw[:, :], wmean[:, 1:2], tg[:, 2:3], 1.0 / 127.0, ALU.mult, ALU.mult))
            v.wait()
            dve.wait_ge(s_wB, 32)
            for n, (w, wq) in enumerate(((w1, w1q), (w2, w2q))):
                w, wq = (t.rearrange("p c i -> p (c i)") for t in (w, wq))
                v(ts(w, w, wscale[:, n:n + 1], ROUND, ALU.mult, ALU.add))
                v.wait()
                v(ts(w, w, ROUND, 1.0, ALU.subtract, ALU.min))
                v.wait()
                v(ts(wq, w, -1.0, None, ALU.max))
            v.wait()
            ts(tb[:, 1, :], tb[:, 0, :], 1.0, None, ALU.mult).then_inc(s_b0, 1)

            def xb(at):
                return x_all[:, bass.ds(at.b, 1), :].rearrange("p b d -> p (b d)")

            def round_x(at):
                if at.rep >= 1:
                    dve.wait_ge(s_xi, at.count(1, 0))
                ts(xr[:, :], xb(at), stat[:, bass.ds(at.b, 1), 0], tb[:, 7, bass.ds(at.b, 1)],
                   ALU.subtract, ALU.mult).then_inc(s_xr, 1)
                dve.wait_ge(s_xr, at.count(1, 1))
                if at.rep >= 2:
                    dve.wait_ge(s_xiT, at.count(1, -1))
                ts(xi[:, at.odd, :], xr[:, :], ROUND, ROUND, ALU.add, ALU.subtract)\
                    .then_inc(s_xi, 1)

            def round_h(at):
                q = tq[:, at.odd, :]
                col = lambda n: q[:, n:n + 1]
                steps_ = [0]
                def done(ins):
                    steps_[0] += 1
                    ins.then_inc(s_tq, 1)
                    dve.wait_ge(s_tq, at.count(8, steps_[0]))
                dve.wait_ge(s_g2, at.count(1, 1))
                if at.rep >= 2:
                    dve.wait_ge(s_xB, at.count(1, -1))
                done(nc.vector.tensor_reduce(col(0), h2[:, at.odd, :], AX.X, ALU.max,
                                             apply_absolute_value=True))
                dve.wait_ge(s_nr, at.count(1, 1))
                done(ts(col(1), nrm[:, at.odd:at.odd + 1], 1e-12, None, ALU.max))
                done(nc.vector.reciprocal(col(2), col(1)))
                done(ts(col(3), col(0), col(2), float(INNER) ** 0.5, ALU.mult, ALU.mult))
                done(ts(col(4), col(3), EPS, None, ALU.max))
                done(nc.vector.reciprocal(col(5), col(4)))
                ts(col(7), col(4), dqw[:, 0:1], None, ALU.mult)
                done(ts(col(6), col(5), col(2), 127.0 * float(INNER) ** 0.5, ALU.mult, ALU.mult))
                done(ts(hr, h2[:, at.odd, :], col(6), ROUND, ALU.mult, ALU.add))
                if at.rep >= 2:
                    dve.wait_ge(s_hT, at.count(1, -1))
                ts(hi[:, at.odd, :], hr, ROUND, None, ALU.subtract).then_inc(s_hi, 1)

            def store_hT(at):
                dve.wait_ge(s_hT, at.count(1, 1))
                if at.rep >= 2:
                    dve.wait_ge(s_yB, at.count(1, -1))
                nc.vector.tensor_copy(hT[:, at.odd, :, :],
                                      psHT[at.odd].rearrange("p (c s) -> p c s", c=8))\
                  .then_inc(s_hTs, 1)

            def new_stats(at, updated, bn, ready):
                dve.wait_ge(updated, at.count(1, 1))
                if at.rep >= 1:
                    dve.wait_ge(ready, at.count(1, 0))
                apart(dve)
                nc.vector.bn_stats(bnst[:, 0, :], xb(at)).then_inc(bn, 1)
                dve.wait_ge(bn, at.count(2, 1))
                apart(dve)
                nc.vector.bn_aggr(agg[:, :], bnst[:, 0, :]).then_inc(bn, 1)
                dve.wait_ge(bn, at.count(2, 2))
                ts(stat[:, bass.ds(at.b, 1), :].rearrange("p b d -> p (b d)"), agg[:, :], 0.0,
                   None, ALU.add).then_inc(ready, 1)

            def update_b(at):
                dve.wait_ge(s_yB, at.count(1, 1))
                nc.vector.scalar_tensor_tensor(xb(at), psYB[:, 0:D], tq[:, at.odd, 7:8], xb(at),
                                               ALU.mult, ALU.add).then_inc(s_xB, 1)
                new_stats(at, s_xB, s_bnB, s_stB)

            def step_b(at):
                if at.real():
                    round_h(at)
                if at.plus(-1).real():
                    update_b(at.plus(-1))
                if at.plus(2).real():
                    round_x(at.plus(2))
                if at.real():
                    store_hT(at)

            step_b(At(-1, 0))
            step_b(At(-1, 1))
            steps(dve, step_b, 0, B + 1, 2, 2)

            dve.wait_ge(s_stB, B)
            ts(rstd[:, :], var, EPS, None, ALU.add).then_inc(s_c0, 1)
            dve.wait_ge(s_pool0, 10)

            def normal_c(at):
                if at.rep >= 2:
                    dve.wait_ge(s_xcT, at.count(1, -1))
                ts(xc[:, at.odd, :], xb(at), stat[:, bass.ds(at.b, 1), 0],
                   rstd[:, bass.ds(at.b, 1)], ALU.subtract, ALU.mult).then_inc(s_xc, 1)

            def step_c(at):
                nxt, three = at.plus(1), at.plus(3)
                if nxt.real():
                    dve.wait_ge(s_qkC, nxt.count(1, 1))
                    if nxt.rep >= 2:
                        dve.wait_ge(s_sC, nxt.count(1, -1))
                    nc.vector.tensor_copy(qTc[:, nxt.odd, :, :],
                                          psQK[:, 0:D].rearrange("p (c s) -> p c s", c=2))
                    nc.vector.tensor_copy(kTc[:, nxt.odd, :, P:D],
                                          psQK[:, D:2 * D].rearrange("p (c s) -> p c s", c=2))\
                      .then_inc(s_qkCs, 1)
                if at.real():
                    dve.wait_ge(s_eC, at.count(1, 1))
                    nc.vector.reciprocal(smc[:, at.odd, 2:3], smc[:, at.odd, 1:2])\
                      .then_inc(s_r0, 1)
                    dve.wait_ge(s_r0, at.count(1, 1))
                    if at.rep >= 2:
                        dve.wait_ge(s_xC, at.count(1, -1))
                    ts(smc[:, at.odd, 3:4], smc[:, at.odd, 2:3], tg[:, 1:2], None, ALU.mult)\
                        .then_inc(s_rC, 1)
                if nxt.real():
                    dve.wait_ge(s_sC, nxt.count(1, 1))
                    nc.vector.tensor_reduce(mxc[:, nxt.odd:nxt.odd + 1], psSc[:, 0:D], AX.X,
                                            ALU.max, negate=True).then_inc(s_c1, 1)
                    dve.wait_ge(s_c1, nxt.count(1, 1))
                    if nxt.rep >= 2:
                        dve.wait_ge(s_eC, nxt.count(1, -1))
                    ts(smc[:, nxt.odd, 0:1], mxc[:, nxt.odd:nxt.odd + 1], float(D) ** -0.5, None,
                       ALU.mult).then_inc(s_mC, 1)
                if at.real():
                    dve.wait_ge(s_yC, at.count(1, 1))
                    dve.wait_ge(s_rC, at.count(1, 1))
                    nc.vector.scalar_tensor_tensor(xb(at), psYC[:, 0:D], smc[:, at.odd, 3:4],
                                                   xb(at), ALU.mult, ALU.add).then_inc(s_xC, 1)
                    new_stats(at, s_xC, s_bnC, s_stC)
                if three.real():
                    normal_c(three)

            normal_c(At(0, 0))
            step_c(At(-1, 0))
            step_c(At(-1, 1))
            steps(dve, step_c, 0, B, 2, 4)

            dve.wait_ge(s_stC, B)
            ts(rstd[:, :], var, EPS, None, ALU.add).then_inc(s_d0, 1)
            dve.wait_ge(s_wD, 16 * 5)
            nc.vector.tensor_reduce(wmax[:, 0:1], wgu.rearrange("p c n -> p (c n)"), AX.X, ALU.max,
                                    apply_absolute_value=True).then_inc(s_d0, 1)
            dve.wait_ge(s_dP, 1)
            nc.vector.tensor_reduce(wmaxr[:, 0:1], bank[0][0:1, 0:P], AX.X, ALU.max)\
              .then_inc(s_d0, 1)
            dve.wait_ge(s_dP, 2)
            ts(wmax[:, 0:1], bank[0][:, 256:257], 1e-30, None, ALU.max).then_inc(s_d0, 1)
            dve.wait_ge(s_d0, 4)
            nc.vector.reciprocal(wmax[:, 1:2], wmax[:, 0:1]).then_inc(s_d0, 1)
            dve.wait_ge(s_d1, 1)
            for c in range(2):
                nc.vector.scalar_tensor_tensor(wgu_lo[:, c, :], wgu[:, c, :], wmax[:, 1:2],
                                               wgu_hi[:, c, :], ALU.mult, ALU.subtract)
            nc.vector.tensor_copy(sel, self_).then_inc(s_d0, 1)
            dve.wait_ge(s_pool0, 11)

            def normal_d(at):
                if at.rep >= 2:
                    dve.wait_ge(s_xdT, at.count(1, -1))
                ts(xd[:, at.odd, :], xb(at), stat[:, bass.ds(at.b, 1), 0],
                   rstd[:, bass.ds(at.b, 1)], ALU.subtract, ALU.mult).then_inc(s_xd, 1)

            def step_r(at):
                if at.plus(1).real():
                    normal_d(at.plus(1))
                if at.real():
                    dve.wait_ge(s_xdTs, at.count(1, 1))
                    cols = bass.ds(at.b * P, P)
                    for c in range(2):
                        ins = tt(xT_lo[:, c, cols], xdT[:, at.odd, c, :],
                                 xT_hi[:, c, cols], ALU.subtract)
                    ins.then_inc(s_xlo, 1)

            step_r(At(-1, 1))
            steps(dve, step_r, 0, B, 2, 2)

            u = Chain(dve, s_ur)
            dve.wait_ge(s_lgs, B)
            l8 = lg[:, :, 0:E]
            u(nc.vector.tensor_reduce(den[:, :], l8, AX.X, ALU.max))
            u.wait()
            wide = lambda t: t.unsqueeze(2).to_broadcast([P, B, E])
            tt(rk[:, 0, :, :], l8, wide(den[:, :]), ALU.subtract).then_inc(s_rt, 1)
            dve.wait_ge(s_rta, 2)
            other = rk[:, 0, :, :].unsqueeze(2).to_broadcast([P, B, E, E])
            own = rk[:, 0, :, :].unsqueeze(3).to_broadcast([P, B, E, E])
            cm = [cmp_[:, n, :].rearrange("p (b e j) -> p b e j", b=B, e=E) for n in range(2)]
            cf2 = [cmp_[:, n, :].rearrange("p (b k) -> p b k", b=B) for n in range(2)]
            tr = [tri[:, n, :].unsqueeze(1).to_broadcast([P, B, E * E]) for n in range(2)]
            u(tt(cm[0], other, own, ALU.is_ge))
            u(tt(cm[1], other, own, ALU.is_gt))
            u.wait()
            u(tt(cf2[0], cf2[0], tr[0], ALU.mult))
            u(tt(cf2[1], cf2[1], tr[1], ALU.mult))
            u.wait()
            u(tt(cmp_[:, 0, :], cmp_[:, 0, :], cmp_[:, 1, :], ALU.add))
            u.wait()
            u(nc.vector.tensor_reduce(rk[:, 1, :, :], cm[0], AX.X, ALU.add))
            u.wait()
            u(ts(rk[:, 1, :, :], rk[:, 1, :, :], 2.0, None, ALU.is_lt))
            u.wait()
            u(tt(rk[:, 2, :, :], rk[:, 0, :, :], rk[:, 1, :, :], ALU.mult))
            u.wait()
            u(nc.vector.tensor_reduce(den[:, :], rk[:, 2, :, :], AX.X, ALU.add))
            u.wait()
            u(nc.vector.reciprocal(den[:, :], den[:, :]))
            u.wait()
            u(tt(cf[:, :, 0:E], rk[:, 2, :, :], wide(den[:, :]), ALU.mult))
            u(ts(cf[:, :, E], cf[:, :, E], 1.0, None, ALU.add))
            u.wait()
            u(nc.vector.reciprocal(cf[:, :, E], cf[:, :, E]))
            u.wait()
            u(ts(cf[:, :, :], cf[:, :, :], tg[:, 3:4], None, ALU.mult))
            u.wait()
            u(nc.vector.tensor_copy(cfp[:, :, 0, :], cf[:, :, :]))
            u.wait()
            u(tt(cfr[:, :, :], cf[:, :, :], cfp[:, :, 0, :], ALU.subtract))
            u.wait()
            u(nc.vector.tensor_copy(cfp[:, :, 1, :], cfr[:, :, :]))
            u.wait()
            tt(cfp[:, :, 2, :], cfr[:, :, :], cfp[:, :, 1, :], ALU.subtract).then_inc(s_rt, 1)
            for s_credit in (s_t, s_hd, s_yD):
                dve.sem_inc(s_credit, 1)
            with dve.Fori(0, NG) as g:
                for c in range(NCH):
                    rows = min(P, HID - c * P)
                    dve.wait_ge(s_si, g * NCH + (c + 2))
                    dve.wait_ge(s_u, g * NCH + (c + 1))
                    nc.vector.scalar_tensor_tensor(hu[0:rows, c % 2, :], psU[c % 2][0:rows, :],
                                                   wmax[0:rows, 0:1], gs[0:rows, c % 2, :],
                                                   ALU.mult, ALU.mult).then_inc(s_t, 1)
                    dve.wait_ge(s_t, g * NCH + (c + 2))
                    dve.wait_ge(s_c, g * NCH + (c + 1))
                    dve.wait_ge(s_dn, g * NCH + max(c - 1, 1))
                    tt(hd[0:rows, c % 3, :], hu[0:rows, c % 2, :], psC[c % 2][0:rows, :],
                       ALU.mult).then_inc(s_hd, 1)
                dve.wait_ge(s_dn, g * NCH + (NCH + 1))
                xg = x_all[:, bass.ds(g * GROUP, GROUP), :].rearrange("p b d -> p (b d)")
                tt(xg, acc, xg, ALU.add).then_inc(s_yD, 1)


def host_arrays(i):
    f = lambda n: np.asarray(i[n])
    qk = np.array([d * H + hf * 8 + h for hf in range(2) for d in range(HD) for h in range(8)])
    swap = np.array([(d ^ 1) * H + hf * 8 + h for hf in range(2) for d in range(HD) for h in range(8)])
    vh = np.array([d * H + h for h in range(H) for d in range(HD)])
    mg = np.array([d * H + 4 * g + j for j in range(4) for d in range(HD) for g in range(4)])
    wq, wk, wv, wm = (f(f"L0_xattn_{n}") for n in ("Wq", "Wk", "Wv", "Wm"))
    bq, bk, bv, bm = (f(f"L0_xattn_{n}") for n in ("bq", "bk", "bv", "bm"))
    sign = np.array([1.0 if d % 2 else -1.0 for _ in range(2) for d in range(HD) for _ in range(8)],
                    np.float32)
    enc = f("L0_xattn_encoding")[:, 0, 0]
    dim = np.array([d for _ in range(2) for d in range(HD) for _ in range(8)])
    pad = np.zeros(P, np.float32)
    chunks = lambda w: w.reshape(-1, P, w.shape[1]).transpose(1, 0, 2)
    flat = lambda w: w.transpose(1, 0, 2).reshape(D, E * I)
    wgu = np.concatenate([flat(f("L1_ffn_w_gate")), f("L1_ffn_sw_gate"),
                          flat(f("L1_ffn_w_up")), f("L1_ffn_sw_up")], 1)
    wd = np.zeros((NCH * P, D), np.float32)
    wd[:HID] = np.concatenate([f("L1_ffn_w_down").reshape(E * I, D), f("L1_ffn_sw_down")], 0)
    expert = np.minimum(np.arange(NCH * P) // I, E)
    sel = np.tile(np.arange(NCO)[:, None] == expert[None, :], (3, 1)).astype(np.float32)
    j, e = np.arange(E)[None, :], np.arange(E)[:, None]
    tri = np.stack([(j < e).ravel(), (j > e).ravel()]).astype(np.float32)
    return {
        "w1": chunks(f("L0_ffn_w1").T), "w2": chunks(f("L0_ffn_w2").T),
        "wC": np.stack([chunks(f(f"L1_xattn_{n}").T) for n in ("wq", "wk", "wv", "wo")], 1),
        "ctxT": f("ctx_2048").transpose(0, 2, 1),
        "wgu": chunks(wgu), "wd": chunks(wd),
        "wr": chunks(np.concatenate([f("L1_ffn_gate_w").T, f("L1_ffn_shared_gate_w")], 1)),
        "sel": sel, "tri": tri,
        "x": f("x"), "ctx": f("ctx_2048"), "g_xattn": f("g_xattn"), "g_ffn": f("g_ffn"),
        "wA": np.stack([wq[qk].T, wq[swap].T, wk[qk].T, wk[swap].T, wv[vh].T, wm[:, mg].T], 1),
        "smallA": np.stack([bq[qk], bq[swap], bk[qk], bk[swap], sign, bm, bv[mg], pad], 1),
        "rot": np.stack([enc[0][:, dim].T, enc[1][:, dim].T], 1),
        "ident": np.eye(P, dtype=np.float32),
    }


def kernel(**inputs):
    import concourse.bacc as bacc
    from concourse.bass_utils import run_bass_kernel_spmd as run

    nc = bacc.Bacc("TRN2", target_bir_lowering=False, num_devices=1)
    arrays = {n: np.ascontiguousarray(v) for n, v in host_arrays(inputs).items()}
    a = {n: nc.dram_tensor(f"in_{n}", v.shape, mybir.dt.from_np(v.dtype), kind="ExternalInput").ap()
         for n, v in arrays.items()}
    out = nc.dram_tensor("out_x", (B, P, D), F32, kind="ExternalOutput").ap()
    build(nc, a, out)
    r = run(nc, [{f"in_{n}": v for n, v in arrays.items()}], core_ids=[0])
    return r.results[0]["out_x"]
```

```python
from contextlib import ExitStack

import numpy as np

import concourse.bass as bass
from concourse import mybir

F32 = mybir.dt.float32
BF16 = mybir.dt.bfloat16
F16 = mybir.dt.float16
ALU = mybir.AluOpType
ACT = mybir.ActivationFunctionType
AX = mybir.AxisListType

P = 128
B = 16
D = 256
H, HD = 16, 8
INNER = 1024
E, I, IS = 8, 176, 704
HID = E * I + IS
NCH = -(-HID // P)
NCO = E + 1
GROUP = 4
NG = B // GROUP
EPS = 1e-5
ROUND = 1.5 * 2.0 ** 23
NPART = 3
STACK = NPART * NPART * HD
MAXROW = 96


class At:

    def __init__(self, half, odd, rep=None):
        self.half, self.odd = half, odd
        self.rep = 2 * half + odd if rep is None else rep

    def plus(self, k):
        n = self.odd + k
        return At(self.half + n // 2, n % 2, self.rep + k)

    @property
    def b(self):
        return self.half * 2 + self.odd

    def count(self, per, more):
        return self.half * (2 * per) + (self.odd * per + more)

    def real(self):
        return 0 <= self.rep < B


def steps(eng, body, first, last, lead, tail):
    for n in range(first, lead):
        body(At(n // 2, n % 2))
    with eng.Fori(lead // 2, (B - tail) // 2) as half:
        body(At(half, 0, lead))
        body(At(half, 1, lead + 1))
    for n in range(B - tail, last):
        body(At(n // 2, n % 2))


def build(nc, a, out):
    ctx = ExitStack()
    with ctx:
        def sb(name, shape, dt=F32):
            return ctx.enter_context(nc.sbuf_tensor(name, shape, dt))

        def sem(name):
            return ctx.enter_context(nc.semaphore(name))

        class Arena:

            def __init__(self, name, words):
                self.t, self.words, self.at = sb(name, [P, words]), words, 0

            def __call__(self, shape, dt=F32, rows=P):
                n = int(np.prod(shape)) if dt is F32 else int(np.prod(shape)) // 2
                v = self.t[0:rows, self.at:self.at + n]
                self.at += n
                assert self.at <= self.words, (self.at, self.words)
                v = v if dt is F32 else v.bitcast(dt)
                names = "abcd"[:len(shape)]
                if len(shape) == 1:
                    return v
                return v.rearrange(f"p ({' '.join(names)}) -> p {' '.join(names)}",
                                   **{k: n for k, n in zip(names, shape)})

        first = Arena("first_arena", 15360)
        qst = first([2, H, D], BF16)
        kst = first([2, H, D], BF16)
        pT = first([8, 2 * D])
        vst = first([2, 2, H, 32])
        o_sb = first([4, D])
        first.at = 0
        wgu = first([2, 2 * HID])
        wd = first([NCH, D])
        wC = first([4, 2, D])
        second = Arena("second_arena", 2 * 2 * HID)
        w1 = second([2, INNER])
        w2 = second([8, D])
        second.at = 0
        wgu_hi = second([2, 2 * HID], F16)
        wgu_lo = second([2, 2 * HID], F16)
        third = Arena("third_arena", 9856)
        w1q = third([2, INNER], BF16)
        w2q = third([8, D], BF16)
        h1 = third([INNER])
        h2 = third([2, INNER])
        hr = third([2, INNER])
        hT = third([2, 8, P], BF16)
        third.at = 0
        kTc = third([2, 2, D])
        vc = third([2, 2, D])
        xc = third([2, D])
        xcT = third([2, 2, P])
        qTc = third([2, 2, P])
        pc = third([2, D])
        pcT = third([2, P])
        oTc = third([2, P])
        third.at = 0
        gs = third([2, 512])
        hu = third([2, 512])
        hd = third([3, 512])
        third.at = 0
        cmp_ = third([2, B * E * E])
        third.at = 9 * 512
        self_ = third([NCH * P], rows=3 * NCO)
        sel = third([NCH * P], BF16, rows=3 * NCO)
        cT = third([B * P], BF16, rows=3 * NCO)

        fourth = Arena("fourth_arena", 5632)
        ctx_in = fourth([2, D])
        xn = fourth([2, D])
        rt = fourth([2, 2, D])
        res = fourth([2, D])
        parts = fourth([2, 2, 3, D], BF16)
        oc = fourth([2, D])
        rden = fourth([D])
        on = fourth([D])
        fourth.at = 0
        xT_hi = fourth([2, B * P], F16)
        xT_lo = fourth([2, B * P], F16)
        xd = fourth([2, D])
        xdT = fourth([2, 2, P])

        x_all = sb("x_all", [P, B, D])
        stat = sb("stat", [P, B, 2])
        bnst = sb("bnst", [P, 2, 6])
        agg = sb("agg", [P, 2])
        rstd = sb("rstd", [P, B])
        half_pow = sb("half_pow", [P, 2 * B])
        ident = sb("ident", [P, P])
        identb = sb("identb", [P, P], BF16)
        gates = sb("gates", [P, 4])
        tg = sb("tg", [P, 4])
        pair = [ctx.enter_context(nc.psum_tensor(f"pair{n}", [P, 1024], F32)) for n in range(3)]
        last2 = [ctx.enter_context(nc.psum_tensor(f"bank{n}", [P, 512], F32)) for n in range(6, 8)]
        bank = [pair[n // 2][:, (n % 2) * 512:(n % 2) * 512 + 512] for n in range(6)]
        bank += [t[:, :] for t in last2]

        smallA = sb("smallA", [P, 8])
        wA = sb("wA", [P, 6, P])
        rot = sb("rot", [P, 2, D])
        tgbm = sb("tgbm", [P, 1])
        nmax = sb("nmax", [P, 2, 2, 2, 8])
        npart = sb("npart", [P, 2, 2, 2, 8], BF16)
        nmT = sb("nmT", [16, 2, D], BF16)

        wsum = sb("wsum", [P, 2])
        onesf = sb("onesf", [P, P])
        wmean = sb("wmean", [P, 2])
        wscale = sb("wscale", [P, 2])
        tb = sb("tb", [P, 8, B])
        xr = sb("xr", [P, D])
        xi = sb("xi", [P, 2, D], BF16)
        xiT = sb("xiT", [P, 2, 2, P], BF16)
        ssq = sb("ssq", [P, 2])
        dqw = sb("dqw", [P, 1])
        mxc = sb("mxc", [P, 2])
        den = sb("den", [P, B])
        nrm = sb("nrm", [P, 2])
        tq = sb("tq", [P, 2, 8])
        smc = sb("smc", [P, 2, 4])
        wr = sb("wr", [P, 2, NCO])
        wmax = sb("wmax", [P, 2])
        wmaxr = sb("wmaxr", [1, P])
        lg = sb("lg", [P, B, NCO])
        rk = sb("rk", [P, 4, B, E])
        tri = sb("tri", [P, 2, E * E])
        cf = sb("cf", [P, B, NCO])
        cfr = sb("cfr", [P, B, NCO])
        cfp = sb("cfp", [P, B, 3, NCO], BF16)

        s_wB = sem("ffn_weights_loaded")
        s_wC = sem("attention_weights_loaded")
        s_wD = sem("expert_weights_loaded")
        s_b0 = sem("prepared_b")
        s_b1 = sem("prepared_b_scalar")
        s_xi = sem("x_rounded")
        s_xiT = sem("x_rounded_turned")
        s_xiTs = sem("x_rounded_turned_stored")
        s_h = sem("hidden_done")
        s_g1 = sem("gelu1_done")
        s_g2 = sem("gelu2_done")
        s_sq = sem("squares_summed")
        s_nr = sem("norm_done")
        s_tq = sem("hidden_scale_step")
        s_t5 = sem("hidden_scale_inverted")
        s_hi = sem("hidden_rounded")
        s_hT = sem("hidden_turned")
        s_hTs = sem("hidden_turned_stored")
        s_yB = sem("ffn_output_done")
        s_xB = sem("x_updated_b")
        s_bnB = sem("bn_stats_done_b")
        s_stB = sem("stats_ready_b")
        s_c0 = sem("prepared_c")
        s_kv = [sem("ctx_keys_loaded_even"), sem("ctx_keys_loaded_odd")]
        s_xc = sem("xc_ready")
        s_xcT = sem("xc_turned")
        s_xcTs = sem("xc_turned_stored")
        s_qkC = sem("qk_done_c")
        s_qkCs = sem("qk_stored_c")
        s_vC = sem("v_done_c")
        s_vCs = sem("v_stored_c")
        s_sC = sem("scores_done_c")
        s_mC = sem("max_ready_c")
        s_eC = sem("exp_done_c")
        s_rC = sem("sum_inverted_c")
        s_pT = sem("probs_turned")
        s_pTs = sem("probs_turned_stored")
        s_oC = sem("o_done_c")
        s_oCs = sem("o_stored_c")
        s_yC = sem("attention_output_done")
        s_xC = sem("x_updated_c")
        s_bnC = sem("bn_stats_done_c")
        s_stC = sem("stats_ready_c")
        s_d0 = sem("prepared_d")
        s_d1 = sem("prepared_d_scalar")
        s_dP = sem("prepared_d_tensor")
        s_xd = sem("xd_ready")
        s_xdT = sem("xd_turned")
        s_xdTs = sem("xdT_stored")
        s_xr = sem("x_scaled")
        s_vb = sem("vector_step_b")
        s_ur = sem("vector_step_routing")
        s_ws = sem("weights_summed")
        s_c1 = sem("max_found_c")
        s_r0 = sem("sum_inverted_step")
        s_xhi = sem("xT_hi_stored")
        s_xlo = sem("xT_lo_stored")
        s_lg = sem("logits_done")
        s_lgs = sem("logits_stored")
        s_rt = sem("routing_step")
        s_rta = sem("routing_exp_done")
        s_cT = sem("coefficients_turned")
        s_cTs = sem("coefficients_turned_stored")
        s_g = sem("gate_done")
        s_u = sem("up_done")
        s_c = sem("coefficients_spread")
        s_si = sem("silu_done")
        s_t = sem("gate_times_up")
        s_hd = sem("hidden_ready_d")
        s_dn = sem("down_done")
        s_yD = sem("outputs_ready")

        s_x = [sem(f"x_loaded_{g}") for g in range(4)]
        s_cst = sem("constants_loaded")
        s_ctx = [sem("ctx_loaded_even"), sem("ctx_loaded_odd")]
        s_prep = sem("prepared_by_vector")
        s_pool0 = sem("prepared_by_gpsimd")
        s_act0 = sem("prepared_by_scalar")
        s_bm = sem("bias_product_done")
        s_dve = sem("vector_step")
        s_pool = sem("gpsimd_step")
        s_xn = sem("xn_ready")
        s_q = sem("q_done")
        s_qu = sem("q_used")
        s_k = sem("k_done")
        s_ku = sem("k_used")
        s_v = sem("v_done")
        s_vu = sem("v_stored")
        s_qp = sem("q_parts_ready")
        s_kp = sem("k_parts_ready")
        s_stk = [[sem(f"stack_loaded_{u}_{hf}") for hf in range(2)] for u in range(2)]
        s_qw = [sem("q_parts_written_even"), sem("q_parts_written_odd")]
        s_kw = [sem("k_parts_written_even"), sem("k_parts_written_odd")]
        s_ow = sem("o_written")
        s_s = sem("scores_done")
        s_max = sem("max_done")
        s_sp = sem("max_parts_ready")
        s_mt = sem("max_turned")
        s_me = sem("max_rows_stored")
        s_mx = [[sem(f"max_rows_loaded_{u}_{hf}") for hf in range(2)] for u in range(2)]
        s_st = sem("shifted_scores_done")
        s_exp = sem("exp_done")
        s_pv = sem("pv_done")
        s_oe = sem("o_stored")
        s_oc = sem("o_compact")
        s_on = sem("o_normalised")
        s_rd = sem("denominators_inverted")
        s_bn = sem("bn_stats_done_a")
        s_ag = sem("bn_aggregate_done_a")
        s_apart = {e: sem(f"apart_{n}") for n, e in enumerate(
            (mybir.EngineType.SP, mybir.EngineType.Pool, mybir.EngineType.PE,
             mybir.EngineType.DVE))}
        s_wm = sem("merge_done")
        s_xA = sem("x_updated_a")
        s_st_r = sem("stats_ready_a")
        s_out = sem("stored")

        block = ctx.enter_context(nc.Block())

        CONST_DMAS = 6
        PB_RSTD, PB_NORM, PB_DONE = 1, 2, 3
        PD_WMAX, PD_DONE = 5, 6
        RT_DONE = 2
        q_scr = [nc.dram_tensor(f"q_scratch_{u}", (2, NPART * HD, 8 * D), BF16).ap() for u in range(2)]
        k_scr = [nc.dram_tensor(f"k_scratch_{u}", (2, NPART * HD, 8 * D), BF16).ap() for u in range(2)]
        o_scr = nc.dram_tensor("o_scratch", (4, 32, 4 * D), F32).ap()
        psS = pair
        psST = [bank[4], bank[5]]
        psPV = bank[6]
        psM = bank[7]
        psMb = bank[7].bitcast(BF16)
        psXT, psH = bank[7].bitcast(BF16), [pair[0][:, :], pair[1][:, :]]
        psHT = pair[2][:, :]
        psYB = bank[6]
        psTx, psTp, psQK, psV, psO, psSc, psYC = bank[0:7]
        psTd, psLg = bank[4:6], bank[6:8]
        psG, psU, psC, acc = bank[4:6], bank[6:8], bank[0:2], pair[1][:, :]

        class Chain:

            def __init__(self, eng, s):
                self.eng, self.s, self.n, self.base = eng, s, 0, 0

            def __call__(self, ins):
                ins.then_inc(self.s, 1)
                self.n += 1
                return ins

            def wait(self):
                self.eng.wait_ge(self.s, self.base + self.n)

        def apart(eng):
            eng.sem_inc(s_apart[eng.engine], 1)

        @block.sync
        def _(sp):
            for g in range(4):
                sp.dma_start(x_all[:, 4 * g:4 * g + 4, :],
                             a["x"][4 * g:4 * g + 4].rearrange("b s d -> s b d")).then_inc(s_x[g], 16)
            sp.dma_start(wA[:, :, :], a["wA"]).then_inc(s_cst, 16)
            sp.dma_start(rot[:, :, :], a["rot"]).then_inc(s_cst, 16)
            sp.dma_start(smallA[:, :], a["smallA"]).then_inc(s_cst, 16)
            sp.dma_start(ident[:, :], a["ident"]).then_inc(s_cst, 16)
            sp.dma_start(gates[:, 0:2], a["g_xattn"].partition_broadcast(P)).then_inc(s_cst, 16)
            sp.dma_start(gates[:, 2:4], a["g_ffn"].partition_broadcast(P)).then_inc(s_cst, 16)

            sp.dma_start(w1, a["w1"]).then_inc(s_wB, 16)
            sp.dma_start(w2, a["w2"]).then_inc(s_wB, 16)

            def load_ctx(at):
                if at.rep >= 2:
                    sp.wait_ge(s_v, at.count(1, -1))
                    apart(sp)
                sp.dma_start(ctx_in[:, at.odd, :], a["ctx"][bass.ds(at.b, 1)]
                             .rearrange("b s d -> (b s) d")).then_inc(s_ctx[at.odd], 16)

            def write_parts(at, w):
                scr, ready, written = ((q_scr, s_qp, s_qw), (k_scr, s_kp, s_kw))[w]
                sp.wait_ge(ready, at.count(1, 1))
                for hf in range(2):
                    sp.dma_start(scr[at.odd][hf].rearrange("(a d) (h n) -> (d h) a n", a=NPART, n=D),
                                 parts[64 * hf:64 * hf + 64, at.odd, w, :, :])\
                      .then_inc(written[at.odd], 16)

            def load_stack(at, hf):
                if at.rep >= 2:
                    sp.wait_ge(s_st, at.count(16, -32 + 8 * hf + 8))
                    apart(sp)
                sp.wait_ge(s_qw[at.odd], at.half * 32 + 32)
                sp.wait_ge(s_kw[at.odd], at.half * 32 + 32)
                heads = slice(8 * hf, 8 * hf + 8)
                n = NPART * HD
                sp.dma_start(kst[0:STACK, at.odd, heads, :],
                             k_scr[at.odd][hf].unsqueeze(0).to_broadcast([NPART, n, 8 * D]))\
                  .then_inc(s_stk[at.odd][hf], 16)
                for a_ in range(NPART):
                    sp.dma_start(qst[n * a_:n * a_ + n, at.odd, heads, :],
                                 q_scr[at.odd][hf, HD * a_:HD * a_ + HD].unsqueeze(0)
                                 .to_broadcast([NPART, HD, 8 * D])).then_inc(s_stk[at.odd][hf], 16)

            def load_max(at, hf):
                sp.wait_ge(s_me, at.count(2, hf + 1))
                sp.dma_start(qst[MAXROW:MAXROW + 2, at.odd, 8 * hf:8 * hf + 8, :], nmT[:, hf, :])\
                  .then_inc(s_mx[at.odd][hf], 16)

            def write_o(at):
                sp.wait_ge(s_oe, at.count(2, 2))
                apart(sp)
                if at.rep >= 1:
                    sp.wait_ge(s_oc, at.count(32, 0))
                sp.dma_start(o_scr.rearrange("j r n -> (j r) n"), o_sb).then_inc(s_ow, 16)

            def compact(at):
                sp.wait_ge(s_ow, at.count(16, 16))
                apart(sp)
                if at.rep >= 1:
                    sp.wait_ge(s_on, at.count(1, 0))
                for w in range(2):
                    sp.dma_start(oc[:, w, :], o_scr[:, HD * w:HD * w + HD, :]
                                 .rearrange("j d (g n) -> j (d g) n", g=4)).then_inc(s_oc, 16)

            def step(at):
                last, nxt, two, three = at.plus(-1), at.plus(1), at.plus(2), at.plus(3)
                if nxt.real():
                    load_stack(nxt, 1)
                if two.real():
                    write_parts(two, 0)
                if at.real():
                    load_max(at, 1)
                if last.real():
                    write_o(last)
                if two.real():
                    write_parts(two, 1)
                if last.real():
                    compact(last)
                if two.real():
                    load_stack(two, 0)
                if three.real():
                    load_ctx(three)
                if nxt.real():
                    load_max(nxt, 0)

            load_ctx(At(0, 0))
            sp.wait_ge(s_prep, 1)
            sp.wait_ge(s_pool0, 6)
            step(At(-1, 0))
            step(At(-1, 1))
            steps(sp, step, 0, B + 1, 4, 4)

            sp.wait_ge(s_xA, B)
            sp.dma_start(wC[:, :, :, :], a["wC"]).then_inc(s_wC, 16)
            sp.dma_start(wgu[:, :, :], a["wgu"]).then_inc(s_wD, 16)
            sp.dma_start(wd[:, :, :], a["wd"]).then_inc(s_wD, 16)
            sp.dma_start(wr[:, :, :], a["wr"]).then_inc(s_wD, 16)
            sp.dma_start(tri[:, :, :], a["tri"].partition_broadcast(P)).then_inc(s_wD, 16)

            sp.wait_ge(s_xB, B)
            sp.dma_start(self_, a["sel"]).then_inc(s_wD, 16)

            def load_keys(at):
                if at.rep >= 2:
                    sp.wait_ge(s_sC, at.count(1, -1))
                    sp.wait_ge(s_oC, at.count(1, -1))
                sp.dma_start(kTc[:, at.odd, :, 0:P],
                             a["ctxT"][bass.ds(at.b, 1)].rearrange("b (c p) s -> p (b c) s", p=P))\
                  .then_inc(s_kv[at.odd], 16)
                sp.dma_start(vc[:, at.odd, 0, :], a["ctx"][bass.ds(at.b, 1)]
                             .rearrange("b s d -> (b s) d")).then_inc(s_kv[at.odd], 16)

            steps(sp, load_keys, 0, B, 2, 2)

            for g in range(NG):
                sp.wait_ge(s_yD, g + 2)
                sp.dma_start(out[GROUP * g:GROUP * g + GROUP].rearrange("b s d -> s b d"),
                             x_all[:, GROUP * g:GROUP * g + GROUP, :]).then_inc(s_out, 16)
            sp.wait_ge(s_out, 16 * NG)

        @block.gpsimd
        def _(pool):
            ch = Chain(pool, s_pool0)
            ch(nc.gpsimd.memset(half_pow[:, 0:B], -0.5))
            ch(nc.gpsimd.memset(half_pow[:, B:2 * B], 0.5))
            nc.gpsimd.memset(onesf[:, :], 1.0)
            ch(nc.gpsimd.memset(vst[:, :, :, :, 0:8], 0.0))
            ch(nc.gpsimd.memset(vst[:, :, :, :, 8:16], 1.0))
            ch(nc.gpsimd.memset(vst[:, :, :, :, 16:32], 0.0))
            ch(nc.gpsimd.memset(qst[:, :, :, :].bitcast(F32), 0.0))
            ch.wait()
            pool.wait_ge(s_prep, 2)
            ch(nc.gpsimd.tensor_tensor(rstd[:, :], rstd[:, :], half_pow[:, 0:B], ALU.pow))

            def split(at, w, used, ready, written):
                pool.wait_ge(used, at.count(1, 1))
                if at.rep >= 2:
                    pool.wait_ge(written[at.odd], at.half * 32)
                base = at.count(8, 4 * w)
                def done(ins, k):
                    ins.then_inc(s_pool, 1)
                    pool.wait_ge(s_pool, base + k)
                    if k in (1, 3):
                        apart(pool)
                r = res[:, w, :]
                done(nc.gpsimd.tensor_tensor(r, rt[:, w, 0, :], rt[:, w, 1, :], ALU.add), 1)
                done(nc.gpsimd.tensor_copy(parts[:, at.odd, w, 0, :], r), 2)
                done(nc.gpsimd.tensor_tensor(r, r, parts[:, at.odd, w, 0, :], ALU.subtract), 3)
                done(nc.gpsimd.tensor_copy(parts[:, at.odd, w, 1, :], r), 4)
                nc.gpsimd.tensor_tensor(parts[:, at.odd, w, 2, :], r, parts[:, at.odd, w, 1, :],
                                        ALU.subtract).then_inc(ready, 1)

            def divide(at):
                pool.wait_ge(s_rd, at.count(1, 1))
                if at.rep >= 1:
                    pool.wait_ge(s_wm, at.count(1, 0))
                nc.gpsimd.tensor_tensor(on[:, :], oc[:, 0, :], rden, ALU.mult)\
                  .then_inc(s_on, 1)

            def step(at):
                if at.plus(2).real():
                    split(at.plus(2), 1, s_ku, s_kp, s_kw)
                if at.plus(-2).real():
                    divide(at.plus(-2))
                if at.plus(3).real():
                    split(at.plus(3), 0, s_qu, s_qp, s_qw)

            split(At(0, 0), 0, s_qu, s_qp, s_qw)
            step(At(-1, 0))
            step(At(-1, 1))
            steps(pool, step, 0, B + 2, 4, 4)

            pool.wait_ge(s_b0, PB_RSTD)
            nc.gpsimd.tensor_tensor(rstd[:, :], rstd[:, :], half_pow[:, 0:B], ALU.pow)\
              .then_inc(s_pool0, 1)
            pool.wait_ge(s_b0, PB_NORM)
            nc.gpsimd.tensor_tensor(tb[:, 3, :], tb[:, 3, :], half_pow[:, B:2 * B], ALU.pow)\
              .then_inc(s_pool0, 1)

            def norm_b(at):
                pool.wait_ge(s_sq, at.count(1, 1))
                if at.rep >= 2:
                    pool.wait_ge(s_hi, at.count(1, -1))
                nc.gpsimd.tensor_tensor(nrm[:, at.odd:at.odd + 1], ssq[:, at.odd:at.odd + 1],
                                        half_pow[:, B:B + 1], ALU.pow).then_inc(s_nr, 1)

            steps(pool, norm_b, 0, B, 2, 2)
            pool.wait_ge(s_c0, 1)
            nc.gpsimd.tensor_tensor(rstd[:, :], rstd[:, :], half_pow[:, 0:B], ALU.pow)\
              .then_inc(s_pool0, 1)
            pool.wait_ge(s_d0, 1)
            nc.gpsimd.tensor_tensor(rstd[:, :], rstd[:, :], half_pow[:, 0:B], ALU.pow)\
              .then_inc(s_pool0, 1)

        @block.scalar
        def _(act):
            act.wait_ge(s_cst, 16 * CONST_DMAS)
            nc.scalar.activation(tg[:, :], gates[:, :], ACT.Tanh).then_inc(s_act0, 1)

            def exp(at, h):
                act.wait_ge(s_st, at.count(16, h + 1))
                if at.rep > 0 or h >= 8:
                    act.wait_ge(s_pv, at.count(4, h // 4 - 1))
                nc.scalar.activation(pT[:, h % 8, :], psST[h % 2][:, :], ACT.Exp,
                                     scale=float(HD) ** -0.5).then_inc(s_exp, 1)

            def store_o(at, pair):
                act.wait_ge(s_pv, at.count(4, 2 * pair + 2))
                if at.rep >= 1:
                    act.wait_ge(s_ow, at.count(16, 0))
                nc.scalar.activation(o_sb[:, 2 * pair:2 * pair + 2, :],
                                     psPV[:, :].rearrange("p (g n) -> p g n", g=2),
                                     ACT.Copy).then_inc(s_oe, 1)

            def store_max(at, hf):
                act.wait_ge(s_mt, at.count(2, hf + 1))
                if at.rep >= 1:
                    last = at.plus(-1)
                    act.wait_ge(s_mx[last.odd][hf], last.half * 16 + 16)
                nc.scalar.activation(nmT[:, hf, :], psMb[0:16, 0:D], ACT.Copy).then_inc(s_me, 1)

            def store_v(at):
                act.wait_ge(s_v, at.count(1, 1))
                if at.rep == 0:
                    act.wait_ge(s_pool0, 5)
                if at.rep >= 2:
                    act.wait_ge(s_pv, at.count(4, -4))
                for c in range(2):
                    ins = nc.scalar.activation(
                        vst[:, at.odd, c, :, 0:HD],
                        psM[:, c * P:c * P + P].rearrange("p (h d) -> p h d", h=H), ACT.Copy)
                ins.then_inc(s_vu, 1)

            def step(at):
                nxt, last = at.plus(1), at.plus(-1)
                for slot in range(8):
                    if at.real():
                        exp(at, 2 * slot)
                        exp(at, 2 * slot + 1)
                    if slot == 0 and last.real():
                        store_o(last, 1)
                    if slot == 1 and at.real():
                        store_max(at, 1)
                    if slot == 3 and nxt.real():
                        store_v(nxt)
                    if slot == 4 and at.real():
                        store_o(at, 0)
                    if slot == 5 and nxt.real():
                        store_max(nxt, 0)

            step(At(-1, 1))
            steps(act, step, 0, B + 1, 2, 2)

            act.wait_ge(s_xA, B)
            act.wait_ge(s_wB, 32)
            nc.scalar.activation(h2[:, :, :], w1[:, :, :], ACT.Abs, accum_out=wsum[:, 0:1])\
              .then_inc(s_b1, 1)
            act.wait_ge(s_b1, 1)
            nc.scalar.activation(h2[:, :, :].rearrange("p c i -> p (c i)"),
                                 w2[:, :, :].rearrange("p c i -> p (c i)"), ACT.Abs,
                                 accum_out=wsum[:, 1:2]).then_inc(s_b1, 1)
            act.wait_ge(s_b0, PB_DONE)

            def store_xiT(at):
                act.wait_ge(s_xiT, at.count(1, 1))
                if at.rep >= 2:
                    act.wait_ge(s_h, at.count(1, -1))
                nc.scalar.activation(xiT[:, at.odd, :, :],
                                     psXT[:, 0:D].rearrange("p (c s) -> p c s", c=2), ACT.Copy)\
                  .then_inc(s_xiTs, 1)

            def gelu(at):
                act.wait_ge(s_h, at.count(1, 1))
                if at.rep >= 1:
                    act.wait_ge(s_sq, at.count(1, 0))
                nc.scalar.activation(h1[:, :], psH[at.odd], ACT.Gelu,
                                     scale=tb[:, 6, bass.ds(at.b, 1)]).then_inc(s_g1, 1)

            def gelu_again(at):
                act.wait_ge(s_g1, at.count(1, 1))
                if at.rep >= 2:
                    act.wait_ge(s_hi, at.count(1, -1))
                elif at.rep == 0:
                    act.wait_ge(s_b1, 2)
                nc.scalar.activation(h2[:, at.odd, :], h1[:, :], ACT.Gelu).then_inc(s_g2, 1)

            def squares(at):
                act.wait_ge(s_g2, at.count(1, 1))
                nc.scalar.activation(h1[:, :], h2[:, at.odd, :], ACT.Square,
                                     accum_out=ssq[:, at.odd:at.odd + 1]).then_inc(s_sq, 1)

            def store_hT(at):
                act.wait_ge(s_hT, at.count(1, 1))
                if at.rep >= 2:
                    act.wait_ge(s_yB, at.count(1, -1))
                nc.scalar.activation(hT[:, at.odd, :, :], psHT.rearrange("p (c s) -> p c s", c=8),
                                     ACT.Copy, bias=-ROUND).then_inc(s_hTs, 1)

            def act_b(at):
                last, nxt, two = at.plus(-1), at.plus(1), at.plus(2)
                if two.real():
                    store_xiT(two)
                if nxt.real():
                    gelu(nxt)
                if last.real():
                    store_hT(last)
                if nxt.real():
                    gelu_again(nxt)
                    squares(nxt)

            act_b(At(-1, 0))
            act_b(At(-1, 1))
            steps(act, act_b, 0, B + 1, 4, 4)

            act.wait_ge(s_xB, B)

            def act_c(at):
                nxt, two = at.plus(1), at.plus(2)
                if nxt.real():
                    act.wait_ge(s_vC, nxt.count(1, 1))
                    if nxt.rep >= 2:
                        act.wait_ge(s_oC, nxt.count(1, -1))
                    nc.scalar.activation(vc[:, nxt.odd, 1, :], psV[:, 0:D], ACT.Copy)\
                      .then_inc(s_vCs, 1)
                if at.real():
                    act.wait_ge(s_pT, at.count(1, 1))
                    if at.rep >= 1:
                        act.wait_ge(s_oC, at.count(1, 0))
                    nc.scalar.activation(pcT[:, :, :],
                                         psTp[:, 0:D].rearrange("p (c s) -> p c s", c=2),
                                         ACT.Copy).then_inc(s_pTs, 1)
                if two.real():
                    act.wait_ge(s_xcT, two.count(1, 1))
                    if two.rep >= 2:
                        act.wait_ge(s_vC, two.count(1, -1))
                    nc.scalar.activation(xcT[:, two.odd, :, :],
                                         psTx[:, 0:D].rearrange("p (c s) -> p c s", c=2),
                                         ACT.Copy).then_inc(s_xcTs, 1)
                if at.real():
                    act.wait_ge(s_oC, at.count(1, 1))
                    if at.rep >= 1:
                        act.wait_ge(s_yC, at.count(1, 0))
                    nc.scalar.activation(oTc[:, :, :],
                                         psO[:, 0:D].rearrange("p (c s) -> p c s", c=2),
                                         ACT.Copy).then_inc(s_oCs, 1)
                if nxt.real():
                    act.wait_ge(s_mC, nxt.count(1, 1))
                    if nxt.rep >= 2:
                        act.wait_ge(s_pT, nxt.count(1, -1))
                    nc.scalar.activation(pc[:, nxt.odd, :], psSc[:, 0:D], ACT.Exp,
                                         bias=smc[:, nxt.odd, 0:1], scale=float(D) ** -0.5,
                                         accum_out=smc[:, nxt.odd, 1:2]).then_inc(s_eC, 1)

            act_c(At(-1, 0))
            act_c(At(-1, 1))
            steps(act, act_c, 0, B, 2, 2)

            act.wait_ge(s_xC, B)
            act.wait_ge(s_d0, PD_WMAX)
            nc.scalar.activation(wgu_hi[:, :, :], wgu[:, :, :], ACT.Copy, scale=wmax[:, 1:2])\
              .then_inc(s_d1, 1)

            def act_route(at):
                act.wait_ge(s_xdT, at.count(1, 1))
                for c in range(2):
                    ins = nc.scalar.activation(xT_hi[:, c, bass.ds(at.b * P, P)],
                                               psTd[at.odd][:, c * P:c * P + P], ACT.Copy)
                ins.then_inc(s_xhi, 1)
                if at.rep >= 2:
                    act.wait_ge(s_xlo, at.count(1, -1))
                    act.wait_ge(s_lg, at.count(1, -1))
                nc.scalar.activation(xdT[:, at.odd, :, :],
                                     psTd[at.odd][:, 0:D].rearrange("p (c s) -> p c s", c=2),
                                     ACT.Copy).then_inc(s_xdTs, 1)
                act.wait_ge(s_lg, at.count(1, 1))
                nc.scalar.activation(lg[:, bass.ds(at.b, 1), :].rearrange("p b e -> p (b e)"),
                                     psLg[at.odd][:, 0:NCO], ACT.Copy).then_inc(s_lgs, 1)

            steps(act, act_route, 0, B, 2, 2)
            act.wait_ge(s_rt, 1)
            nc.scalar.activation(rk[:, 0, :, :], rk[:, 0, :, :], ACT.Exp).then_inc(s_rta, 1)
            nc.scalar.activation(cf[:, :, E], lg[:, :, E], ACT.Exp, scale=-1.0).then_inc(s_rta, 1)
            for g in range(NG):
                act.wait_ge(s_cT, g + 1)
                nc.scalar.activation(cT[:, g * 512:g * 512 + 512],
                                     bank[g].bitcast(BF16)[0:3 * NCO, 0:512], ACT.Copy)\
                  .then_inc(s_cTs, 1)
            act.sem_inc(s_si, 1)
            with act.Fori(0, NG) as g:
                for c in range(NCH):
                    rows = min(P, HID - c * P)
                    act.wait_ge(s_g, g * NCH + (c + 1))
                    act.wait_ge(s_t, g * NCH + max(c, 1))
                    nc.scalar.activation(gs[0:rows, c % 2, :], psG[c % 2][0:rows, :], ACT.Silu,
                                         scale=wmax[0:rows, 0:1]).then_inc(s_si, 1)

        @block.tensor
        def _(pe):
            pe.wait_ge(s_cst, 16 * CONST_DMAS)
            pe.wait_ge(s_prep, 3)
            nc.tensor.matmul(psM[:, 0:1], wA[:, 5, :], smallA[:, 6:7], start=True, stop=True)\
              .then_inc(s_bm, 1)
            pe.wait_ge(s_prep, 4)

            def project_q(at):
                pe.wait_ge(s_xn, at.count(1, 1))
                for w in range(2):
                    ins = nc.tensor.matmul(psM[:, w * D:w * D + D], wA[:, w, :], xn[:, at.odd, :],
                                           start=True, stop=True)
                ins.then_inc(s_q, 1)

            def project_k(at):
                pe.wait_ge(s_ctx[at.odd], at.half * 16 + 16)
                for w in range(2):
                    ins = nc.tensor.matmul(psM[:, w * D:w * D + D], wA[:, 2 + w, :],
                                           ctx_in[:, at.odd, :], start=True, stop=True)
                ins.then_inc(s_k, 1)

            def project_v(at):
                for c in range(2):
                    ins = nc.tensor.matmul(psM[:, c * P:c * P + P],
                                           ctx_in[:, at.odd, c * P:c * P + P], wA[:, 4, :],
                                           start=True, stop=True)
                ins.then_inc(s_v, 1)

            def scores(at, n):
                hf, c, hg = n // 4, (n // 2) % 2, n % 2
                if n in (0, 4):
                    pe.wait_ge(s_stk[at.odd][hf], at.half * 64 + 64)
                if at.rep > 0 or n >= 2:
                    pe.wait_ge(s_max, at.count(8, n - 1))
                for i in range(4):
                    h = 8 * hf + 4 * hg + i
                    ins = nc.tensor.matmul(psS[n % 2][:, i * D:i * D + D],
                                           qst[0:MAXROW, at.odd, h, c * P:c * P + P],
                                           kst[0:MAXROW, at.odd, h, :], start=True, stop=True)
                ins.then_inc(s_s, 1)

            def turn_max(at, hf):
                pe.wait_ge(s_sp, at.count(2, hf + 1))
                for c in range(2):
                    ins = nc.tensor.transpose(psMb[0:16, c * P:c * P + P],
                                              npart[:, hf, c, :, :].rearrange("p a h -> p (a h)"),
                                              identb[:, :])
                ins.then_inc(s_mt, 1)

            def shifted(at, h):
                if h in (0, 8):
                    pe.wait_ge(s_mx[at.odd][h // 8], at.half * 16 + 16)
                if at.rep > 0 or h >= 2:
                    pe.wait_ge(s_exp, at.count(16, h - 1))
                for c in range(2):
                    ins = nc.tensor.matmul(psST[h % 2][:, c * D:c * D + D],
                                           kst[0:MAXROW + 2, at.odd, h, c * P:c * P + P],
                                           qst[0:MAXROW + 2, at.odd, h, :], start=True, stop=True)
                ins.then_inc(s_st, 1)

            def values(at, g):
                pe.wait_ge(s_exp, at.count(16, 4 * g + 4))
                if g == 0:
                    pe.wait_ge(s_vu, at.count(1, 1))
                if g == 0 and at.rep > 0:
                    pe.wait_ge(s_oe, at.count(2, 0))
                if g == 2:
                    pe.wait_ge(s_oe, at.count(2, 1))
                for c in range(2):
                    for j in range(4):
                        h = 4 * g + j
                        ins = nc.tensor.matmul(
                            psPV[32 * j:32 * j + 32, (g % 2) * D:(g % 2) * D + D],
                            vst[:, at.odd, c, h, :], pT[:, h % 8, c * D:c * D + D],
                            start=(c == 0), stop=(c == 1))
                ins.then_inc(s_pv, 1)

            def merge(at):
                pe.wait_ge(s_on, at.count(1, 1))
                nc.tensor.matmul(psM[:, 0:D], wA[:, 5, :], on[:, :], start=True, stop=True)\
                  .then_inc(s_wm, 1)

            def step(at):
                last, nxt, two, three = at.plus(-1), at.plus(1), at.plus(2), at.plus(3)
                old = at.plus(-2)
                for slot in range(8):
                    if at.real():
                        shifted(at, 2 * slot)
                        shifted(at, 2 * slot + 1)
                    if nxt.real():
                        scores(nxt, slot)
                    if slot == 0:
                        if two.real():
                            pe.wait_ge(s_qu, two.count(1, 1))
                            project_k(two)
                        if last.real():
                            values(last, 3)
                    if slot == 1 and at.real():
                        if two.real():
                            pe.wait_ge(s_ku, two.count(1, 1))
                        else:
                            pe.wait_ge(s_me, at.count(2, 1))
                        turn_max(at, 1)
                    if slot == 2 and at.real():
                        values(at, 0)
                    if slot == 3 and nxt.real():
                        if at.real():
                            pe.wait_ge(s_me, at.count(2, 2))
                        else:
                            pe.wait_ge(s_ku, two.count(1, 1))
                        project_v(nxt)
                    if slot == 4:
                        if old.real():
                            if nxt.real():
                                pe.wait_ge(s_vu, nxt.count(1, 1))
                            elif at.real():
                                pe.wait_ge(s_me, at.count(2, 2))
                            else:
                                pe.wait_ge(s_xA, at.count(1, -2))
                            merge(old)
                        if at.real():
                            values(at, 1)
                    if slot == 5 and nxt.real():
                        if old.real():
                            pe.wait_ge(s_xA, old.count(1, 1))
                        else:
                            pe.wait_ge(s_vu, nxt.count(1, 1))
                        turn_max(nxt, 0)
                    if slot == 6:
                        if three.real():
                            pe.wait_ge(s_me, nxt.count(2, 1))
                            project_q(three)
                        if at.real():
                            values(at, 2)

            project_q(At(0, 0))
            pe.wait_ge(s_qu, 1)
            project_k(At(0, 0))
            pe.wait_ge(s_ku, 1)
            project_q(At(0, 1))
            step(At(-1, 1))
            steps(pe, step, 0, B + 2, 4, 4)

            pe.wait_ge(s_xA, B)
            pe.wait_ge(s_b1, 2)
            nc.tensor.matmul(psYB[:, 0:2], onesf[:, :], wsum[:, :], start=True, stop=True)\
              .then_inc(s_ws, 1)
            pe.wait_ge(s_b0, PB_DONE)

            def turn_x(at):
                pe.wait_ge(s_xi, at.count(1, 1))
                if at.rep >= 1:
                    pe.wait_ge(s_xiTs, at.count(1, 0))
                for c in range(2):
                    ins = nc.tensor.transpose(psXT[:, c * P:c * P + P],
                                              xi[:, at.odd, c * P:c * P + P], identb[:, :])
                ins.then_inc(s_xiT, 1)

            def hidden(at):
                pe.wait_ge(s_xiTs, at.count(1, 1))
                if at.rep >= 2:
                    pe.wait_ge(s_g1, at.count(1, -1))
                for n in range(2):
                    for c in range(2):
                        ins = nc.tensor.matmul(psH[at.odd][:, n * 512:n * 512 + 512],
                                               xiT[:, at.odd, c, :],
                                               w1q[:, c, n * 512:n * 512 + 512],
                                               start=(c == 0), stop=(c == 1))
                ins.then_inc(s_h, 1)

            def turn_h(at):
                pe.wait_ge(s_hi, at.count(1, 1))
                if at.rep >= 1:
                    pe.wait_ge(s_hTs, at.count(1, 0))
                for c in range(8):
                    ins = nc.tensor.transpose(psHT[:, c * P:c * P + P],
                                              hr[:, at.odd, c * P:c * P + P], ident[:, :])
                ins.then_inc(s_hT, 1)

            def output(at):
                pe.wait_ge(s_hTs, at.count(1, 1))
                if at.rep >= 1:
                    pe.wait_ge(s_xB, at.count(1, 0))
                for c in range(8):
                    ins = nc.tensor.matmul(psYB[:, 0:D], hT[:, at.odd, c, :], w2q[:, c, :],
                                           start=(c == 0), stop=(c == 7))
                ins.then_inc(s_yB, 1)

            def step_b(at):
                last, old, two = at.plus(-1), at.plus(-2), at.plus(2)
                if two.real():
                    turn_x(two)
                if old.real():
                    output(old)
                if last.real():
                    turn_h(last)
                if two.real():
                    hidden(two)

            step_b(At(-1, 0))
            step_b(At(-1, 1))
            steps(pe, step_b, 0, B + 2, 4, 4)

            pe.wait_ge(s_xB, B)
            pe.wait_ge(s_wC, 16)

            def step_c(at):
                last, nxt, two = at.plus(-1), at.plus(1), at.plus(2)
                if nxt.real():
                    pe.wait_ge(s_xcTs, nxt.count(1, 1))
                    if nxt.rep >= 1:
                        pe.wait_ge(s_qkCs, nxt.count(1, 0))
                    for w in range(2):
                        for e in range(2):
                            for c in range(2):
                                ins = nc.tensor.matmul(
                                    psQK[:, w * D + e * P:w * D + e * P + P],
                                    wC[:, w, c, e * P:e * P + P], xcT[:, nxt.odd, c, :],
                                    start=(c == 0), stop=(c == 1))
                    ins.then_inc(s_qkC, 1)
                if last.real():
                    pe.wait_ge(s_oCs, last.count(1, 1))
                    if last.rep >= 1:
                        pe.wait_ge(s_xC, last.count(1, 0))
                    for e in range(2):
                        ins = nc.tensor.matmul(psYC[:, 0:D], oTc[:, e, :], wC[:, 3, e, :],
                                               start=(e == 0), stop=(e == 1))
                    ins.then_inc(s_yC, 1)
                if nxt.real():
                    if nxt.rep >= 1:
                        pe.wait_ge(s_vCs, nxt.count(1, 0))
                    for c in range(2):
                        ins = nc.tensor.matmul(psV[:, 0:D], xcT[:, nxt.odd, c, :], wC[:, 2, c, :],
                                               start=(c == 0), stop=(c == 1))
                    ins.then_inc(s_vC, 1)
                if at.real():
                    pe.wait_ge(s_eC, at.count(1, 1))
                    if at.rep >= 1:
                        pe.wait_ge(s_pTs, at.count(1, 0))
                    for c in range(2):
                        ins = nc.tensor.transpose(psTp[:, c * P:c * P + P],
                                                  pc[:, at.odd, c * P:c * P + P], ident[:, :])
                    ins.then_inc(s_pT, 1)
                if two.real():
                    pe.wait_ge(s_xc, two.count(1, 1))
                    if two.rep >= 1:
                        pe.wait_ge(s_xcTs, two.count(1, 0))
                    for c in range(2):
                        ins = nc.tensor.transpose(psTx[:, c * P:c * P + P],
                                                  xc[:, two.odd, c * P:c * P + P], ident[:, :])
                    ins.then_inc(s_xcT, 1)
                if nxt.real():
                    pe.wait_ge(s_qkCs, nxt.count(1, 1))
                    pe.wait_ge(s_kv[nxt.odd], nxt.half * 32 + 32)
                    if nxt.rep >= 1:
                        pe.wait_ge(s_eC, nxt.count(1, 0))
                    for e in range(2):
                        ins = nc.tensor.matmul(psSc[:, 0:D], qTc[:, nxt.odd, e, :],
                                               kTc[:, nxt.odd, e, :], start=(e == 0), stop=(e == 1))
                    ins.then_inc(s_sC, 1)
                if at.real():
                    pe.wait_ge(s_pTs, at.count(1, 1))
                    if at.rep >= 1:
                        pe.wait_ge(s_oCs, at.count(1, 0))
                    for e in range(2):
                        for c in range(2):
                            ins = nc.tensor.matmul(psO[:, e * P:e * P + P],
                                                   vc[:, at.odd, c, e * P:e * P + P],
                                                   pcT[:, c, :], start=(c == 0), stop=(c == 1))
                    ins.then_inc(s_oC, 1)

            step_c(At(-1, 0))
            step_c(At(-1, 1))
            steps(pe, step_c, 0, B + 1, 4, 2)

            pe.wait_ge(s_xC, B)
            pe.wait_ge(s_d0, 2)
            nc.tensor.transpose(bank[0][0:1, 0:P], wmax[:, 0:1], ident[:, :]).then_inc(s_dP, 1)
            pe.wait_ge(s_d0, 3)
            nc.tensor.matmul(bank[0][:, 256:257], onesf[0:1, :], wmaxr[0:1, 0:1],
                             start=True, stop=True).then_inc(s_dP, 1)

            def turn_x(at):
                pe.wait_ge(s_xd, at.count(1, 1))
                if at.rep >= 2:
                    pe.wait_ge(s_xdTs, at.count(1, -1))
                for c in range(2):
                    ins = nc.tensor.transpose(psTd[at.odd][:, c * P:c * P + P],
                                              xd[:, at.odd, c * P:c * P + P], ident[:, :])
                ins.then_inc(s_xdT, 1)

            def logits(at):
                pe.wait_ge(s_xdTs, at.count(1, 1))
                if at.rep >= 2:
                    pe.wait_ge(s_lgs, at.count(1, -1))
                for c in range(2):
                    ins = nc.tensor.matmul(psLg[at.odd][:, 0:NCO], xdT[:, at.odd, c, :],
                                           wr[:, c, :], start=(c == 0), stop=(c == 1))
                ins.then_inc(s_lg, 1)

            def pe_route(at):
                turn_x(at)
                logits(at)

            pe.wait_ge(s_wD, 16 * 5)
            steps(pe, pe_route, 0, B, 2, 2)
            pe.wait_ge(s_rt, RT_DONE)
            for b in range(B):
                ins = nc.tensor.transpose(
                    bank[b // 4].bitcast(BF16)[0:3 * NCO, (b % 4) * P:(b % 4) * P + P],
                    cfp[:, b, :, :].rearrange("p a e -> p (a e)"), identb[:, :])
                if b % 4 == 3:
                    ins.then_inc(s_cT, 1)
            pe.wait_ge(s_cTs, NG)
            pe.wait_ge(s_d0, PD_DONE)
            pe.sem_inc(s_dn, 1)
            with pe.Fori(0, NG) as g:
                def down(c):
                    rows = min(P, HID - c * P)
                    pe.wait_ge(s_hd, g * NCH + (c + 2))
                    if c == 0:
                        pe.wait_ge(s_yD, g + 1)
                    for n in range(GROUP):
                        ins = nc.tensor.matmul(acc[:, n * D:n * D + D],
                                               hd[0:rows, c % 3, n * P:n * P + P],
                                               wd[0:rows, c, :], start=(c == 0 and n % 2 == 0),
                                               stop=(c == NCH - 1), skip_group_check=True)
                    ins.then_inc(s_dn, 1)

                for c in range(NCH):
                    rows = min(P, HID - c * P)
                    for ps, first_col, free, done in ((psG, 0, s_si, s_g), (psU, HID, s_t, s_u)):
                        pe.wait_ge(free, g * NCH + max(c, 1))
                        if rows < P:
                            apart(pe)
                        k = 0
                        for d in range(2):
                            cols = slice(first_col + c * P, first_col + c * P + rows)
                            for w, x in ((wgu_hi, xT_hi), (wgu_hi, xT_lo), (wgu_lo, xT_hi)):
                                ins = nc.tensor.matmul(ps[c % 2][0:rows, :], w[:, d, cols],
                                                       x[:, d, bass.ds(g * 512, 512)],
                                                       start=(k == 0), stop=(k == 5))
                                k += 1
                        ins.then_inc(done, 1)
                    pe.wait_ge(s_hd, g * NCH + max(c, 1))
                    apart(pe)
                    nc.tensor.matmul(psC[c % 2], sel[:, c * P:c * P + P],
                                     cT[:, bass.ds(g * 512, 512)], start=True, stop=True)\
                      .then_inc(s_c, 1)
                    if c >= 1:
                        down(c - 1)
                down(NCH - 1)

        @block.vector
        def _(dve):
            nc.vector.memset(kst[:, :, :, :].bitcast(F32), 0.0).then_inc(s_dve, 1)
            dve.wait_ge(s_dve, 1)
            nc.vector.memset(kst[MAXROW:MAXROW + 2, :, :, :], 1.0).then_inc(s_prep, 1)
            for b in range(B):
                if b % 4 == 0:
                    dve.wait_ge(s_x[b // 4], 16)
                nc.vector.bn_stats(bnst[:, b % 2, :], x_all[:, b, :]).then_inc(s_dve, 1)
                dve.wait_ge(s_dve, 2 + 2 * b)
                nc.vector.bn_aggr(stat[:, b, :], bnst[:, b % 2, :]).then_inc(s_dve, 1)
            n = 1 + 2 * B
            dve.wait_ge(s_dve, n)
            nc.vector.tensor_scalar(rstd[:, :], stat[:, :, 1], EPS, None, ALU.add)\
              .then_inc(s_prep, 1)
            dve.wait_ge(s_cst, 16 * CONST_DMAS)
            dve.wait_ge(s_act0, 1)
            nc.vector.tensor_scalar(rot[:, 1, :], rot[:, 1, :], smallA[:, 4:5], None, ALU.mult)
            nc.vector.tensor_copy(identb[:, :], ident[:, :])
            nc.vector.tensor_scalar(wA[:, 5, :], wA[:, 5, :], tg[:, 0:1], None, ALU.mult)\
              .then_inc(s_prep, 1)
            dve.wait_ge(s_bm, 1)
            nc.vector.scalar_tensor_tensor(tgbm[:, :], smallA[:, 5:6], tg[:, 0:1], psM[:, 0:1],
                                           ALU.mult, ALU.add).then_inc(s_prep, 1)
            dve.wait_ge(s_prep, 4)
            dve.wait_ge(s_pool0, 7)

            def normalise(at):
                if at.rep >= 2:
                    dve.wait_ge(s_q, at.count(1, -1))
                nc.vector.tensor_scalar(xn[:, at.odd, :], x_all[:, bass.ds(at.b, 1), :].rearrange("p b d -> p (b d)"),
                                        stat[:, bass.ds(at.b, 1), 0], rstd[:, bass.ds(at.b, 1)],
                                        ALU.subtract, ALU.mult).then_inc(s_xn, 1)

            def rotate(at, w, made, used, ready):
                dve.wait_ge(made, at.count(1, 1))
                if at.rep >= 1:
                    dve.wait_ge(ready, at.count(1, 0))
                for i in range(2):
                    ins = nc.vector.scalar_tensor_tensor(
                        rt[:, w, i, :], psM[:, i * D:i * D + D],
                        smallA[:, 2 * w + i:2 * w + i + 1], rot[:, i, :], ALU.add, ALU.mult)
                ins.then_inc(used, 1)

            def maximum(at, n):
                hf, c, hg = n // 4, (n // 2) % 2, n % 2
                dve.wait_ge(s_s, at.count(8, n + 1))
                if n == 0 and at.rep >= 2:
                    dve.wait_ge(s_sp, at.count(2, -2))
                nc.vector.tensor_reduce(
                    nmax[:, at.odd, hf, c, 4 * hg:4 * hg + 4],
                    psS[n % 2][:, :].rearrange("p (h m) -> p h m", h=4), AX.X, ALU.max,
                    negate=True).then_inc(s_max, 1)

            def split_max(at, hf):
                dve.wait_ge(s_max, at.count(8, 4 * hf + 4))
                if at.rep >= 1:
                    dve.wait_ge(s_mt, at.count(2, hf - 1))
                m = nmax[:, at.odd, hf, :, :]
                nc.vector.tensor_copy(npart[:, hf, :, 0, :], m).then_inc(s_dve, 1)
                dve.wait_ge(s_dve, at.count(2, hf) + n + 1)
                nc.vector.tensor_tensor(npart[:, hf, :, 1, :], m, npart[:, hf, :, 0, :],
                                        ALU.subtract).then_inc(s_sp, 1)

            def invert(at):
                dve.wait_ge(s_oc, at.count(32, 32))
                if at.rep >= 1:
                    dve.wait_ge(s_on, at.count(1, 0))
                nc.vector.reciprocal(rden, oc[:, 1, :]).then_inc(s_rd, 1)

            def update(at):
                dve.wait_ge(s_wm, at.count(1, 1))
                xb = x_all[:, bass.ds(at.b, 1), :].rearrange("p b d -> p (b d)")
                nc.vector.scalar_tensor_tensor(xb, psM[:, 0:D], tgbm[:, 0:1], xb,
                                               ALU.add, ALU.add).then_inc(s_xA, 1)

            def statistics(at):
                dve.wait_ge(s_xA, at.count(1, 1))
                if at.rep >= 1:
                    dve.wait_ge(s_st_r, at.count(1, 0))
                apart(dve)
                nc.vector.bn_stats(bnst[:, 0, :],
                                   x_all[:, bass.ds(at.b, 1), :].rearrange("p b d -> p (b d)"))\
                  .then_inc(s_bn, 1)
                dve.wait_ge(s_bn, at.count(1, 1))
                apart(dve)
                nc.vector.bn_aggr(agg[:, :], bnst[:, 0, :]).then_inc(s_ag, 1)
                dve.wait_ge(s_ag, at.count(1, 1))
                nc.vector.tensor_scalar(stat[:, bass.ds(at.b, 1), :].rearrange("p b d -> p (b d)"),
                                        agg[:, :], 0.0, None, ALU.add).then_inc(s_st_r, 1)

            def step(at):
                old, nxt, two, three = at.plus(-2), at.plus(1), at.plus(2), at.plus(3)
                for slot in range(8):
                    if slot == 0 and at.real():
                        split_max(at, 1)
                    if nxt.real():
                        maximum(nxt, slot)
                    if slot == 0 and two.real():
                        rotate(two, 1, s_k, s_ku, s_kp)
                    if slot == 1 and old.real():
                        invert(old)
                    if slot == 4:
                        if nxt.real():
                            split_max(nxt, 0)
                        if old.real():
                            update(old)
                    if slot == 5:
                        if three.real():
                            normalise(three)
                        if old.real():
                            statistics(old)
                    if slot == 6 and three.real():
                        rotate(three, 0, s_q, s_qu, s_qp)

            normalise(At(0, 0))
            normalise(At(0, 1))
            rotate(At(0, 0), 0, s_q, s_qu, s_qp)
            rotate(At(0, 0), 1, s_k, s_ku, s_kp)
            rotate(At(0, 1), 0, s_q, s_qu, s_qp)
            step(At(-1, 1))
            steps(dve, step, 0, B + 2, 4, 4)

            v = Chain(dve, s_vb)
            tt, ts = nc.vector.tensor_tensor, nc.vector.tensor_scalar
            dve.wait_ge(s_st_r, B)
            mean, var = stat[:, :, 0], stat[:, :, 1]
            ts(rstd[:, :], var, EPS, None, ALU.add).then_inc(s_b0, 1)
            v(nc.vector.tensor_reduce(tb[:, 0, :], x_all[:, :, :], AX.X, ALU.max))
            v(nc.vector.tensor_reduce(tb[:, 1, :], x_all[:, :, :], AX.X, ALU.min))
            v.wait()
            v(tt(tb[:, 0, :], tb[:, 0, :], mean, ALU.subtract))
            v(tt(tb[:, 1, :], mean, tb[:, 1, :], ALU.subtract))
            v.wait()
            dve.wait_ge(s_pool0, 8)
            v(tt(tb[:, 0, :], tb[:, 0, :], tb[:, 1, :], ALU.max))
            v(tt(tb[:, 3, :], var, rstd[:, :], ALU.mult))
            v.wait()
            v(tt(tb[:, 2, :], tb[:, 0, :], rstd[:, :], ALU.mult))
            v(tt(tb[:, 4, :], tb[:, 3, :], rstd[:, :], ALU.mult))
            v.wait()
            ts(tb[:, 3, :], tb[:, 4, :], float(D), None, ALU.mult).then_inc(s_b0, 1)
            dve.wait_ge(s_pool0, 9)
            v(ts(tb[:, 3, :], tb[:, 3, :], 1e-12, None, ALU.max))
            v.wait()
            v(nc.vector.reciprocal(tb[:, 4, :], tb[:, 3, :]))
            v.wait()
            v(tt(tb[:, 5, :], tb[:, 2, :], tb[:, 4, :], ALU.mult))
            v(tt(tb[:, 0, :], tb[:, 4, :], rstd[:, :], ALU.mult))
            v.wait()
            v(ts(tb[:, 5, :], tb[:, 5, :], float(D) ** 0.5, EPS, ALU.mult, ALU.max))
            v.wait()
            v(nc.vector.reciprocal(tb[:, 7, :], tb[:, 5, :]))
            v.wait()
            v(tt(tb[:, 7, :], tb[:, 7, :], tb[:, 0, :], ALU.mult))
            v.wait()
            v(ts(tb[:, 7, :], tb[:, 7, :], 127.0 * float(D) ** 0.5, None, ALU.mult))
            dve.wait_ge(s_ws, 1)
            v(ts(wmean[:, :], psYB[:, 0:2], 1.0 / (INNER * D), EPS, ALU.mult, ALU.max))
            v.wait()
            v(nc.vector.reciprocal(wscale[:, :], wmean[:, :]))
            v(ts(tb[:, 6, :], tb[:, 5, :], wmean[:, 0:1], 1.0 / 127.0, ALU.mult, ALU.mult))
            v(ts(dqw[:, :], wmean[:, 1:2], tg[:, 2:3], 1.0 / 127.0, ALU.mult, ALU.mult))
            v.wait()
            dve.wait_ge(s_wB, 32)
            for n, (w, wq) in enumerate(((w1, w1q), (w2, w2q))):
                w, wq = (t.rearrange("p c i -> p (c i)") for t in (w, wq))
                v(ts(w, w, wscale[:, n:n + 1], ROUND, ALU.mult, ALU.add))
                v.wait()
                v(ts(w, w, ROUND, 1.0, ALU.subtract, ALU.min))
                v.wait()
                v(ts(wq, w, -1.0, None, ALU.max))
            v.wait()
            ts(tb[:, 1, :], tb[:, 0, :], 1.0, None, ALU.mult).then_inc(s_b0, 1)

            def xb(at):
                return x_all[:, bass.ds(at.b, 1), :].rearrange("p b d -> p (b d)")

            def scale_x(at):
                if at.rep >= 1:
                    dve.wait_ge(s_xi, at.count(1, 0))
                ts(xr[:, :], xb(at), stat[:, bass.ds(at.b, 1), 0], tb[:, 7, bass.ds(at.b, 1)],
                   ALU.subtract, ALU.mult).then_inc(s_xr, 1)

            def round_x(at):
                dve.wait_ge(s_xr, at.count(1, 1))
                if at.rep >= 2:
                    dve.wait_ge(s_xiT, at.count(1, -1))
                ts(xi[:, at.odd, :], xr[:, :], ROUND, ROUND, ALU.add, ALU.subtract)\
                    .then_inc(s_xi, 1)

            def update_b(at):
                dve.wait_ge(s_yB, at.count(1, 1))
                nc.vector.scalar_tensor_tensor(xb(at), psYB[:, 0:D], tq[:, at.odd, 7:8], xb(at),
                                               ALU.mult, ALU.add).then_inc(s_xB, 1)

            def stats_1(at, updated, bn, ready):
                dve.wait_ge(updated, at.count(1, 1))
                if at.rep >= 1:
                    dve.wait_ge(ready, at.count(1, 0))
                apart(dve)
                nc.vector.bn_stats(bnst[:, 0, :], xb(at)).then_inc(bn, 1)

            def stats_2(at, bn):
                dve.wait_ge(bn, at.count(2, 1))
                apart(dve)
                nc.vector.bn_aggr(agg[:, :], bnst[:, 0, :]).then_inc(bn, 1)

            def stats_3(at, bn, ready):
                dve.wait_ge(bn, at.count(2, 2))
                ts(stat[:, bass.ds(at.b, 1), :].rearrange("p b d -> p (b d)"), agg[:, :], 0.0,
                   None, ALU.add).then_inc(ready, 1)

            def step_b(at):
                old, three = at.plus(-2), at.plus(3)
                q = tq[:, at.odd, :]
                col = lambda n: q[:, n:n + 1]
                here = at.real()

                def scale(k, make):
                    if here:
                        if k > 1:
                            dve.wait_ge(s_tq, at.count(6, k - 1))
                        make().then_inc(s_tq, 1)

                if here:
                    dve.wait_ge(s_g2, at.count(1, 1))
                scale(1, lambda: nc.vector.tensor_reduce(col(0), h2[:, at.odd, :], AX.X, ALU.max,
                                                         apply_absolute_value=True))
                if old.real():
                    update_b(old)
                if here:
                    dve.wait_ge(s_nr, at.count(1, 1))
                scale(2, lambda: ts(col(1), nrm[:, at.odd:at.odd + 1], 1e-12, None, ALU.max))
                if three.real():
                    scale_x(three)
                scale(3, lambda: nc.vector.reciprocal(col(2), col(1)))
                if old.real():
                    stats_1(old, s_xB, s_bnB, s_stB)
                scale(4, lambda: ts(col(3), col(0), col(2), float(INNER) ** 0.5, ALU.mult,
                                    ALU.mult))
                if three.real():
                    round_x(three)
                if here:
                    dve.wait_ge(s_tq, at.count(6, 4))
                    if at.rep >= 2:
                        dve.wait_ge(s_xB, at.count(1, -1))
                    ts(col(7), col(3), EPS, dqw[:, 0:1], ALU.max, ALU.mult)
                scale(5, lambda: ts(col(4), col(3), EPS, None, ALU.max))
                if old.real():
                    stats_2(old, s_bnB)
                if here:
                    dve.wait_ge(s_tq, at.count(6, 5))
                    nc.vector.reciprocal(col(5), col(4)).then_inc(s_t5, 1)
                if old.real():
                    stats_3(old, s_bnB, s_stB)
                if here:
                    dve.wait_ge(s_t5, at.count(1, 1))
                scale(6, lambda: ts(col(6), col(5), col(2), 127.0 * float(INNER) ** 0.5,
                                    ALU.mult, ALU.mult))
                if here:
                    dve.wait_ge(s_tq, at.count(6, 6))
                    if at.rep >= 2:
                        dve.wait_ge(s_hT, at.count(1, -1))
                    ts(hr[:, at.odd, :], h2[:, at.odd, :], col(6), ROUND, ALU.mult, ALU.add)\
                        .then_inc(s_hi, 1)

            step_b(At(-2, 1))
            step_b(At(-1, 0))
            step_b(At(-1, 1))
            steps(dve, step_b, 0, B + 2, 4, 4)

            dve.wait_ge(s_stB, B)
            ts(rstd[:, :], var, EPS, None, ALU.add).then_inc(s_c0, 1)
            dve.wait_ge(s_pool0, 10)

            def normal_c(at):
                if at.rep >= 2:
                    dve.wait_ge(s_xcT, at.count(1, -1))
                ts(xc[:, at.odd, :], xb(at), stat[:, bass.ds(at.b, 1), 0],
                   rstd[:, bass.ds(at.b, 1)], ALU.subtract, ALU.mult).then_inc(s_xc, 1)

            def step_c(at):
                last, nxt, three = at.plus(-1), at.plus(1), at.plus(3)
                if nxt.real():
                    dve.wait_ge(s_qkC, nxt.count(1, 1))
                    if nxt.rep >= 2:
                        dve.wait_ge(s_sC, nxt.count(1, -1))
                    nc.vector.tensor_copy(qTc[:, nxt.odd, :, :],
                                          psQK[:, 0:D].rearrange("p (c s) -> p c s", c=2))
                    nc.vector.tensor_copy(kTc[:, nxt.odd, :, P:D],
                                          psQK[:, D:2 * D].rearrange("p (c s) -> p c s", c=2))\
                      .then_inc(s_qkCs, 1)
                if last.real():
                    dve.wait_ge(s_yC, last.count(1, 1))
                    dve.wait_ge(s_rC, last.count(1, 1))
                    nc.vector.scalar_tensor_tensor(xb(last), psYC[:, 0:D], smc[:, last.odd, 3:4],
                                                   xb(last), ALU.mult, ALU.add).then_inc(s_xC, 1)
                if at.real():
                    dve.wait_ge(s_eC, at.count(1, 1))
                    nc.vector.reciprocal(smc[:, at.odd, 2:3], smc[:, at.odd, 1:2])\
                      .then_inc(s_r0, 1)
                if last.real():
                    stats_1(last, s_xC, s_bnC, s_stC)
                if at.real():
                    dve.wait_ge(s_r0, at.count(1, 1))
                    if at.rep >= 2:
                        dve.wait_ge(s_xC, at.count(1, -1))
                    ts(smc[:, at.odd, 3:4], smc[:, at.odd, 2:3], tg[:, 1:2], None, ALU.mult)\
                        .then_inc(s_rC, 1)
                if three.real():
                    normal_c(three)
                if last.real():
                    stats_2(last, s_bnC)
                if nxt.real():
                    dve.wait_ge(s_sC, nxt.count(1, 1))
                    nc.vector.tensor_reduce(mxc[:, nxt.odd:nxt.odd + 1], psSc[:, 0:D], AX.X,
                                            ALU.max, negate=True).then_inc(s_c1, 1)
                if last.real():
                    stats_3(last, s_bnC, s_stC)
                if nxt.real():
                    dve.wait_ge(s_c1, nxt.count(1, 1))
                    if nxt.rep >= 2:
                        dve.wait_ge(s_eC, nxt.count(1, -1))
                    ts(smc[:, nxt.odd, 0:1], mxc[:, nxt.odd:nxt.odd + 1], float(D) ** -0.5, None,
                       ALU.mult).then_inc(s_mC, 1)

            normal_c(At(0, 0))
            step_c(At(-1, 0))
            step_c(At(-1, 1))
            steps(dve, step_c, 0, B + 1, 4, 4)

            dve.wait_ge(s_stC, B)
            ts(rstd[:, :], var, EPS, None, ALU.add).then_inc(s_d0, 1)
            dve.wait_ge(s_wD, 16 * 5)
            nc.vector.tensor_reduce(wmax[:, 0:1], wgu.rearrange("p c n -> p (c n)"), AX.X, ALU.max,
                                    apply_absolute_value=True).then_inc(s_d0, 1)
            dve.wait_ge(s_dP, 1)
            nc.vector.tensor_reduce(wmaxr[:, 0:1], bank[0][0:1, 0:P], AX.X, ALU.max)\
              .then_inc(s_d0, 1)
            dve.wait_ge(s_dP, 2)
            ts(wmax[:, 0:1], bank[0][:, 256:257], 1e-30, None, ALU.max).then_inc(s_d0, 1)
            dve.wait_ge(s_d0, 4)
            nc.vector.reciprocal(wmax[:, 1:2], wmax[:, 0:1]).then_inc(s_d0, 1)
            dve.wait_ge(s_d1, 1)
            for c in range(2):
                nc.vector.scalar_tensor_tensor(wgu_lo[:, c, :], wgu[:, c, :], wmax[:, 1:2],
                                               wgu_hi[:, c, :], ALU.mult, ALU.subtract)
            nc.vector.tensor_copy(sel, self_).then_inc(s_d0, 1)
            dve.wait_ge(s_pool0, 11)

            def normal_d(at):
                if at.rep >= 2:
                    dve.wait_ge(s_xdT, at.count(1, -1))
                ts(xd[:, at.odd, :], xb(at), stat[:, bass.ds(at.b, 1), 0],
                   rstd[:, bass.ds(at.b, 1)], ALU.subtract, ALU.mult).then_inc(s_xd, 1)

            def step_r(at):
                if at.plus(1).real():
                    normal_d(at.plus(1))
                if at.real():
                    dve.wait_ge(s_xdTs, at.count(1, 1))
                    cols = bass.ds(at.b * P, P)
                    for c in range(2):
                        ins = tt(xT_lo[:, c, cols], xdT[:, at.odd, c, :],
                                 xT_hi[:, c, cols], ALU.subtract)
                    ins.then_inc(s_xlo, 1)

            step_r(At(-1, 1))
            steps(dve, step_r, 0, B, 2, 2)

            u = Chain(dve, s_ur)
            dve.wait_ge(s_lgs, B)
            l8 = lg[:, :, 0:E]
            u(nc.vector.tensor_reduce(den[:, :], l8, AX.X, ALU.max))
            u.wait()
            wide = lambda t: t.unsqueeze(2).to_broadcast([P, B, E])
            tt(rk[:, 0, :, :], l8, wide(den[:, :]), ALU.subtract).then_inc(s_rt, 1)
            dve.wait_ge(s_rta, 2)
            other = rk[:, 0, :, :].unsqueeze(2).to_broadcast([P, B, E, E])
            own = rk[:, 0, :, :].unsqueeze(3).to_broadcast([P, B, E, E])
            cm = [cmp_[:, n, :].rearrange("p (b e j) -> p b e j", b=B, e=E) for n in range(2)]
            cf2 = [cmp_[:, n, :].rearrange("p (b k) -> p b k", b=B) for n in range(2)]
            tr = [tri[:, n, :].unsqueeze(1).to_broadcast([P, B, E * E]) for n in range(2)]
            u(tt(cm[0], other, own, ALU.is_ge))
            u(tt(cm[1], other, own, ALU.is_gt))
            u.wait()
            u(tt(cf2[0], cf2[0], tr[0], ALU.mult))
            u(tt(cf2[1], cf2[1], tr[1], ALU.mult))
            u.wait()
            u(tt(cmp_[:, 0, :], cmp_[:, 0, :], cmp_[:, 1, :], ALU.add))
            u.wait()
            u(nc.vector.tensor_reduce(rk[:, 1, :, :], cm[0], AX.X, ALU.add))
            u.wait()
            u(ts(rk[:, 1, :, :], rk[:, 1, :, :], 2.0, None, ALU.is_lt))
            u.wait()
            u(tt(rk[:, 2, :, :], rk[:, 0, :, :], rk[:, 1, :, :], ALU.mult))
            u.wait()
            u(nc.vector.tensor_reduce(den[:, :], rk[:, 2, :, :], AX.X, ALU.add))
            u.wait()
            u(nc.vector.reciprocal(den[:, :], den[:, :]))
            u.wait()
            u(tt(cf[:, :, 0:E], rk[:, 2, :, :], wide(den[:, :]), ALU.mult))
            u(ts(cf[:, :, E], cf[:, :, E], 1.0, None, ALU.add))
            u.wait()
            u(nc.vector.reciprocal(cf[:, :, E], cf[:, :, E]))
            u.wait()
            u(ts(cf[:, :, :], cf[:, :, :], tg[:, 3:4], None, ALU.mult))
            u.wait()
            u(nc.vector.tensor_copy(cfp[:, :, 0, :], cf[:, :, :]))
            u.wait()
            u(tt(cfr[:, :, :], cf[:, :, :], cfp[:, :, 0, :], ALU.subtract))
            u.wait()
            u(nc.vector.tensor_copy(cfp[:, :, 1, :], cfr[:, :, :]))
            u.wait()
            tt(cfp[:, :, 2, :], cfr[:, :, :], cfp[:, :, 1, :], ALU.subtract).then_inc(s_rt, 1)
            for s_credit in (s_t, s_hd, s_yD):
                dve.sem_inc(s_credit, 1)
            with dve.Fori(0, NG) as g:
                for c in range(NCH):
                    rows = min(P, HID - c * P)
                    dve.wait_ge(s_si, g * NCH + (c + 2))
                    dve.wait_ge(s_u, g * NCH + (c + 1))
                    nc.vector.scalar_tensor_tensor(hu[0:rows, c % 2, :], psU[c % 2][0:rows, :],
                                                   wmax[0:rows, 0:1], gs[0:rows, c % 2, :],
                                                   ALU.mult, ALU.mult).then_inc(s_t, 1)
                    dve.wait_ge(s_t, g * NCH + (c + 2))
                    dve.wait_ge(s_c, g * NCH + (c + 1))
                    dve.wait_ge(s_dn, g * NCH + max(c - 1, 1))
                    tt(hd[0:rows, c % 3, :], hu[0:rows, c % 2, :], psC[c % 2][0:rows, :],
                       ALU.mult).then_inc(s_hd, 1)
                dve.wait_ge(s_dn, g * NCH + (NCH + 1))
                xg = x_all[:, bass.ds(g * GROUP, GROUP), :].rearrange("p b d -> p (b d)")
                tt(xg, acc, xg, ALU.add).then_inc(s_yD, 1)


def host_arrays(i):
    f = lambda n: np.asarray(i[n])
    qk = np.array([d * H + hf * 8 + h for hf in range(2) for d in range(HD) for h in range(8)])
    swap = np.array([(d ^ 1) * H + hf * 8 + h for hf in range(2) for d in range(HD) for h in range(8)])
    vh = np.array([d * H + h for h in range(H) for d in range(HD)])
    mg = np.array([d * H + 4 * g + j for j in range(4) for d in range(HD) for g in range(4)])
    wq, wk, wv, wm = (f(f"L0_xattn_{n}") for n in ("Wq", "Wk", "Wv", "Wm"))
    bq, bk, bv, bm = (f(f"L0_xattn_{n}") for n in ("bq", "bk", "bv", "bm"))
    sign = np.array([1.0 if d % 2 else -1.0 for _ in range(2) for d in range(HD) for _ in range(8)],
                    np.float32)
    enc = f("L0_xattn_encoding")[:, 0, 0]
    dim = np.array([d for _ in range(2) for d in range(HD) for _ in range(8)])
    pad = np.zeros(P, np.float32)
    chunks = lambda w: w.reshape(-1, P, w.shape[1]).transpose(1, 0, 2)
    flat = lambda w: w.transpose(1, 0, 2).reshape(D, E * I)
    wgu = np.concatenate([flat(f("L1_ffn_w_gate")), f("L1_ffn_sw_gate"),
                          flat(f("L1_ffn_w_up")), f("L1_ffn_sw_up")], 1)
    wd = np.zeros((NCH * P, D), np.float32)
    wd[:HID] = np.concatenate([f("L1_ffn_w_down").reshape(E * I, D), f("L1_ffn_sw_down")], 0)
    expert = np.minimum(np.arange(NCH * P) // I, E)
    sel = np.tile(np.arange(NCO)[:, None] == expert[None, :], (3, 1)).astype(np.float32)
    j, e = np.arange(E)[None, :], np.arange(E)[:, None]
    tri = np.stack([(j < e).ravel(), (j > e).ravel()]).astype(np.float32)
    return {
        "w1": chunks(f("L0_ffn_w1").T), "w2": chunks(f("L0_ffn_w2").T),
        "wC": np.stack([chunks(f(f"L1_xattn_{n}").T) for n in ("wq", "wk", "wv", "wo")], 1),
        "ctxT": f("ctx_2048").transpose(0, 2, 1),
        "wgu": chunks(wgu), "wd": chunks(wd),
        "wr": chunks(np.concatenate([f("L1_ffn_gate_w").T, f("L1_ffn_shared_gate_w")], 1)),
        "sel": sel, "tri": tri,
        "x": f("x"), "ctx": f("ctx_2048"), "g_xattn": f("g_xattn"), "g_ffn": f("g_ffn"),
        "wA": np.stack([wq[qk].T, wq[swap].T, wk[qk].T, wk[swap].T, wv[vh].T, wm[:, mg].T], 1),
        "smallA": np.stack([bq[qk], bq[swap], bk[qk], bk[swap], sign, bm, bv[mg], pad], 1),
        "rot": np.stack([enc[0][:, dim].T, enc[1][:, dim].T], 1),
        "ident": np.eye(P, dtype=np.float32),
    }


def kernel(**inputs):
    import concourse.bacc as bacc
    from concourse.bass_utils import run_bass_kernel_spmd as run

    nc = bacc.Bacc("TRN2", target_bir_lowering=False, num_devices=1)
    arrays = {n: np.ascontiguousarray(v) for n, v in host_arrays(inputs).items()}
    a = {n: nc.dram_tensor(f"in_{n}", v.shape, mybir.dt.from_np(v.dtype), kind="ExternalInput").ap()
         for n, v in arrays.items()}
    out = nc.dram_tensor("out_x", (B, P, D), F32, kind="ExternalOutput").ap()
    build(nc, a, out)
    r = run(nc, [{f"in_{n}": v for n, v in arrays.items()}], core_ids=[0])
    return r.results[0]["out_x"]
```

```python
from contextlib import ExitStack

import numpy as np

import concourse.bass as bass
from concourse import mybir

F32 = mybir.dt.float32
BF16 = mybir.dt.bfloat16
F16 = mybir.dt.float16
ALU = mybir.AluOpType
ACT = mybir.ActivationFunctionType
AX = mybir.AxisListType

P = 128
B = 16
D = 256
H, HD = 16, 8
INNER = 1024
E, I, IS = 8, 176, 704
HID = E * I + IS
NCH = -(-HID // P)
FULL = HID // P * P
NCO = E + 1
GROUP = 4
NG = B // GROUP
EPS = 1e-5
ROUND = 1.5 * 2.0 ** 23
NPART = 3
STACK = NPART * NPART * HD
ONES = float(np.array([0x3F803F80], np.uint32).view(np.float32)[0])


class At:

    def __init__(self, half, odd, rep=None):
        self.half, self.odd = half, odd
        self.rep = 2 * half + odd if rep is None else rep

    def plus(self, k):
        n = self.odd + k
        return At(self.half + n // 2, n % 2, self.rep + k)

    @property
    def b(self):
        return self.half * 2 + self.odd

    def count(self, per, more):
        return self.half * (2 * per) + (self.odd * per + more)

    def real(self):
        return 0 <= self.rep < B


def steps(eng, body, first, last, lead, tail, cut=None, between=None):
    for n in range(first, lead):
        body(At(n // 2, n % 2))
    marks = [lead] + [cut] * (cut is not None) + [B - tail]
    for k in range(len(marks) - 1):
        if k:
            between()
        with eng.Fori(marks[k] // 2, marks[k + 1] // 2) as half:
            body(At(half, 0, marks[k]))
            body(At(half, 1, marks[k] + 1))
    for n in range(B - tail, last):
        body(At(n // 2, n % 2))


def build(nc, a, out):
    ctx = ExitStack()
    with ctx:
        def sb(name, shape, dt=F32):
            return ctx.enter_context(nc.sbuf_tensor(name, shape, dt))

        def sem(name):
            return ctx.enter_context(nc.semaphore(name))

        class Arena:

            def __init__(self, name, words):
                self.t, self.words, self.at = sb(name, [P, words]), words, 0

            def __call__(self, shape, dt=F32, rows=P):
                n = int(np.prod(shape)) if dt is F32 else int(np.prod(shape)) // 2
                v = self.t[0:rows, self.at:self.at + n]
                self.at += n
                assert self.at <= self.words, (self.at, self.words)
                v = v if dt is F32 else v.bitcast(dt)
                names = "abcd"[:len(shape)]
                if len(shape) == 1:
                    return v
                return v.rearrange(f"p ({' '.join(names)}) -> p {' '.join(names)}",
                                   **{k: n for k, n in zip(names, shape)})

        first = Arena("first_arena", 15360)
        qst = first([2, H, D], BF16)
        kst = first([2, H, D], BF16)
        pT = first([8, 2 * D])
        vst = first([2, 2, H, 32])
        o_sb = first([4, D])
        first.at = 0
        wgu = first([2, 2 * HID])
        first.at = 0
        wd_hi = first([NCH, D], F16)
        wd_lo = first([NCH, D], F16)
        first.at = 2 * 2 * HID
        wd = first([NCH, D])
        wC = first([4, 2, D])
        second = Arena("second_arena", 2 * 2 * HID)
        w1 = second([2, INNER])
        w2 = second([8, D])
        second.at = 0
        wgu_hi = second([2, 2 * HID], F16)
        wgu_lo = second([2, 2 * HID], F16)
        third = Arena("third_arena", 9856)
        w1q = third([2, INNER], BF16)
        w2q = third([8, D], BF16)
        h1 = third([INNER])
        h2 = third([2, INNER])
        hr = third([2, INNER])
        hT = third([2, 8, P], BF16)
        third.at = 0
        kTc = third([2, 2, D])
        vc = third([2, 2, D])
        xc = third([2, D])
        xcT = third([2, 2, P])
        qTc = third([2, 2, P])
        pc = third([2, D])
        pcT = third([2, P])
        oTc = third([2, P])
        third.at = 0
        gs = third([2, 512])
        hu = third([3, 512])
        hd_hi = third([2, 512], F16)
        hd_lo = third([2, 512], F16)
        third.at -= 2 * 512
        cmp_ = third([2, B * E * E])
        third.at = 9 * 512
        self_ = third([NCH * P], rows=3 * NCO)
        sel = third([NCH * P], BF16, rows=3 * NCO)
        cT = third([B * P], BF16, rows=3 * NCO)

        fourth = Arena("fourth_arena", 5632)
        ctx_in = fourth([2, D])
        xn = fourth([2, D])
        rt = fourth([2, 2, D])
        res = fourth([2, D])
        parts = fourth([2, 2, 3, D], BF16)
        oc = fourth([2, D])
        rden = fourth([D])
        on = fourth([D])
        fourth.at = 0
        xT_hi = fourth([2, B * P], F16)
        xT_lo = fourth([2, B * P], F16)
        xd = fourth([2, D])
        xdT = fourth([2, 2, P])

        x_all = sb("x_all", [P, B, D])
        stat = sb("stat", [P, B, 2])
        bnst = sb("bnst", [P, 2, 6])
        agg = sb("agg", [P, 2])
        rstd = sb("rstd", [P, B])
        half_pow = sb("half_pow", [P, 2 * B])
        ident = sb("ident", [P, P])
        identb = sb("identb", [P, P], BF16)
        gates = sb("gates", [P, 4])
        tg = sb("tg", [P, 4])
        pair = [ctx.enter_context(nc.psum_tensor(f"pair{n}", [P, 1024], F32)) for n in range(3)]
        last2 = [ctx.enter_context(nc.psum_tensor(f"bank{n}", [P, 512], F32)) for n in range(6, 8)]
        bank = [pair[n // 2][:, (n % 2) * 512:(n % 2) * 512 + 512] for n in range(6)]
        bank += [t[:, :] for t in last2]

        smallA = sb("smallA", [P, 8])
        wA = sb("wA", [P, 6, P])
        rot = sb("rot", [P, 2, D])
        tgbm = sb("tgbm", [P, 1])
        nmr = sb("nmr", [P, B])
        nmax = sb("nmax", [P, 2, 2, 2, 8])
        npart = sb("npart", [P, 2, 2, 2, 8], BF16)
        nmT = sb("nmT", [16, 2, D], BF16)

        wsum = sb("wsum", [P, 2])
        onesf = sb("onesf", [P, P])
        wmean = sb("wmean", [P, 2])
        wscale = sb("wscale", [P, 2])
        tb = sb("tb", [P, 8, B])
        xr = sb("xr", [P, D])
        xi = sb("xi", [P, 2, D], BF16)
        xiT = sb("xiT", [P, 2, 2, P], BF16)
        ssq = sb("ssq", [P, 2])
        dqw = sb("dqw", [P, 1])
        mxc = sb("mxc", [P, 2])
        den = sb("den", [P, B])
        nrm = sb("nrm", [P, 2])
        tq = sb("tq", [P, 2, 8])
        smc = sb("smc", [P, 2, 4])
        wr = sb("wr", [P, 2, NCO])
        wmp = sb("wmp", [P, 2, 8])
        wmax = sb("wmax", [P, 2])
        wmaxr = sb("wmaxr", [1, 2])
        wsc = sb("wsc", [P, 8])
        vard = sb("vard", [P, 4])
        rstdd = sb("rstdd", [P, 2])
        lg = sb("lg", [P, B, NCO])
        rk = sb("rk", [P, 4, B, E])
        tri = sb("tri", [P, E * E])
        cf = sb("cf", [P, B, NCO])
        cfr = sb("cfr", [P, B, NCO])
        cfp = sb("cfp", [P, B, 3, NCO], BF16)

        s_wB = sem("ffn_weights_loaded")
        s_wC = sem("attention_weights_loaded")
        s_wD = sem("expert_weights_loaded")
        s_wS = sem("sel_loaded")
        s_b0 = sem("prepared_b")
        s_b1 = sem("prepared_b_scalar")
        s_xi = sem("x_rounded")
        s_xiT = sem("x_rounded_turned")
        s_xiTs = sem("x_rounded_turned_stored")
        s_h = sem("hidden_done")
        s_g1 = sem("gelu1_done")
        s_g2 = sem("gelu2_done")
        s_sq = sem("squares_summed")
        s_nr = sem("norm_done")
        s_tq = sem("hidden_scale_step")
        s_t5 = sem("hidden_scale_inverted")
        s_hi = sem("hidden_rounded")
        s_hT = sem("hidden_turned")
        s_hTs = sem("hidden_turned_stored")
        s_yB = sem("ffn_output_done")
        s_xB = sem("x_updated_b")
        s_bnB = sem("bn_stats_done_b")
        s_stB = sem("stats_ready_b")
        s_kv = [sem("ctx_keys_loaded_even"), sem("ctx_keys_loaded_odd")]
        s_xc = sem("xc_ready")
        s_xcT = sem("xc_turned")
        s_xcTs = sem("xc_turned_stored")
        s_qkC = sem("qk_done_c")
        s_qkCs = sem("qk_stored_c")
        s_vC = sem("v_done_c")
        s_vCs = sem("v_stored_c")
        s_sC = sem("scores_done_c")
        s_mC = sem("max_ready_c")
        s_eC = sem("exp_done_c")
        s_rC = sem("sum_inverted_c")
        s_pT = sem("probs_turned")
        s_pTs = sem("probs_turned_stored")
        s_oC = sem("o_done_c")
        s_oCs = sem("o_stored_c")
        s_yC = sem("attention_output_done")
        s_xC = sem("x_updated_c")
        s_bnC = sem("bn_stats_done_c")
        s_stC = sem("stats_ready_c")
        s_d0 = sem("prepared_d")
        s_dP = sem("prepared_d_tensor")
        s_xd = sem("xd_ready")
        s_xdT = sem("xd_turned")
        s_xdTs = sem("xdT_stored")
        s_xr = sem("x_scaled")
        s_vb = sem("vector_step_b")
        s_ur = sem("vector_step_routing")
        s_ws = sem("weights_summed")
        s_c1 = sem("max_found_c")
        s_r0 = sem("sum_inverted_step")
        s_vB = sem("variance_ready_b")
        s_rsB = sem("rstd_ready_b")
        s_vd = sem("variance_ready_d")
        s_rsd = sem("rstd_ready_d")
        s_wmp = sem("weight_maxima_of_pieces")
        s_whi = sem("weights_high_parts")
        s_wlo = sem("weights_low_parts")
        s_sel = sem("sel_ready")
        s_xlo = sem("xT_lo_stored")
        s_hu = sem("up_taken")
        s_hh = sem("hidden_high_part")
        s_hl = sem("hidden_low_part")
        s_lg = sem("logits_done")
        s_lgs = sem("logits_stored")
        s_rt = sem("routing_step")
        s_rta = sem("routing_exp_done")
        s_cT = sem("coefficients_turned")
        s_cTs = sem("coefficients_turned_stored")
        s_g = sem("gate_done")
        s_u = sem("up_done")
        s_c = sem("coefficients_spread")
        s_si = sem("silu_done")
        s_hd = sem("hidden_ready_d")
        s_dn = sem("down_done")
        s_yD = sem("outputs_ready")

        s_x = [sem(f"x_loaded_{g}") for g in range(4)]
        s_cst = sem("constants_loaded")
        s_ctx = [sem("ctx_loaded_even"), sem("ctx_loaded_odd")]
        s_prep = sem("prepared_by_vector")
        s_pool0 = sem("prepared_by_gpsimd")
        s_act0 = sem("prepared_by_scalar")
        s_bm = sem("bias_product_done")
        s_dve = sem("vector_step")
        s_pool = sem("gpsimd_step")
        s_xn = sem("xn_ready")
        s_q = sem("q_done")
        s_qu = sem("q_used")
        s_k = sem("k_done")
        s_ku = sem("k_used")
        s_v = sem("v_done")
        s_vu = sem("v_stored")
        s_qp = sem("q_parts_ready")
        s_kp = sem("k_parts_ready")
        s_stk = [[sem(f"stack_loaded_{u}_{hf}") for hf in range(2)] for u in range(2)]
        s_qw = [sem("q_parts_written_even"), sem("q_parts_written_odd")]
        s_kw = [sem("k_parts_written_even"), sem("k_parts_written_odd")]
        s_ow = sem("o_written")
        s_s = sem("scores_done")
        s_max = sem("max_done")
        s_sp = sem("max_parts_ready")
        s_mt = sem("max_turned")
        s_me = sem("max_rows_stored")
        s_mx = [[sem(f"max_rows_loaded_{u}_{hf}") for hf in range(2)] for u in range(2)]
        s_st = sem("shifted_scores_done")
        s_exp = sem("exp_done")
        s_pv = sem("pv_done")
        s_oe = sem("o_stored")
        s_oc = sem("o_compact")
        s_on = sem("o_normalised")
        s_rd = sem("denominators_inverted")
        s_bn = sem("bn_stats_done_a")
        s_ag = sem("bn_aggregate_done_a")
        s_apart = {e: sem(f"apart_{n}") for n, e in enumerate(
            (mybir.EngineType.SP, mybir.EngineType.Pool, mybir.EngineType.PE,
             mybir.EngineType.DVE))}
        s_wm = sem("merge_done")
        s_xA = sem("x_updated_a")
        s_st_r = sem("stats_ready_a")
        s_out = sem("stored")

        block = ctx.enter_context(nc.Block())

        CONST_DMAS = 6
        PB_EARLY, PB_LATE = 2, 4
        PD_COMBINED, PD_ROW, PD_SPREAD, PD_SCALES = 1, 2, 3, 6
        RT_DONE = 2
        q_scr = [nc.dram_tensor(f"q_scratch_{u}", (2, NPART * HD, 8 * D), BF16).ap() for u in range(2)]
        k_scr = [nc.dram_tensor(f"k_scratch_{u}", (2, NPART * HD, 8 * D), BF16).ap() for u in range(2)]
        o_scr = nc.dram_tensor("o_scratch", (4, 32, 4 * D), F32).ap()
        psS = pair
        psST = [bank[4], bank[5]]
        psPV = bank[6]
        psM = bank[7]
        psMb = bank[7].bitcast(BF16)
        psXT, psH = bank[7].bitcast(BF16), [pair[0][:, :], pair[1][:, :]]
        psHT = pair[2][:, :]
        psYB = bank[6]
        psTx, psTp, psQK, psV, psO, psSc, psYC = bank[0:7]
        psTd = bank[7]
        psWm = bank[7]
        psG, psU, psC, acc = bank[4:6], bank[6:8], bank[0:2], pair[1][:, :]

        GU_PIECE, DN_PIECE = 2 * 2 * HID // 8, NCH * D // 8

        def rows_of(c):
            return min(P, HID - (c % NCH) * P)

        def slot(c):
            return c % NCH % 2

        def hu_slot(c):
            return 2 if c % NCH == NCH - 1 else c % NCH % 2

        def exists(g, c):
            return c >= 0 or not (isinstance(g, int) and g == 0)

        def wait_slot(eng, s_used, g, c):
            if exists(g, c - 2):
                eng.wait_ge(s_used, g * NCH + max(c - 1, min(c, 0)))

        class Chain:

            def __init__(self, eng, s):
                self.eng, self.s, self.n, self.base = eng, s, 0, 0

            def __call__(self, ins):
                ins.then_inc(self.s, 1)
                self.n += 1
                return ins

            def wait(self):
                self.eng.wait_ge(self.s, self.base + self.n)

        def apart(eng):
            eng.sem_inc(s_apart[eng.engine], 1)

        @block.sync
        def _(sp):
            def load_x(g):
                sp.dma_start(x_all[:, 4 * g:4 * g + 4, :],
                             a["x"][4 * g:4 * g + 4].rearrange("b s d -> s b d")).then_inc(s_x[g], 16)

            def load_ctx(at):
                if at.rep >= 2:
                    sp.wait_ge(s_v, at.count(1, -1))
                    apart(sp)
                sp.dma_start(ctx_in[:, at.odd, :], a["ctx"][bass.ds(at.b, 1)]
                             .rearrange("b s d -> (b s) d")).then_inc(s_ctx[at.odd], 16)

            load_x(0)
            sp.dma_start(smallA[:, :], a["smallA"]).then_inc(s_cst, 16)
            sp.dma_start(wA[:, :, :], a["wA"]).then_inc(s_cst, 16)
            sp.dma_start(rot[:, :, :], a["rot"]).then_inc(s_cst, 16)
            sp.dma_start(ident[:, :], a["ident"]).then_inc(s_cst, 16)
            sp.dma_start(gates[:, 0:2], a["g_xattn"].partition_broadcast(P)).then_inc(s_cst, 16)
            sp.dma_start(gates[:, 2:4], a["g_ffn"].partition_broadcast(P)).then_inc(s_cst, 16)
            load_ctx(At(0, 0))
            load_ctx(At(0, 1))
            for g in range(1, 4):
                load_x(g)
            sp.dma_start(w1, a["w1"]).then_inc(s_wB, 16)
            sp.dma_start(w2, a["w2"]).then_inc(s_wB, 16)

            def write_parts(at, w):
                scr, ready, written = ((q_scr, s_qp, s_qw), (k_scr, s_kp, s_kw))[w]
                sp.wait_ge(ready, at.count(1, 1))
                for hf in range(2):
                    sp.dma_start(scr[at.odd][hf].rearrange("(a d) (h n) -> (d h) a n", a=NPART, n=D),
                                 parts[64 * hf:64 * hf + 64, at.odd, w, :, :])\
                      .then_inc(written[at.odd], 16)

            def load_stack(at, hf, half_way=lambda: None):
                if at.rep >= 2:
                    sp.wait_ge(s_st, at.count(16, -32 + 8 * hf + 8))
                    apart(sp)
                sp.wait_ge(s_qw[at.odd], at.half * 32 + 32)
                sp.wait_ge(s_kw[at.odd], at.half * 32 + 32)
                heads = slice(8 * hf, 8 * hf + 8)
                n = NPART * HD
                sp.dma_start(kst[0:STACK, at.odd, heads, :],
                             k_scr[at.odd][hf].unsqueeze(0).to_broadcast([NPART, n, 8 * D]))\
                  .then_inc(s_stk[at.odd][hf], 16)
                for a_ in range(NPART):
                    if a_ == 1:
                        half_way()
                    sp.dma_start(qst[n * a_:n * a_ + n, at.odd, heads, :],
                                 q_scr[at.odd][hf, HD * a_:HD * a_ + HD].unsqueeze(0)
                                 .to_broadcast([NPART, HD, 8 * D])).then_inc(s_stk[at.odd][hf], 16)

            def load_max(at, hf):
                sp.wait_ge(s_me, at.count(2, hf + 1))
                sp.dma_start(qst[STACK:STACK + 2, at.odd, 8 * hf:8 * hf + 8, :], nmT[:, hf, :])\
                  .then_inc(s_mx[at.odd][hf], 16)

            def write_o(at):
                sp.wait_ge(s_oe, at.count(2, 2))
                apart(sp)
                if at.rep >= 1:
                    sp.wait_ge(s_oc, at.count(32, 0))
                sp.dma_start(o_scr.rearrange("j r n -> (j r) n"), o_sb).then_inc(s_ow, 16)

            def compact(at):
                sp.wait_ge(s_ow, at.count(16, 16))
                apart(sp)
                if at.rep >= 1:
                    sp.wait_ge(s_on, at.count(1, 0))
                for w in range(2):
                    sp.dma_start(oc[:, w, :], o_scr[:, HD * w:HD * w + HD, :]
                                 .rearrange("j d (g n) -> j (d g) n", g=4)).then_inc(s_oc, 16)

            def step(at):
                last, nxt, two, three = at.plus(-1), at.plus(1), at.plus(2), at.plus(3)
                if nxt.real():
                    load_stack(nxt, 1)
                if at.real():
                    load_max(at, 1)
                if last.real():
                    write_o(last)
                if two.real():
                    write_parts(two, 1)
                if three.real() and three.rep >= 2:
                    load_ctx(three)
                rows = lambda: load_max(nxt, 0) if nxt.real() else None
                if two.real():
                    load_stack(two, 0, rows)
                else:
                    rows()
                if last.real():
                    compact(last)
                if three.real():
                    if three.rep >= 2:
                        for hf in range(2):
                            sp.wait_ge(s_stk[three.odd][hf], three.half * 64)
                            apart(sp)
                    write_parts(three, 0)

            sp.wait_ge(s_pool0, 1)
            write_parts(At(0, 0), 0)
            step(At(-1, 0))
            step(At(-1, 1))
            steps(sp, step, 0, B + 1, 4, 4)

            sp.wait_ge(s_xA, B)
            sp.dma_start(wC[:, :, :, :], a["wC"]).then_inc(s_wC, 16)
            sp.dma_start(wr[:, :, :], a["wr"]).then_inc(s_wC, 16)
            sp.dma_start(wgu[:, :, :], a["wgu"]).then_inc(s_wD, 16)
            sp.dma_start(wd[:, :, :], a["wd"]).then_inc(s_wD, 16)
            sp.dma_start(tri[:, :], a["tri"].partition_broadcast(P)).then_inc(s_wD, 16)

            sp.wait_ge(s_xB, B)
            sp.dma_start(self_, a["sel"]).then_inc(s_wS, 16)

            def load_keys(at):
                if at.rep >= 2:
                    sp.wait_ge(s_sC, at.count(1, -1))
                    sp.wait_ge(s_oC, at.count(1, -1))
                sp.dma_start(kTc[:, at.odd, :, 0:P],
                             a["ctxT"][bass.ds(at.b, 1)].rearrange("b (c p) s -> p (b c) s", p=P))\
                  .then_inc(s_kv[at.odd], 16)
                sp.dma_start(vc[:, at.odd, 0, :], a["ctx"][bass.ds(at.b, 1)]
                             .rearrange("b s d -> (b s) d")).then_inc(s_kv[at.odd], 16)

            steps(sp, load_keys, 0, B, 2, 2)

            for g in range(NG):
                sp.wait_ge(s_yD, g + 1)
                sp.dma_start(out[GROUP * g:GROUP * g + GROUP].rearrange("b s d -> s b d"),
                             x_all[:, GROUP * g:GROUP * g + GROUP, :]).then_inc(s_out, 16)
            sp.wait_ge(s_out, 16 * NG)

        @block.gpsimd
        def _(pool):
            ch = Chain(pool, s_pool0)
            ch(nc.gpsimd.memset(kst[64:96, :, :, :].bitcast(F32), ONES))
            ch.wait()
            ch(nc.gpsimd.memset(half_pow[:, 0:B], -0.5))
            ch(nc.gpsimd.memset(half_pow[:, B:2 * B], 0.5))
            nc.gpsimd.memset(onesf[:, :], 1.0)
            ch(nc.gpsimd.memset(vst[:, :, :, :, 8:16], 1.0))
            ch(nc.gpsimd.memset(vst[:, :, :, :, 16:32], 0.0))
            ch.wait()

            def power_of_variance(batches, after):
                pool.wait_ge(s_prep, after)
                n = batches.stop - batches.start
                nc.gpsimd.tensor_tensor(rstd[:, batches], rstd[:, batches], half_pow[:, 0:n],
                                        ALU.pow).then_inc(s_pool0, 1)

            power_of_variance(slice(0, 4), 1)

            def split(at, w, used, ready, written):
                pool.wait_ge(used, at.count(1, 1))
                if at.rep >= 2:
                    pool.wait_ge(written[at.odd], at.half * 32)
                base = at.count(8, 4 * w - 4) if at.rep >= 1 else 0
                def done(ins, k):
                    ins.then_inc(s_pool, 1)
                    pool.wait_ge(s_pool, base + k)
                    if k in (1, 3):
                        apart(pool)
                r = res[:, w, :]
                done(nc.gpsimd.tensor_tensor(r, rt[:, w, 0, :], rt[:, w, 1, :], ALU.add), 1)
                done(nc.gpsimd.tensor_copy(parts[:, at.odd, w, 0, :], r), 2)
                done(nc.gpsimd.tensor_tensor(r, r, parts[:, at.odd, w, 0, :], ALU.subtract), 3)
                done(nc.gpsimd.tensor_copy(parts[:, at.odd, w, 1, :], r), 4)
                nc.gpsimd.tensor_tensor(parts[:, at.odd, w, 2, :], r, parts[:, at.odd, w, 1, :],
                                        ALU.subtract).then_inc(ready, 1)

            def divide(at):
                pool.wait_ge(s_rd, at.count(1, 1))
                if at.rep >= 1:
                    pool.wait_ge(s_wm, at.count(1, 0))
                nc.gpsimd.tensor_tensor(on[:, :], oc[:, 0, :], rden, ALU.mult)\
                  .then_inc(s_on, 1)

            def norms(batches, after):
                pool.wait_ge(s_b0, after)
                n = batches.stop - batches.start
                nc.gpsimd.tensor_tensor(rstd[:, batches], rstd[:, batches], half_pow[:, 0:n],
                                        ALU.pow)
                nc.gpsimd.tensor_tensor(tb[:, 3, batches], tb[:, 3, batches],
                                        half_pow[:, B:B + n], ALU.pow).then_inc(s_pool0, 1)

            def step(at):
                if at.plus(-2).real():
                    divide(at.plus(-2))
                if at.plus(3).real():
                    split(at.plus(3), 0, s_qu, s_qp, s_qw)
                    split(at.plus(3), 1, s_ku, s_kp, s_kw)

            split(At(0, 0), 0, s_qu, s_qp, s_qw)
            split(At(0, 1), 0, s_qu, s_qp, s_qw)
            split(At(0, 1), 1, s_ku, s_kp, s_kw)
            power_of_variance(slice(4, B), 5)
            step(At(-1, 1))
            steps(pool, step, 0, B, 4, 4)
            norms(slice(0, B - 3), 1)
            step(At(B // 2, 0))
            step(At(B // 2, 1))
            norms(slice(B - 3, B), 3)

            def rstd_b(at):
                pool.wait_ge(s_vB, at.count(1, 1))
                apart(pool)
                nc.gpsimd.tensor_tensor(rstd[:, bass.ds(at.b, 1)], vard[:, 2 + at.odd:3 + at.odd],
                                        half_pow[:, 0:1], ALU.pow).then_inc(s_rsB, 1)

            def norm_b(at):
                pool.wait_ge(s_sq, at.count(1, 1))
                if at.rep >= 2:
                    pool.wait_ge(s_hi, at.count(1, -1))
                nc.gpsimd.tensor_tensor(nrm[:, at.odd:at.odd + 1], ssq[:, at.odd:at.odd + 1],
                                        half_pow[:, B:B + 1], ALU.pow).then_inc(s_nr, 1)

            def step_b(at):
                if at.real():
                    norm_b(at)
                if at.plus(-3).real():
                    rstd_b(at.plus(-3))

            steps(pool, step_b, 0, B + 3, 4, 4)
            pool.wait_ge(s_wS, 16)
            nc.gpsimd.tensor_copy(sel, self_).then_inc(s_sel, 1)

            def rstd_d(at):
                pool.wait_ge(s_vd, at.count(1, 1))
                if at.rep >= 2:
                    pool.wait_ge(s_xd, at.count(1, -1))
                nc.gpsimd.tensor_tensor(rstdd[:, at.odd:at.odd + 1], vard[:, at.odd:at.odd + 1],
                                        half_pow[:, 0:1], ALU.pow).then_inc(s_rsd, 1)

            steps(pool, rstd_d, 0, B, 2, 2)

        @block.scalar
        def _(act):
            act.wait_ge(s_cst, 16 * CONST_DMAS)
            nc.scalar.activation(tg[:, :], gates[:, :], ACT.Tanh).then_inc(s_act0, 1)
            def normalise(at):
                if at.rep >= 2:
                    act.wait_ge(s_q, at.count(1, -1))
                if at.rep == 4:
                    act.wait_ge(s_prep, 6)
                nc.scalar.activation(
                    xn[:, at.odd, :], x_all[:, bass.ds(at.b, 1), :].rearrange("p b d -> p (b d)"),
                    ACT.Identity, bias=nmr[:, bass.ds(at.b, 1)], scale=rstd[:, bass.ds(at.b, 1)])\
                  .then_inc(s_xn, 1)

            act.wait_ge(s_prep, 4)
            normalise(At(0, 0))
            normalise(At(0, 1))
            act.wait_ge(s_wB, 32)
            nc.scalar.activation(h2[:, :, :], w1[:, :, :], ACT.Abs, accum_out=wsum[:, 0:1])\
              .then_inc(s_b1, 1)
            act.wait_ge(s_b1, 1)
            nc.scalar.activation(h2[:, :, :].rearrange("p c i -> p (c i)"),
                                 w2[:, :, :].rearrange("p c i -> p (c i)"), ACT.Abs,
                                 accum_out=wsum[:, 1:2]).then_inc(s_b1, 1)

            def exp(at, h):
                act.wait_ge(s_st, at.count(16, h + 1))
                if at.rep > 0 or h >= 8:
                    act.wait_ge(s_pv, at.count(4, h // 4 - 1))
                nc.scalar.activation(pT[:, h % 8, :], psST[h % 2][:, :], ACT.Exp,
                                     scale=float(HD) ** -0.5).then_inc(s_exp, 1)

            def store_o(at, pair):
                act.wait_ge(s_pv, at.count(4, 2 * pair + 2))
                if at.rep >= 1:
                    act.wait_ge(s_ow, at.count(16, 0))
                nc.scalar.activation(o_sb[:, 2 * pair:2 * pair + 2, :],
                                     psPV[:, :].rearrange("p (g n) -> p g n", g=2),
                                     ACT.Copy).then_inc(s_oe, 1)

            def store_max(at, hf):
                act.wait_ge(s_mt, at.count(2, hf + 1))
                if at.rep >= 1:
                    last = at.plus(-1)
                    act.wait_ge(s_mx[last.odd][hf], last.half * 16 + 16)
                nc.scalar.activation(nmT[:, hf, :], psMb[0:16, 0:D], ACT.Copy).then_inc(s_me, 1)

            def store_v(at):
                act.wait_ge(s_v, at.count(1, 1))
                if at.rep == 0:
                    act.wait_ge(s_pool0, 5)
                if at.rep >= 2:
                    act.wait_ge(s_pv, at.count(4, -4))
                for c in range(2):
                    ins = nc.scalar.activation(
                        vst[:, at.odd, c, :, 0:HD],
                        psM[:, c * P:c * P + P].rearrange("p (h d) -> p h d", h=H), ACT.Copy)
                ins.then_inc(s_vu, 1)

            def step(at):
                nxt, last, three = at.plus(1), at.plus(-1), at.plus(3)
                for slot in range(8):
                    if at.real():
                        exp(at, 2 * slot)
                        exp(at, 2 * slot + 1)
                    if slot == 1 and last.real():
                        store_o(last, 1)
                    if slot == 1 and at.real():
                        store_max(at, 1)
                    if slot == 2 and nxt.real():
                        store_v(nxt)
                    if slot == 0 and three.real():
                        normalise(three)
                    if slot == 5 and at.real():
                        store_o(at, 0)
                    if slot == 5 and nxt.real():
                        store_max(nxt, 0)

            step(At(-1, 1))
            steps(act, step, 0, B + 1, 2, 4)

            act.wait_ge(s_b0, PB_EARLY)

            def store_xiT(at):
                act.wait_ge(s_xiT, at.count(1, 1))
                if at.rep >= 2:
                    act.wait_ge(s_h, at.count(1, -1))
                nc.scalar.activation(xiT[:, at.odd, :, :],
                                     psXT[:, 0:D].rearrange("p (c s) -> p c s", c=2), ACT.Copy)\
                  .then_inc(s_xiTs, 1)

            def gelu(at):
                act.wait_ge(s_h, at.count(1, 1))
                if at.rep >= 1:
                    act.wait_ge(s_sq, at.count(1, 0))
                nc.scalar.activation(h1[:, :], psH[at.odd], ACT.Gelu,
                                     scale=tb[:, 6, bass.ds(at.b, 1)]).then_inc(s_g1, 1)

            def gelu_again(at):
                act.wait_ge(s_g1, at.count(1, 1))
                if at.rep >= 2:
                    act.wait_ge(s_hi, at.count(1, -1))
                elif at.rep == 0:
                    act.wait_ge(s_b1, 2)
                nc.scalar.activation(h2[:, at.odd, :], h1[:, :], ACT.Gelu).then_inc(s_g2, 1)

            def squares(at):
                act.wait_ge(s_g2, at.count(1, 1))
                nc.scalar.activation(h1[:, :], h2[:, at.odd, :], ACT.Square,
                                     accum_out=ssq[:, at.odd:at.odd + 1]).then_inc(s_sq, 1)

            def store_hT(at):
                act.wait_ge(s_hT, at.count(1, 1))
                if at.rep >= 2:
                    act.wait_ge(s_yB, at.count(1, -1))
                nc.scalar.activation(hT[:, at.odd, :, :], psHT.rearrange("p (c s) -> p c s", c=8),
                                     ACT.Copy, bias=-ROUND).then_inc(s_hTs, 1)

            def act_b(at):
                last, nxt, two = at.plus(-1), at.plus(1), at.plus(2)
                if two.real():
                    store_xiT(two)
                if nxt.real():
                    gelu(nxt)
                if last.real():
                    store_hT(last)
                if nxt.real():
                    gelu_again(nxt)
                    squares(nxt)

            act_b(At(-1, 0))
            act_b(At(-1, 1))
            steps(act, act_b, 0, B + 1, 4, 4)

            act.wait_ge(s_xB, B)

            flat = lambda t: t.rearrange("p a b -> p (a b)")

            def high_part(n, at, src, dst, size, scale):
                cols = bass.ds(at.count(size, -n * size), size)
                nc.scalar.activation(flat(dst)[:, cols], flat(src)[:, cols], ACT.Copy,
                                     scale=scale).then_inc(s_whi, 1)

            def act_c(at):
                nxt, two, old, older = at.plus(1), at.plus(2), at.plus(-2), at.plus(-3)
                if older.real():
                    act.wait_ge(s_lg, older.count(1, 1))
                    nc.scalar.activation(lg[:, bass.ds(older.b, 1), :].rearrange("p b e -> p (b e)"),
                                         psTd[:, D:D + NCO], ACT.Copy).then_inc(s_lgs, 1)
                if nxt.real():
                    act.wait_ge(s_vC, nxt.count(1, 1))
                    if nxt.rep >= 2:
                        act.wait_ge(s_oC, nxt.count(1, -1))
                    nc.scalar.activation(vc[:, nxt.odd, 1, :], psV[:, 0:D], ACT.Copy)\
                      .then_inc(s_vCs, 1)
                if at.real():
                    act.wait_ge(s_pT, at.count(1, 1))
                    if at.rep >= 1:
                        act.wait_ge(s_oC, at.count(1, 0))
                    nc.scalar.activation(pcT[:, :, :],
                                         psTp[:, 0:D].rearrange("p (c s) -> p c s", c=2),
                                         ACT.Copy).then_inc(s_pTs, 1)
                if two.real():
                    act.wait_ge(s_xcT, two.count(1, 1))
                    if two.rep >= 2:
                        act.wait_ge(s_vC, two.count(1, -1))
                    nc.scalar.activation(xcT[:, two.odd, :, :],
                                         psTx[:, 0:D].rearrange("p (c s) -> p c s", c=2),
                                         ACT.Copy).then_inc(s_xcTs, 1)
                if 8 <= at.rep < 12:
                    high_part(8, at, wgu, wgu_hi, 2 * GU_PIECE, wsc[:, 2:3])
                elif 12 <= at.rep < 16:
                    if at.rep == 12:
                        act.wait_ge(s_wlo, 4)
                    high_part(12, at, wd, wd_hi, 2 * DN_PIECE, wsc[:, 3:4])
                if at.real():
                    act.wait_ge(s_oC, at.count(1, 1))
                    if at.rep >= 1:
                        act.wait_ge(s_yC, at.count(1, 0))
                    nc.scalar.activation(oTc[:, :, :],
                                         psO[:, 0:D].rearrange("p (c s) -> p c s", c=2),
                                         ACT.Copy).then_inc(s_oCs, 1)
                if nxt.real():
                    act.wait_ge(s_mC, nxt.count(1, 1))
                    if nxt.rep >= 2:
                        act.wait_ge(s_pT, nxt.count(1, -1))
                    nc.scalar.activation(pc[:, nxt.odd, :], psSc[:, 0:D], ACT.Exp,
                                         bias=smc[:, nxt.odd, 0:1], scale=float(D) ** -0.5,
                                         accum_out=smc[:, nxt.odd, 1:2]).then_inc(s_eC, 1)
                if old.real():
                    act.wait_ge(s_xdT, old.count(1, 1))
                    turned = psTd[:, 0:D].rearrange("p (c s) -> p c s", c=2)
                    nc.scalar.activation(xT_hi[:, :, bass.ds(old.b * P, P)], turned, ACT.Copy)
                    if old.rep >= 2:
                        act.wait_ge(s_xlo, old.count(1, -1))
                        act.wait_ge(s_lg, old.count(1, -1))
                    nc.scalar.activation(xdT[:, old.odd, :, :], turned, ACT.Copy)\
                      .then_inc(s_xdTs, 1)

            act_c(At(-1, 0))
            act_c(At(-1, 1))
            steps(act, act_c, 0, B + 3, 4, 4, 8, lambda: act.wait_ge(s_d0, PD_SCALES))

            act.wait_ge(s_rt, 1)
            nc.scalar.activation(rk[:, 0, :, :], rk[:, 0, :, :], ACT.Exp).then_inc(s_rta, 1)
            nc.scalar.activation(cf[:, :, E], lg[:, :, E], ACT.Exp, scale=-1.0).then_inc(s_rta, 1)

            def silu(g, c):
                n = rows_of(c)
                act.wait_ge(s_g, g * NCH + (c + 1))
                wait_slot(act, s_hu, g, c)
                nc.scalar.activation(gs[0:n, slot(c), :], psG[slot(c)][0:n, :], ACT.Silu,
                                     scale=wsc[0:n, 0:1]).then_inc(s_si, 1)

            def high_hidden(g, c):
                n = rows_of(c)
                act.wait_ge(s_hd, g * NCH + (c + 1))
                wait_slot(act, s_dn, g, c)
                nc.scalar.activation(hd_hi[0:n, slot(c), :], hu[0:n, hu_slot(c), :], ACT.Copy)\
                  .then_inc(s_hh, 1)

            def act_group(g):
                for c in range(NCH):
                    silu(g, c)
                    if not exists(g, 0 - 1) and c == 1:
                        for k in range(NG):
                            act.wait_ge(s_cT, k + 1)
                            nc.scalar.activation(cT[:, k * 512:k * 512 + 512],
                                                 bank[k].bitcast(BF16)[0:3 * NCO, 0:512], ACT.Copy)\
                              .then_inc(s_cTs, 1)
                    if exists(g, c - 1):
                        high_hidden(g, c - 1)

            act_group(0)
            with act.Fori(1, NG) as g:
                act_group(g)
            high_hidden(NG - 1, NCH - 1)

        @block.tensor
        def _(pe):
            pe.wait_ge(s_cst, 16 * CONST_DMAS)
            pe.wait_ge(s_prep, 2)
            nc.tensor.matmul(psM[:, 0:1], wA[:, 5, :], smallA[:, 6:7], start=True, stop=True)\
              .then_inc(s_bm, 1)
            pe.wait_ge(s_prep, 3)

            def project_q(at):
                pe.wait_ge(s_xn, at.count(1, 1))
                for w in range(2):
                    ins = nc.tensor.matmul(psM[:, w * D:w * D + D], wA[:, w, :], xn[:, at.odd, :],
                                           start=True, stop=True)
                ins.then_inc(s_q, 1)

            def project_k(at):
                pe.wait_ge(s_ctx[at.odd], at.half * 16 + 16)
                for w in range(2):
                    ins = nc.tensor.matmul(psM[:, w * D:w * D + D], wA[:, 2 + w, :],
                                           ctx_in[:, at.odd, :], start=True, stop=True)
                ins.then_inc(s_k, 1)

            def project_v(at):
                for c in range(2):
                    ins = nc.tensor.matmul(psM[:, c * P:c * P + P],
                                           ctx_in[:, at.odd, c * P:c * P + P], wA[:, 4, :],
                                           start=True, stop=True)
                ins.then_inc(s_v, 1)

            def scores(at, n):
                hf, c, hg = n // 4, (n // 2) % 2, n % 2
                if n in (0, 4):
                    pe.wait_ge(s_stk[at.odd][hf], at.half * 64 + 64)
                if at.rep > 0 or n >= 2:
                    pe.wait_ge(s_max, at.count(8, n - 1))
                for i in range(4):
                    h = 8 * hf + 4 * hg + i
                    ins = nc.tensor.matmul(psS[n % 2][:, i * D:i * D + D],
                                           qst[0:STACK, at.odd, h, c * P:c * P + P],
                                           kst[0:STACK, at.odd, h, :], start=True, stop=True)
                ins.then_inc(s_s, 1)

            def turn_max(at, hf):
                pe.wait_ge(s_sp, at.count(2, hf + 1))
                for c in range(2):
                    ins = nc.tensor.transpose(psMb[0:16, c * P:c * P + P],
                                              npart[:, hf, c, :, :].rearrange("p a h -> p (a h)"),
                                              identb[:, :])
                ins.then_inc(s_mt, 1)

            def shifted(at, h):
                if h in (0, 8):
                    pe.wait_ge(s_mx[at.odd][h // 8], at.half * 16 + 16)
                if at.rep > 0 or h >= 2:
                    pe.wait_ge(s_exp, at.count(16, h - 1))
                for c in range(2):
                    ins = nc.tensor.matmul(psST[h % 2][:, c * D:c * D + D],
                                           kst[0:STACK + 2, at.odd, h, c * P:c * P + P],
                                           qst[0:STACK + 2, at.odd, h, :], start=True, stop=True)
                ins.then_inc(s_st, 1)

            def values(at, n):
                g, c = n // 2, n % 2
                if c == 0:
                    pe.wait_ge(s_exp, at.count(16, 4 * g + 4))
                if n == 0:
                    pe.wait_ge(s_vu, at.count(1, 1))
                if n == 0 and at.rep > 0:
                    pe.wait_ge(s_oe, at.count(2, 0))
                if n == 4:
                    pe.wait_ge(s_oe, at.count(2, 1))
                for j in range(4):
                    h = 4 * g + j
                    ins = nc.tensor.matmul(
                        psPV[32 * j:32 * j + 32, (g % 2) * D:(g % 2) * D + D],
                        vst[:, at.odd, c, h, :], pT[:, h % 8, c * D:c * D + D],
                        start=(c == 0), stop=(c == 1))
                if c == 1:
                    ins.then_inc(s_pv, 1)

            def some_values(at, slot):
                if slot < 2 and at.plus(-1).real():
                    values(at.plus(-1), 6 + slot)
                if slot >= 2 and at.real():
                    values(at, slot - 2)

            def merge(at):
                pe.wait_ge(s_on, at.count(1, 1))
                nc.tensor.matmul(psM[:, 0:D], wA[:, 5, :], on[:, :], start=True, stop=True)\
                  .then_inc(s_wm, 1)

            def step(at):
                last, nxt, two, three = at.plus(-1), at.plus(1), at.plus(2), at.plus(3)
                old = at.plus(-2)
                for slot in range(8):
                    if at.real():
                        shifted(at, 2 * slot)
                        shifted(at, 2 * slot + 1)
                    if nxt.real():
                        scores(nxt, slot)
                    if slot not in (3, 7):
                        some_values(at, slot)
                    if slot == 1 and at.real():
                        if two.real():
                            pe.wait_ge(s_ku, two.count(1, 1))
                        else:
                            pe.wait_ge(s_me, at.count(2, 1))
                        turn_max(at, 1)
                    if slot == 2 and nxt.real():
                        if at.real():
                            pe.wait_ge(s_me, at.count(2, 2))
                        else:
                            pe.wait_ge(s_ku, two.count(1, 1))
                        project_v(nxt)
                    if slot == 3 and three.real():
                        pe.wait_ge(s_vu, nxt.count(1, 1))
                        project_q(three)
                    if slot == 4:
                        if old.real():
                            if three.real():
                                pe.wait_ge(s_qu, three.count(1, 1))
                            elif nxt.real():
                                pe.wait_ge(s_vu, nxt.count(1, 1))
                            elif at.real():
                                pe.wait_ge(s_me, at.count(2, 2))
                            else:
                                pe.wait_ge(s_xA, at.count(1, -2))
                            merge(old)
                    if slot == 5 and nxt.real():
                        if old.real():
                            pe.wait_ge(s_xA, old.count(1, 1))
                        else:
                            pe.wait_ge(s_qu, three.count(1, 1))
                        turn_max(nxt, 0)
                    if slot == 7 and three.real():
                        pe.wait_ge(s_me, nxt.count(2, 1))
                        project_k(three)
                    if slot in (3, 7):
                        some_values(at, slot)

            project_q(At(0, 0))
            pe.wait_ge(s_qu, 1)
            project_k(At(0, 0))
            pe.wait_ge(s_ku, 1)
            project_q(At(0, 1))
            pe.wait_ge(s_qu, 2)
            project_k(At(0, 1))
            pe.wait_ge(s_b1, 2)
            nc.tensor.matmul(psYB[:, 0:2], onesf[:, :], wsum[:, :], start=True, stop=True)\
              .then_inc(s_ws, 1)
            step(At(-1, 1))
            steps(pe, step, 0, B + 1, 4, 4)

            pe.wait_ge(s_b0, PB_EARLY)
            pe.wait_ge(s_xA, B - 1)

            def turn_x(at):
                pe.wait_ge(s_xi, at.count(1, 1))
                if at.rep >= 1:
                    pe.wait_ge(s_xiTs, at.count(1, 0))
                for c in range(2):
                    ins = nc.tensor.transpose(psXT[:, c * P:c * P + P],
                                              xi[:, at.odd, c * P:c * P + P], identb[:, :])
                ins.then_inc(s_xiT, 1)

            def hidden(at):
                pe.wait_ge(s_xiTs, at.count(1, 1))
                if at.rep >= 2:
                    pe.wait_ge(s_g1, at.count(1, -1))
                for n in range(2):
                    for c in range(2):
                        ins = nc.tensor.matmul(psH[at.odd][:, n * 512:n * 512 + 512],
                                               xiT[:, at.odd, c, :],
                                               w1q[:, c, n * 512:n * 512 + 512],
                                               start=(c == 0), stop=(c == 1))
                ins.then_inc(s_h, 1)

            def turn_h(at):
                pe.wait_ge(s_hi, at.count(1, 1))
                if at.rep >= 1:
                    pe.wait_ge(s_hTs, at.count(1, 0))
                for c in range(8):
                    ins = nc.tensor.transpose(psHT[:, c * P:c * P + P],
                                              hr[:, at.odd, c * P:c * P + P], ident[:, :])
                ins.then_inc(s_hT, 1)

            def output(at):
                pe.wait_ge(s_hTs, at.count(1, 1))
                if at.rep >= 1:
                    pe.wait_ge(s_xB, at.count(1, 0))
                for c in range(8):
                    ins = nc.tensor.matmul(psYB[:, 0:D], hT[:, at.odd, c, :], w2q[:, c, :],
                                           start=(c == 0), stop=(c == 7))
                ins.then_inc(s_yB, 1)

            def step_b(at):
                last, old, two = at.plus(-1), at.plus(-2), at.plus(2)
                if two.real():
                    turn_x(two)
                if old.real():
                    output(old)
                if last.real():
                    turn_h(last)
                if two.real():
                    hidden(two)

            step_b(At(-1, 0))
            step_b(At(-1, 1))
            pe.wait_ge(s_xiTs, 2)
            step(At(B // 2, 1))
            pe.wait_ge(s_xA, B)
            steps(pe, step_b, 0, B + 2, 4, 4)

            pe.wait_ge(s_xB, B)
            pe.wait_ge(s_wC, 32)

            def step_c(at):
                last, nxt, two = at.plus(-1), at.plus(1), at.plus(2)
                old, older = at.plus(-2), at.plus(-3)
                if nxt.real():
                    pe.wait_ge(s_xcTs, nxt.count(1, 1))
                    if nxt.rep >= 1:
                        pe.wait_ge(s_qkCs, nxt.count(1, 0))
                    for w in range(2):
                        for e in range(2):
                            for c in range(2):
                                ins = nc.tensor.matmul(
                                    psQK[:, w * D + e * P:w * D + e * P + P],
                                    wC[:, w, c, e * P:e * P + P], xcT[:, nxt.odd, c, :],
                                    start=(c == 0), stop=(c == 1))
                    ins.then_inc(s_qkC, 1)
                if last.real():
                    pe.wait_ge(s_oCs, last.count(1, 1))
                    if last.rep >= 1:
                        pe.wait_ge(s_xC, last.count(1, 0))
                    for e in range(2):
                        ins = nc.tensor.matmul(psYC[:, 0:D], oTc[:, e, :], wC[:, 3, e, :],
                                               start=(e == 0), stop=(e == 1))
                    ins.then_inc(s_yC, 1)
                if older.real():
                    pe.wait_ge(s_xdTs, older.count(1, 1))
                    for c in range(2):
                        ins = nc.tensor.matmul(psTd[:, D:D + NCO], xdT[:, older.odd, c, :],
                                               wr[:, c, :], start=(c == 0), stop=(c == 1))
                    ins.then_inc(s_lg, 1)
                if nxt.real():
                    if nxt.rep >= 1:
                        pe.wait_ge(s_vCs, nxt.count(1, 0))
                    for c in range(2):
                        ins = nc.tensor.matmul(psV[:, 0:D], xcT[:, nxt.odd, c, :], wC[:, 2, c, :],
                                               start=(c == 0), stop=(c == 1))
                    ins.then_inc(s_vC, 1)
                if at.real():
                    pe.wait_ge(s_eC, at.count(1, 1))
                    if at.rep >= 1:
                        pe.wait_ge(s_pTs, at.count(1, 0))
                    for c in range(2):
                        ins = nc.tensor.transpose(psTp[:, c * P:c * P + P],
                                                  pc[:, at.odd, c * P:c * P + P], ident[:, :])
                    ins.then_inc(s_pT, 1)
                if two.real():
                    pe.wait_ge(s_xc, two.count(1, 1))
                    if two.rep >= 1:
                        pe.wait_ge(s_xcTs, two.count(1, 0))
                    for c in range(2):
                        ins = nc.tensor.transpose(psTx[:, c * P:c * P + P],
                                                  xc[:, two.odd, c * P:c * P + P], ident[:, :])
                    ins.then_inc(s_xcT, 1)
                if nxt.real():
                    pe.wait_ge(s_qkCs, nxt.count(1, 1))
                    pe.wait_ge(s_kv[nxt.odd], nxt.half * 32 + 32)
                    if nxt.rep >= 1:
                        pe.wait_ge(s_eC, nxt.count(1, 0))
                    for e in range(2):
                        ins = nc.tensor.matmul(psSc[:, 0:D], qTc[:, nxt.odd, e, :],
                                               kTc[:, nxt.odd, e, :], start=(e == 0), stop=(e == 1))
                    ins.then_inc(s_sC, 1)
                if at.real():
                    pe.wait_ge(s_pTs, at.count(1, 1))
                    if at.rep >= 1:
                        pe.wait_ge(s_oCs, at.count(1, 0))
                    for e in range(2):
                        for c in range(2):
                            ins = nc.tensor.matmul(psO[:, e * P:e * P + P],
                                                   vc[:, at.odd, c, e * P:e * P + P],
                                                   pcT[:, c, :], start=(c == 0), stop=(c == 1))
                    ins.then_inc(s_oC, 1)
                if old.real():
                    pe.wait_ge(s_xd, old.count(1, 1))
                    if old.rep >= 1:
                        pe.wait_ge(s_lgs, old.count(1, 0))
                    for c in range(2):
                        ins = nc.tensor.transpose(psTd[:, c * P:c * P + P],
                                                  xd[:, old.odd, c * P:c * P + P], ident[:, :])
                    ins.then_inc(s_xdT, 1)

            def largest_weights():
                pe.wait_ge(s_d0, PD_COMBINED)
                pe.wait_ge(s_xdTs, 6)
                for k in range(2):
                    ins = nc.tensor.transpose(psWm[0:1, k * P:k * P + P], wmax[:, k:k + 1],
                                              ident[:, :])
                ins.then_inc(s_dP, 1)
                pe.wait_ge(s_d0, PD_ROW)
                nc.tensor.matmul(psWm[:, D:D + 2], onesf[0:1, :], wmaxr[0:1, :],
                                 start=True, stop=True).then_inc(s_dP, 1)
                pe.wait_ge(s_d0, PD_SPREAD)

            step_c(At(-1, 0))
            step_c(At(-1, 1))
            steps(pe, step_c, 0, B + 3, 4, 4, 8, largest_weights)

            def gate_up(g, c):
                n, last = rows_of(c), c == NCH - 1
                assert n == (HID - FULL if last else P) and 2 * (HID - FULL) == P
                for ps, part, free, done in ((psG, 0, s_si, s_g), (psU, 1, s_hu, s_u))[:2 - last]:
                    wait_slot(pe, free, g, c)
                    if part == 0 and (last or c == 0 and exists(g, -1)):
                        wait_slot(pe, s_hu, g, c)
                    k = 0
                    for d in range(2):
                        for w, x in ((wgu_hi, xT_hi), (wgu_hi, xT_lo), (wgu_lo, xT_hi)):
                            first = 2 * FULL if last else part * FULL + c * P
                            ins = nc.tensor.matmul(ps[slot(c)], w[:, d, first:first + P],
                                                   x[:, d, bass.ds(g * 512, 512)],
                                                   start=(k == 0), stop=(k == 5))
                            k += 1
                    ins.then_inc(done, 1)

            def spread(g, c):
                wait_slot(pe, s_hd, g, c)
                apart(pe)
                first_token, unit = (g * 512, c * P) if c >= 0 else (g * 512 - 512, (c + NCH) * P)
                nc.tensor.matmul(psC[slot(c)], sel[:, unit:unit + P],
                                 cT[:, bass.ds(first_token, 512)], start=True, stop=True)\
                  .then_inc(s_c, 1)

            def down(g, c):
                n, chunk = rows_of(c), c % NCH
                pe.wait_ge(s_hl, g * NCH + (c + 1))
                if chunk == 0 and exists(g, -1):
                    pe.wait_ge(s_yD, g)
                for t in range(GROUP):
                    tokens = slice(t * P, t * P + P)
                    for k, (h, w) in enumerate(((hd_hi, wd_hi), (hd_lo, wd_hi), (hd_hi, wd_lo))):
                        ins = nc.tensor.matmul(acc[:, t * D:t * D + D], h[0:n, slot(c), tokens],
                                               w[0:n, chunk, :],
                                               start=(chunk == 0 and t % 2 == 0 and k == 0),
                                               stop=(chunk == NCH - 1 and k == 2),
                                               skip_group_check=True)
                ins.then_inc(s_dn, 1)

            def pe_group(g):
                for c in range(NCH):
                    gate_up(g, c)
                    if not exists(g, -1) and c == 1:
                        pe.wait_ge(s_rt, RT_DONE)
                        for b in range(B):
                            ins = nc.tensor.transpose(
                                bank[b // 4].bitcast(BF16)[0:3 * NCO, (b % 4) * P:(b % 4) * P + P],
                                cfp[:, b, :, :].rearrange("p a e -> p (a e)"), identb[:, :])
                            if b % 4 == 3:
                                ins.then_inc(s_cT, 1)
                    if not exists(g, -1) and 1 <= c <= 2:
                        pe.wait_ge(s_cTs, (1, NG)[c - 1])
                    if exists(g, c - 1):
                        spread(g, c - 1)
                    if exists(g, c - 2):
                        down(g, c - 2)

            pe.wait_ge(s_sel, 1)
            pe.wait_ge(s_wlo, 8)
            pe.wait_ge(s_xlo, B)
            pe.wait_ge(s_lgs, B)
            pe_group(0)
            with pe.Fori(1, NG) as g:
                pe_group(g)
            spread(NG - 1, NCH - 1)
            down(NG - 1, NCH - 2)
            down(NG - 1, NCH - 1)

        @block.vector
        def _(dve):
            def statistics_of_input(b):
                if b % 4 == 0:
                    dve.wait_ge(s_x[b // 4], 16)
                nc.vector.bn_stats(bnst[:, b % 2, :], x_all[:, b, :]).then_inc(s_dve, 1)
                dve.wait_ge(s_dve, 2 * b + 1)
                nc.vector.bn_aggr(stat[:, b, :], bnst[:, b % 2, :]).then_inc(s_dve, 1)

            def add_eps(batches):
                dve.wait_ge(s_dve, 2 * batches.stop)
                nc.vector.tensor_scalar(rstd[:, batches], stat[:, batches, 1], EPS, None, ALU.add)\
                  .then_inc(s_prep, 1)

            n = 2 * B
            for b in range(4):
                statistics_of_input(b)
            add_eps(slice(0, 4))
            dve.wait_ge(s_cst, 16 * CONST_DMAS)
            dve.wait_ge(s_act0, 1)
            nc.vector.tensor_scalar(rot[:, 1, :], rot[:, 1, :], smallA[:, 4:5], None, ALU.mult)
            nc.vector.tensor_copy(identb[:, :], ident[:, :])
            nc.vector.tensor_scalar(wA[:, 5, :], wA[:, 5, :], tg[:, 0:1], None, ALU.mult)\
              .then_inc(s_prep, 1)
            dve.wait_ge(s_bm, 1)
            nc.vector.scalar_tensor_tensor(tgbm[:, :], smallA[:, 5:6], tg[:, 0:1], psM[:, 0:1],
                                           ALU.mult, ALU.add).then_inc(s_prep, 1)
            dve.wait_ge(s_prep, 3)
            dve.wait_ge(s_pool0, 6)
            v = Chain(dve, s_vb)
            tt, ts = nc.vector.tensor_tensor, nc.vector.tensor_scalar

            def minus_mean(batches):
                nc.vector.scalar_tensor_tensor(nmr[:, batches], stat[:, batches, 0], -1.0,
                                               rstd[:, batches], ALU.mult, ALU.mult)\
                  .then_inc(s_prep, 1)

            def rotate(at, w, made, used, ready):
                dve.wait_ge(made, at.count(1, 1))
                if at.rep >= 1:
                    dve.wait_ge(ready, at.count(1, 0))
                for i in range(2):
                    ins = nc.vector.scalar_tensor_tensor(
                        rt[:, w, i, :], psM[:, i * D:i * D + D],
                        smallA[:, 2 * w + i:2 * w + i + 1], rot[:, i, :], ALU.add, ALU.mult)
                ins.then_inc(used, 1)

            def maximum(at, n):
                hf, c, hg = n // 4, (n // 2) % 2, n % 2
                dve.wait_ge(s_s, at.count(8, n + 1))
                if n == 0 and at.rep >= 2:
                    dve.wait_ge(s_sp, at.count(2, -2))
                nc.vector.tensor_reduce(
                    nmax[:, at.odd, hf, c, 4 * hg:4 * hg + 4],
                    psS[n % 2][:, :].rearrange("p (h m) -> p h m", h=4), AX.X, ALU.max,
                    negate=True).then_inc(s_max, 1)

            def high_max(at, hf):
                dve.wait_ge(s_max, at.count(8, 4 * hf + 4))
                if at.rep >= 1:
                    dve.wait_ge(s_mt, at.count(2, hf - 1))
                nc.vector.tensor_copy(npart[:, hf, :, 0, :], nmax[:, at.odd, hf, :, :])\
                  .then_inc(s_dve, 1)

            def low_max(at, hf):
                dve.wait_ge(s_dve, at.count(2, hf) + n + 1)
                nc.vector.tensor_tensor(npart[:, hf, :, 1, :], nmax[:, at.odd, hf, :, :],
                                        npart[:, hf, :, 0, :], ALU.subtract).then_inc(s_sp, 1)

            def invert(at):
                dve.wait_ge(s_oc, at.count(32, 32))
                if at.rep >= 1:
                    dve.wait_ge(s_on, at.count(1, 0))
                nc.vector.reciprocal(rden, oc[:, 1, :]).then_inc(s_rd, 1)

            def update(at):
                dve.wait_ge(s_wm, at.count(1, 1))
                xb = x_all[:, bass.ds(at.b, 1), :].rearrange("p b d -> p (b d)")
                nc.vector.scalar_tensor_tensor(xb, psM[:, 0:D], tgbm[:, 0:1], xb,
                                               ALU.add, ALU.add).then_inc(s_xA, 1)

            early, late = slice(0, B - 3), slice(B - 3, B)
            mean, var = stat[:, :, 0], stat[:, :, 1]

            def variances(batches):
                dve.wait_ge(s_st_r, batches.stop)
                ts(rstd[:, batches], var[:, batches], EPS, None, ALU.add)
                ts(tb[:, 3, batches], var[:, batches], float(D), None, ALU.mult).then_inc(s_b0, 1)

            def extremes(batches, n, op):
                dve.wait_ge(s_xA, batches.stop)
                v(nc.vector.tensor_reduce(tb[:, n, batches], x_all[:, batches, :], AX.X, op))

            def token_scales(batches, powers):
                t = lambda n: tb[:, n, batches]
                inverse = rstd[:, batches]
                v.wait()
                v(tt(t(0), t(0), mean[:, batches], ALU.subtract))
                v(tt(t(1), mean[:, batches], t(1), ALU.subtract))
                v.wait()
                dve.wait_ge(s_pool0, powers)
                v(tt(t(0), t(0), t(1), ALU.max))
                v(tt(t(3), t(3), inverse, ALU.mult))
                v.wait()
                v(tt(t(2), t(0), inverse, ALU.mult))
                v(ts(t(3), t(3), 1e-12, None, ALU.max))
                v.wait()
                v(nc.vector.reciprocal(t(4), t(3)))
                v.wait()
                v(tt(t(5), t(2), t(4), ALU.mult))
                v(tt(t(0), t(4), inverse, ALU.mult))
                v.wait()
                v(ts(t(5), t(5), float(D) ** 0.5, EPS, ALU.mult, ALU.max))
                v.wait()
                v(nc.vector.reciprocal(t(7), t(5)))
                ts(t(6), t(5), wmean[:, 0:1], 1.0 / 127.0, ALU.mult, ALU.mult)
                v.wait()
                v(tt(t(7), t(7), t(0), ALU.mult))
                v.wait()
                ts(t(7), t(7), 127.0 * float(D) ** 0.5, None, ALU.mult).then_inc(s_b0, 1)

            def statistics_1(at):
                dve.wait_ge(s_xA, at.count(1, 1))
                if at.rep >= 1:
                    dve.wait_ge(s_st_r, at.count(1, 0))
                apart(dve)
                nc.vector.bn_stats(bnst[:, 0, :],
                                   x_all[:, bass.ds(at.b, 1), :].rearrange("p b d -> p (b d)"))\
                  .then_inc(s_bn, 1)

            def statistics_2(at):
                dve.wait_ge(s_bn, at.count(1, 1))
                apart(dve)
                nc.vector.bn_aggr(agg[:, :], bnst[:, 0, :]).then_inc(s_ag, 1)

            def statistics_3(at):
                dve.wait_ge(s_ag, at.count(1, 1))
                nc.vector.tensor_scalar(stat[:, bass.ds(at.b, 1), :].rearrange("p b d -> p (b d)"),
                                        agg[:, :], 0.0, None, ALU.add).then_inc(s_st_r, 1)

            def first_parts_of_k():
                r, p = res[:, 1, :], lambda a_: parts[:, 0, 1, a_, :]
                dve.wait_ge(s_ku, 1)
                v(tt(r, rt[:, 1, 0, :], rt[:, 1, 1, :], ALU.add))
                v.wait()
                v(nc.vector.tensor_copy(p(0), r))
                v.wait()
                v(tt(r, r, p(0), ALU.subtract))
                v.wait()
                v(nc.vector.tensor_copy(p(1), r))
                v.wait()
                tt(p(2), r, p(1), ALU.subtract).then_inc(s_kp, 1)

            def ternary(k):
                w, wq = ((w1, w1q), (w2, w2q))[k % 2]
                w, wq = (t.rearrange("p c i -> p (c i)") for t in (w, wq))
                v.wait()
                if k < 2:
                    v(ts(w, w, wscale[:, k:k + 1], ROUND, ALU.mult, ALU.add))
                elif k < 4:
                    v(ts(w, w, ROUND, 1.0, ALU.subtract, ALU.min))
                else:
                    v(ts(wq, w, -1.0, None, ALU.max))

            def step(at):
                old, nxt, two, three = at.plus(-2), at.plus(1), at.plus(2), at.plus(3)
                for slot in range(8):
                    if slot == 5 and old.real():
                        statistics_1(old)
                    if nxt.real():
                        maximum(nxt, slot)
                    if slot == 0:
                        if at.real():
                            high_max(at, 1)
                        if at.real():
                            low_max(at, 1)
                    if slot == 1 and old.real():
                        invert(old)
                    if slot >= 2 and at.rep == -1:
                        ternary(slot - 2)
                    if slot == 2 and at.rep == B - 1:
                        variances(early)
                        extremes(early, 0, ALU.max)
                    if slot == 2 and at.rep == B:
                        token_scales(early, 8)
                    if slot == 4:
                        if nxt.real():
                            high_max(nxt, 0)
                        if old.real():
                            update(old)
                        if nxt.real():
                            low_max(nxt, 0)
                    if slot == 5 and old.real():
                        statistics_2(old)
                    if slot == 3 and three.real():
                        rotate(three, 0, s_q, s_qu, s_qp)
                    if slot == 6 and old.real():
                        statistics_3(old)
                    if slot == 7 and three.real():
                        rotate(three, 1, s_k, s_ku, s_kp)

            minus_mean(slice(0, 4))
            rotate(At(0, 0), 0, s_q, s_qu, s_qp)
            for b in range(4, 7):
                statistics_of_input(b)
            rotate(At(0, 0), 1, s_k, s_ku, s_kp)
            first_parts_of_k()
            rotate(At(0, 1), 0, s_q, s_qu, s_qp)
            for b in range(7, 12):
                statistics_of_input(b)
            rotate(At(0, 1), 1, s_k, s_ku, s_kp)
            for b in range(12, B):
                statistics_of_input(b)
            add_eps(slice(4, B))
            dve.wait_ge(s_ws, 1)
            v(ts(wmean[:, :], psYB[:, 0:2], 1.0 / (INNER * D), EPS, ALU.mult, ALU.max))
            v.wait()
            v(nc.vector.reciprocal(wscale[:, :], wmean[:, :]))
            v(ts(dqw[:, :], wmean[:, 1:2], tg[:, 2:3], 1.0 / 127.0, ALU.mult, ALU.mult))
            step(At(-1, 1))
            dve.wait_ge(s_pool0, 7)
            minus_mean(slice(4, B))
            steps(dve, step, 0, B, 4, 4)

            def xb(at):
                return x_all[:, bass.ds(at.b, 1), :].rearrange("p b d -> p (b d)")

            def scale_x(at):
                if at.rep >= 1:
                    dve.wait_ge(s_xi, at.count(1, 0))
                ts(xr[:, :], xb(at), stat[:, bass.ds(at.b, 1), 0], tb[:, 7, bass.ds(at.b, 1)],
                   ALU.subtract, ALU.mult).then_inc(s_xr, 1)

            def round_x(at):
                dve.wait_ge(s_xr, at.count(1, 1))
                if at.rep >= 2:
                    dve.wait_ge(s_xiT, at.count(1, -1))
                ts(xi[:, at.odd, :], xr[:, :], ROUND, ROUND, ALU.add, ALU.subtract)\
                    .then_inc(s_xi, 1)

            def update_b(at):
                dve.wait_ge(s_yB, at.count(1, 1))
                nc.vector.scalar_tensor_tensor(xb(at), psYB[:, 0:D], tq[:, at.odd, 7:8], xb(at),
                                               ALU.mult, ALU.add).then_inc(s_xB, 1)

            def stats_1(at, updated, bn, ready):
                dve.wait_ge(updated, at.count(1, 1))
                if at.rep >= 1:
                    dve.wait_ge(ready, at.count(1, 0))
                apart(dve)
                nc.vector.bn_stats(bnst[:, 0, :], xb(at)).then_inc(bn, 1)

            def stats_2(at, bn):
                dve.wait_ge(bn, at.count(2, 1))
                apart(dve)
                nc.vector.bn_aggr(agg[:, :], bnst[:, 0, :]).then_inc(bn, 1)

            def stats_3(at, bn, ready):
                dve.wait_ge(bn, at.count(2, 2))
                ts(stat[:, bass.ds(at.b, 1), :].rearrange("p b d -> p (b d)"), agg[:, :], 0.0,
                   None, ALU.add).then_inc(ready, 1)

            def step_b(at):
                old, three = at.plus(-2), at.plus(3)
                q = tq[:, at.odd, :]
                col = lambda n: q[:, n:n + 1]
                here = at.real()

                def scale(k, make):
                    if here:
                        if k > 1:
                            dve.wait_ge(s_tq, at.count(6, k - 1))
                        make().then_inc(s_tq, 1)

                if here:
                    dve.wait_ge(s_g2, at.count(1, 1))
                scale(1, lambda: nc.vector.tensor_reduce(col(0), h2[:, at.odd, :], AX.X, ALU.max,
                                                         apply_absolute_value=True))
                if old.real():
                    update_b(old)
                if here:
                    dve.wait_ge(s_nr, at.count(1, 1))
                scale(2, lambda: ts(col(1), nrm[:, at.odd:at.odd + 1], 1e-12, None, ALU.max))
                if three.real():
                    scale_x(three)
                scale(3, lambda: nc.vector.reciprocal(col(2), col(1)))
                if old.real():
                    stats_1(old, s_xB, s_bnB, s_stB)
                scale(4, lambda: ts(col(3), col(0), col(2), float(INNER) ** 0.5, ALU.mult,
                                    ALU.mult))
                if three.real():
                    round_x(three)
                if here:
                    dve.wait_ge(s_tq, at.count(6, 4))
                    if at.rep >= 2:
                        dve.wait_ge(s_xB, at.count(1, -1))
                    ts(col(7), col(3), EPS, dqw[:, 0:1], ALU.max, ALU.mult)
                scale(5, lambda: ts(col(4), col(3), EPS, None, ALU.max))
                if old.real():
                    stats_2(old, s_bnB)
                if here:
                    dve.wait_ge(s_tq, at.count(6, 5))
                    nc.vector.reciprocal(col(5), col(4)).then_inc(s_t5, 1)
                if old.real():
                    stats_3(old, s_bnB, s_stB)
                    if old.rep >= 2:
                        dve.wait_ge(s_rsB, old.count(1, -1))
                    ts(vard[:, 2 + old.odd:3 + old.odd], agg[:, 1:2], EPS, None, ALU.add)\
                        .then_inc(s_vB, 1)
                if here:
                    dve.wait_ge(s_t5, at.count(1, 1))
                scale(6, lambda: ts(col(6), col(5), col(2), 127.0 * float(INNER) ** 0.5,
                                    ALU.mult, ALU.mult))
                if here:
                    dve.wait_ge(s_tq, at.count(6, 6))
                    if at.rep >= 2:
                        dve.wait_ge(s_hT, at.count(1, -1))
                    ts(hr[:, at.odd, :], h2[:, at.odd, :], col(6), ROUND, ALU.mult, ALU.add)\
                        .then_inc(s_hi, 1)

            extremes(early, 1, ALU.min)
            step(At(B // 2, 0))
            dve.wait_ge(s_b0, PB_EARLY)
            step_b(At(-2, 1))
            step_b(At(-1, 0))
            step_b(At(-1, 1))
            step(At(B // 2, 1))
            variances(late)
            extremes(late, 0, ALU.max)
            extremes(late, 1, ALU.min)
            token_scales(late, 9)
            dve.wait_ge(s_b0, PB_LATE)
            steps(dve, step_b, 0, B + 2, 4, 4)


            def normal_c(at):
                dve.wait_ge(s_rsB, at.count(1, 1))
                if at.rep >= 2:
                    dve.wait_ge(s_xcT, at.count(1, -1))
                ts(xc[:, at.odd, :], xb(at), stat[:, bass.ds(at.b, 1), 0],
                   rstd[:, bass.ds(at.b, 1)], ALU.subtract, ALU.mult).then_inc(s_xc, 1)

            def step_c(at):
                last, nxt, three = at.plus(-1), at.plus(1), at.plus(3)
                old, older = at.plus(-2), at.plus(-3)
                if nxt.real():
                    dve.wait_ge(s_qkC, nxt.count(1, 1))
                    if nxt.rep >= 2:
                        dve.wait_ge(s_sC, nxt.count(1, -1))
                    nc.vector.tensor_copy(qTc[:, nxt.odd, :, :],
                                          psQK[:, 0:D].rearrange("p (c s) -> p c s", c=2))
                    nc.vector.tensor_copy(kTc[:, nxt.odd, :, P:D],
                                          psQK[:, D:2 * D].rearrange("p (c s) -> p c s", c=2))\
                      .then_inc(s_qkCs, 1)
                if last.real():
                    dve.wait_ge(s_yC, last.count(1, 1))
                    dve.wait_ge(s_rC, last.count(1, 1))
                    nc.vector.scalar_tensor_tensor(xb(last), psYC[:, 0:D], smc[:, last.odd, 3:4],
                                                   xb(last), ALU.mult, ALU.add).then_inc(s_xC, 1)
                if at.real():
                    dve.wait_ge(s_eC, at.count(1, 1))
                    nc.vector.reciprocal(smc[:, at.odd, 2:3], smc[:, at.odd, 1:2])\
                      .then_inc(s_r0, 1)
                if last.real():
                    stats_1(last, s_xC, s_bnC, s_stC)
                if at.real():
                    dve.wait_ge(s_r0, at.count(1, 1))
                    if at.rep >= 2:
                        dve.wait_ge(s_xC, at.count(1, -1))
                    ts(smc[:, at.odd, 3:4], smc[:, at.odd, 2:3], tg[:, 1:2], None, ALU.mult)\
                        .then_inc(s_rC, 1)
                if three.real():
                    normal_c(three)
                if last.real():
                    stats_2(last, s_bnC)
                if older.real():
                    dve.wait_ge(s_xdTs, older.count(1, 1))
                    cols = bass.ds(older.b * P, P)
                    tt(xT_lo[:, :, cols], xdT[:, older.odd, :, :], xT_hi[:, :, cols],
                       ALU.subtract).then_inc(s_xlo, 1)
                if old.real():
                    normal_d(old)
                if nxt.real():
                    dve.wait_ge(s_sC, nxt.count(1, 1))
                    nc.vector.tensor_reduce(mxc[:, nxt.odd:nxt.odd + 1], psSc[:, 0:D], AX.X,
                                            ALU.max, negate=True).then_inc(s_c1, 1)
                if last.real():
                    stats_3(last, s_bnC, s_stC)
                    if last.rep >= 2:
                        dve.wait_ge(s_rsd, last.count(1, -1))
                    ts(vard[:, last.odd:last.odd + 1], agg[:, 1:2], EPS, None, ALU.add)\
                        .then_inc(s_vd, 1)
                if nxt.real():
                    dve.wait_ge(s_c1, nxt.count(1, 1))
                    if nxt.rep >= 2:
                        dve.wait_ge(s_eC, nxt.count(1, -1))
                    ts(smc[:, nxt.odd, 0:1], mxc[:, nxt.odd:nxt.odd + 1], float(D) ** -0.5, None,
                       ALU.mult).then_inc(s_mC, 1)
                if 0 <= at.rep < 8:
                    if at.rep == 0:
                        dve.wait_ge(s_wD, 48)
                    for k, w, size in ((0, wgu, GU_PIECE), (1, wd, DN_PIECE)):
                        ins = nc.vector.tensor_reduce(wmp[:, k, bass.ds(at.b, 1)],
                                                      flat(w)[:, bass.ds(at.count(size, 0), size)],
                                                      AX.X, ALU.max, apply_absolute_value=True)
                    ins.then_inc(s_wmp, 1)
                elif 8 <= at.rep < 12:
                    low_part(8, at, wgu, wgu_hi, wgu_lo, 2 * GU_PIECE, wsc[:, 2:3], 0)
                elif 12 <= at.rep < 16:
                    low_part(12, at, wd, wd_hi, wd_lo, 2 * DN_PIECE, wsc[:, 3:4], 4)

            flat = lambda t: t.rearrange("p a b -> p (a b)")

            def low_part(n, at, src, high, low, size, scale, done):
                cols = bass.ds(at.count(size, -n * size), size)
                dve.wait_ge(s_whi, at.count(1, 1 - n + done))
                nc.vector.scalar_tensor_tensor(flat(low)[:, cols], flat(src)[:, cols], scale,
                                               flat(high)[:, cols], ALU.mult, ALU.subtract)\
                  .then_inc(s_wlo, 1)

            def largest_weights():
                dve.wait_ge(s_wmp, 8)
                nc.vector.tensor_reduce(wmax[:, :], wmp[:, :, :], AX.X, ALU.max).then_inc(s_d0, 1)
                dve.wait_ge(s_dP, 1)
                nc.vector.tensor_reduce(wmaxr[:, :], psWm[0:1, 0:D]
                                        .rearrange("p (k n) -> p k n", k=2), AX.X, ALU.max)\
                  .then_inc(s_d0, 1)
                dve.wait_ge(s_dP, 2)
                ts(wsc[:, 0:2], psWm[:, D:D + 2], 1e-30, None, ALU.max).then_inc(s_d0, 1)
                dve.wait_ge(s_d0, 3)
                nc.vector.reciprocal(wsc[:, 2:4], wsc[:, 0:2]).then_inc(s_d0, 1)
                ts(wsc[:, 6:7], wsc[:, 0:1], wsc[:, 0:1], 2.0, ALU.mult, ALU.mult)\
                    .then_inc(s_d0, 1)
                dve.wait_ge(s_d0, 5)
                ts(wsc[:, 4:5], wsc[:, 2:3], 0.5, None, ALU.mult)
                ts(wsc[:, 5:6], wsc[:, 6:7], wsc[:, 1:2], None, ALU.mult).then_inc(s_d0, 1)

            def normal_d(at):
                dve.wait_ge(s_rsd, at.count(1, 1))
                if at.rep >= 2:
                    dve.wait_ge(s_xdT, at.count(1, -1))
                ts(xd[:, at.odd, :], xb(at), stat[:, bass.ds(at.b, 1), 0],
                   rstdd[:, at.odd:at.odd + 1], ALU.subtract, ALU.mult).then_inc(s_xd, 1)

            normal_c(At(0, 0))
            step_c(At(-1, 0))
            step_c(At(-1, 1))
            steps(dve, step_c, 0, B + 3, 4, 4, 8, largest_weights)

            u = Chain(dve, s_ur)
            dve.wait_ge(s_lgs, B)
            l8 = lg[:, :, 0:E]
            u(nc.vector.tensor_reduce(den[:, :], l8, AX.X, ALU.max))
            u.wait()
            wide = lambda t: t.unsqueeze(2).to_broadcast([P, B, E])
            tt(rk[:, 0, :, :], l8, wide(den[:, :]), ALU.subtract).then_inc(s_rt, 1)
            dve.wait_ge(s_rta, 2)
            other = rk[:, 0, :, :].unsqueeze(2).to_broadcast([P, B, E, E])
            own = rk[:, 0, :, :].unsqueeze(3).to_broadcast([P, B, E, E])
            cm = [cmp_[:, n, :].rearrange("p (b e j) -> p b e j", b=B, e=E) for n in range(2)]
            cf2 = [cmp_[:, n, :].rearrange("p (b k) -> p b k", b=B) for n in range(2)]
            tr = tri[:, :].unsqueeze(1).to_broadcast([P, B, E * E])
            u(tt(cm[0], other, own, ALU.is_equal))
            u(tt(cm[1], other, own, ALU.is_gt))
            u.wait()
            u(tt(cf2[0], cf2[0], tr, ALU.mult))
            u(ts(cf[:, :, E], cf[:, :, E], 1.0, None, ALU.add))
            u.wait()
            u(tt(cmp_[:, 0, :], cmp_[:, 0, :], cmp_[:, 1, :], ALU.add))
            u(nc.vector.reciprocal(cf[:, :, E], cf[:, :, E]))
            u.wait()
            u(nc.vector.tensor_reduce(rk[:, 1, :, :], cm[0], AX.X, ALU.add))
            u(ts(cf[:, :, E], cf[:, :, E], tg[:, 3:4], None, ALU.mult))
            u.wait()
            u(nc.vector.scalar_tensor_tensor(rk[:, 2, :, :], rk[:, 1, :, :], 2.0, rk[:, 0, :, :],
                                             ALU.is_lt, ALU.mult))
            u.wait()
            u(nc.vector.tensor_reduce(den[:, :], rk[:, 2, :, :], AX.X, ALU.add))
            u.wait()
            u(nc.vector.reciprocal(den[:, :], den[:, :]))
            u.wait()
            u(nc.vector.scalar_tensor_tensor(cf[:, :, 0:E], rk[:, 2, :, :], tg[:, 3:4],
                                             wide(den[:, :]), ALU.mult, ALU.mult))
            u.wait()
            u(nc.vector.tensor_copy(cfp[:, :, 0, :], cf[:, :, :]))
            u.wait()
            u(tt(cfr[:, :, :], cf[:, :, :], cfp[:, :, 0, :], ALU.subtract))
            u.wait()
            u(nc.vector.tensor_copy(cfp[:, :, 1, :], cfr[:, :, :]))
            u.wait()
            tt(cfp[:, :, 2, :], cfr[:, :, :], cfp[:, :, 1, :], ALU.subtract).then_inc(s_rt, 1)

            def take_up(g, c):
                n = rows_of(c)
                up = psU[slot(c)]
                dve.wait_ge(s_si, g * NCH + (c + 1))
                if c == NCH - 1:
                    up = psG[slot(c)][n:2 * n, :]
                else:
                    dve.wait_ge(s_u, g * (NCH - 1) + (c + 1))
                if exists(g, c - 2):
                    dve.wait_ge(s_hl, g * NCH + (c - 1))
                nc.vector.scalar_tensor_tensor(hu[0:n, hu_slot(c), :], up,
                                               wsc[0:n, 4:5], gs[0:n, slot(c), :],
                                               ALU.mult, ALU.mult).then_inc(s_hu, 1)

            def weigh(g, c):
                n, h = rows_of(c), hu[0:rows_of(c), hu_slot(c), :]
                dve.wait_ge(s_hu, g * NCH + (c + 1))
                dve.wait_ge(s_c, g * NCH + (c + 1))
                tt(h, h, psC[slot(c)][0:n, :], ALU.mult).then_inc(s_hd, 1)
                dve.wait_ge(s_hh, g * NCH + (c + 1))
                tt(hd_lo[0:n, slot(c), :], h, hd_hi[0:n, slot(c), :], ALU.subtract)\
                    .then_inc(s_hl, 1)

            def add_group(g, first_batch):
                dve.wait_ge(s_dn, g * NCH)
                xg = x_all[:, bass.ds(first_batch, GROUP), :].rearrange("p b d -> p (b d)")
                nc.vector.scalar_tensor_tensor(xg, acc, wsc[:, 5:6], xg, ALU.mult, ALU.add)\
                  .then_inc(s_yD, 1)

            def dve_group(g):
                for c in range(NCH):
                    take_up(g, c)
                    if exists(g, c - 1):
                        weigh(g, c - 1)
                    if c == 1 and exists(g, -1):
                        add_group(g, g * GROUP - GROUP)

            dve_group(0)
            with dve.Fori(1, NG) as g:
                dve_group(g)
            weigh(NG - 1, NCH - 1)
            add_group(NG, (NG - 1) * GROUP)


def host_arrays(i):
    f = lambda n: np.asarray(i[n])
    qk = np.array([d * H + hf * 8 + h for hf in range(2) for d in range(HD) for h in range(8)])
    swap = np.array([(d ^ 1) * H + hf * 8 + h for hf in range(2) for d in range(HD) for h in range(8)])
    vh = np.array([d * H + h for h in range(H) for d in range(HD)])
    mg = np.array([d * H + 4 * g + j for j in range(4) for d in range(HD) for g in range(4)])
    wq, wk, wv, wm = (f(f"L0_xattn_{n}") for n in ("Wq", "Wk", "Wv", "Wm"))
    bq, bk, bv, bm = (f(f"L0_xattn_{n}") for n in ("bq", "bk", "bv", "bm"))
    sign = np.array([1.0 if d % 2 else -1.0 for _ in range(2) for d in range(HD) for _ in range(8)],
                    np.float32)
    enc = f("L0_xattn_encoding")[:, 0, 0]
    dim = np.array([d for _ in range(2) for d in range(HD) for _ in range(8)])
    pad = np.zeros(P, np.float32)
    chunks = lambda w: w.reshape(-1, P, w.shape[1]).transpose(1, 0, 2)
    flat = lambda w: w.transpose(1, 0, 2).reshape(D, E * I)
    gate, up = (np.concatenate([flat(f(f"L1_ffn_w_{n}")), f(f"L1_ffn_sw_{n}")], 1)
                for n in ("gate", "up"))
    wgu = np.concatenate([gate[:, :FULL], up[:, :FULL], gate[:, FULL:], up[:, FULL:]], 1)
    wd = np.zeros((NCH * P, D), np.float32)
    wd[:HID] = np.concatenate([f("L1_ffn_w_down").reshape(E * I, D), f("L1_ffn_sw_down")], 0)
    expert = np.minimum(np.arange(NCH * P) // I, E)
    sel = np.tile(np.arange(NCO)[:, None] == expert[None, :], (3, 1)).astype(np.float32)
    j, e = np.arange(E)[None, :], np.arange(E)[:, None]
    tri = (j < e).ravel().astype(np.float32)
    return {
        "w1": chunks(f("L0_ffn_w1").T), "w2": chunks(f("L0_ffn_w2").T),
        "wC": np.stack([chunks(f(f"L1_xattn_{n}").T) for n in ("wq", "wk", "wv", "wo")], 1),
        "ctxT": f("ctx_2048").transpose(0, 2, 1),
        "wgu": chunks(wgu), "wd": chunks(wd),
        "wr": chunks(np.concatenate([f("L1_ffn_gate_w").T, f("L1_ffn_shared_gate_w")], 1)),
        "sel": sel, "tri": tri,
        "x": f("x"), "ctx": f("ctx_2048"), "g_xattn": f("g_xattn"), "g_ffn": f("g_ffn"),
        "wA": np.stack([wq[qk].T, wq[swap].T, wk[qk].T, wk[swap].T, wv[vh].T, wm[:, mg].T], 1),
        "smallA": np.stack([bq[qk], bq[swap], bk[qk], bk[swap], sign, bm, bv[mg], pad], 1),
        "rot": np.stack([enc[0][:, dim].T, enc[1][:, dim].T], 1),
        "ident": np.eye(P, dtype=np.float32),
    }


def kernel(**inputs):
    import concourse.bacc as bacc
    from concourse.bass_utils import run_bass_kernel_spmd as run

    nc = bacc.Bacc("TRN2", target_bir_lowering=False, num_devices=1)
    arrays = {n: np.ascontiguousarray(v) for n, v in host_arrays(inputs).items()}
    a = {n: nc.dram_tensor(f"in_{n}", v.shape, mybir.dt.from_np(v.dtype), kind="ExternalInput").ap()
         for n, v in arrays.items()}
    out = nc.dram_tensor("out_x", (B, P, D), F32, kind="ExternalOutput").ap()
    build(nc, a, out)
    r = run(nc, [{f"in_{n}": v for n, v in arrays.items()}], core_ids=[0])
    return r.results[0]["out_x"]
```
